# Optimizing a Trainium2 kernel written in Bass

```python
import numpy as np
import jax
import jax.numpy as jnp

def _softmax(x, axis=-1):
    return jax.nn.softmax(x, axis=axis)

def _gelu(x):
    return jax.nn.gelu(x, approximate=True)

def _silu(x):
    return jax.nn.silu(x)

def _sigmoid(x):
    return jax.nn.sigmoid(x)

def _layernorm(x, axis=-1, eps=1e-05):
    m = jnp.mean(x, axis=axis, keepdims=True)
    v = jnp.var(x, axis=axis, keepdims=True)
    return (x - m) / jnp.sqrt(v + eps)

def _scatter_add(tgt, idx, src, axis=0):
    return tgt.at[idx].add(src)

def _segment_sum(src, seg, n):
    return jax.ops.segment_sum(src, seg, n)
kernel_name = 'mk_audio_tower_d1_tok_audfeat2048_r4_778e33'

def setup_inputs(seed: int=0):
    np.random.seed(seed)
    _w = jnp.asarray

    def _rec_inputs():
        import jax
        import jax.numpy as jnp
        _rk = jax.random.key(seed)
        x = -0.000392918 + 0.999932 * jax.random.normal(jax.random.fold_in(_rk, 1), (64, 125, 64), jnp.float32)
        return x
    x = _rec_inputs()

    def _L0_tok_setup():
        import jax, jax.numpy as jnp
        import numpy as np
        TIN = 16
        FEAT = 64
        IN_DIM = TIN * FEAT
        HDIM = 512
        EPS = 1e-06

        def layer_norm(x, gamma, beta, eps):
            mu = jnp.mean(x, axis=-1, keepdims=True)
            var = jnp.mean(jnp.square(x - mu), axis=-1, keepdims=True)
            return (x - mu) * jax.lax.rsqrt(var + eps) * gamma + beta
        key = jax.random.key(seed)
        ks = jax.random.split(key, 4)
        x = jax.random.normal(ks[0], (64, 1024, FEAT), dtype=jnp.float32)
        W = jax.random.normal(ks[1], (IN_DIM, HDIM), dtype=jnp.float32) / np.sqrt(IN_DIM)
        b = jnp.zeros((HDIM,), dtype=jnp.float32)
        g1 = jnp.ones((IN_DIM,), dtype=jnp.float32)
        b1 = jnp.zeros((IN_DIM,), dtype=jnp.float32)
        g2 = jnp.ones((HDIM,), dtype=jnp.float32)
        b2 = jnp.zeros((HDIM,), dtype=jnp.float32)
        return {'x': x, 'W': W, 'b': b, 'g1': g1, 'b1': b1, 'g2': g2, 'b2': b2}
    _L0_tok_all = _L0_tok_setup()
    _L0_tok_in = {k: v for k, v in _L0_tok_all.items() if k in ('W', 'b', 'g1', 'b1', 'g2', 'b2')}
    del _L0_tok_all

    def _L0_attn_setup():
        import jax, jax.numpy as jnp
        import numpy as np
        EPS_NORM = 1e-06
        EPS_Q = 1e-05

        def rmsnorm(x, g):
            var = jnp.mean(jnp.square(x), axis=-1, keepdims=True)
            return x * jax.lax.rsqrt(var + EPS_NORM) * g

        def act_quant(x):
            scale = 127.0 / jnp.clip(jnp.max(jnp.abs(x), axis=-1, keepdims=True), EPS_Q, None)
            return jnp.clip(jnp.round(x * scale), -128.0, 127.0) / scale

        def weight_quant(w):
            scale = 1.0 / jnp.clip(jnp.mean(jnp.abs(w)), EPS_Q, None)
            return jnp.clip(jnp.round(w * scale), -1.0, 1.0) / scale

        def ste(x, fn):
            return x + jax.lax.stop_gradient(fn(x) - x)

        def bitlinear(x, w, g):
            xn = rmsnorm(x, g)
            xq = ste(xn, act_quant)
            wq = ste(w, weight_quant)
            return jnp.einsum('bsd,od->bso', xq, wq)
        key = jax.random.key(seed)
        k1, k2, k3 = jax.random.split(key, 3)
        B, S, D, I = (4, 1024, 512, 1408)
        x = jax.random.normal(k1, (B, S, D), dtype=jnp.float32)
        w_gate = jax.random.normal(k2, (2 * I, D), dtype=jnp.float32) * D ** (-0.5)
        g_gate = jnp.ones((D,), dtype=jnp.float32)
        w_down = jax.random.normal(k3, (D, I), dtype=jnp.float32) * I ** (-0.5)
        g_down = jnp.ones((I,), dtype=jnp.float32)
        return {'x': x, 'w_gate': w_gate, 'g_gate': g_gate, 'w_down': w_down, 'g_down': g_down}
    _L0_attn_all = _L0_attn_setup()
    _L0_attn_in = {k: v for k, v in _L0_attn_all.items() if k in ('w_gate', 'g_gate', 'w_down', 'g_down')}
    del _L0_attn_all

    def _L0_ffn_setup():
        import jax, jax.numpy as jnp
        import numpy as np
        B, S, H, E, K, I = (2, 256, 512, 32, 8, 192)
        key = jax.random.key(seed)
        ks = jax.random.split(key, 5)
        scaled = lambda k, shp, fan: jax.random.normal(k, shp, jnp.float32) * fan ** (-0.5)
        return {'hidden_states': jax.random.normal(ks[0], (B, S, H), jnp.float32), 'router_w': scaled(ks[1], (E, H), H), 'w_gate': scaled(ks[2], (E, H, I), H), 'w_up': scaled(ks[3], (E, H, I), H), 'w_down': scaled(ks[4], (E, I, H), I)}
    _L0_ffn_all = _L0_ffn_setup()
    _L0_ffn_in = {k: v for k, v in _L0_ffn_all.items() if k in ('router_w', 'w_gate', 'w_up', 'w_down')}
    del _L0_ffn_all
    return {'x': x, 'L0_tok_W': _L0_tok_in['W'], 'L0_tok_b': _L0_tok_in['b'], 'L0_tok_g1': _L0_tok_in['g1'], 'L0_tok_b1': _L0_tok_in['b1'], 'L0_tok_g2': _L0_tok_in['g2'], 'L0_tok_b2': _L0_tok_in['b2'], 'L0_attn_w_gate': _L0_attn_in['w_gate'], 'L0_attn_g_gate': _L0_attn_in['g_gate'], 'L0_attn_w_down': _L0_attn_in['w_down'], 'L0_attn_g_down': _L0_attn_in['g_down'], 'L0_ffn_router_w': _L0_ffn_in['router_w'], 'L0_ffn_w_gate': _L0_ffn_in['w_gate'], 'L0_ffn_w_up': _L0_ffn_in['w_up'], 'L0_ffn_w_down': _L0_ffn_in['w_down']}

def reference(x, L0_tok_W, L0_tok_b, L0_tok_g1, L0_tok_b1, L0_tok_g2, L0_tok_b2, L0_attn_w_gate, L0_attn_g_gate, L0_attn_w_down, L0_attn_g_down, L0_ffn_router_w, L0_ffn_w_gate, L0_ffn_w_up, L0_ffn_w_down):
    import jax
    import jax.numpy as jnp

    def _L0_tok_ref(x, W, b, g1, b1, g2, b2):
        import jax, jax.numpy as jnp
        import numpy as np
        TIN = 16
        FEAT = 64
        IN_DIM = TIN * FEAT
        HDIM = 512
        EPS = 1e-06

        def layer_norm(x, gamma, beta, eps):
            mu = jnp.mean(x, axis=-1, keepdims=True)
            var = jnp.mean(jnp.square(x - mu), axis=-1, keepdims=True)
            return (x - mu) * jax.lax.rsqrt(var + eps) * gamma + beta
        bsz, T, F = x.shape
        n_patch = T // TIN
        x = x[:, :n_patch * TIN, :].reshape(bsz, n_patch, TIN * F)
        x = layer_norm(x, g1, b1, EPS)
        x = jnp.einsum('bpd,dh->bph', x, W) + b
        return layer_norm(x, g2, b2, EPS)

    def _L0_attn_ref(x, w_gate, g_gate, w_down, g_down):
        import jax, jax.numpy as jnp
        import numpy as np
        EPS_NORM = 1e-06
        EPS_Q = 1e-05

        def rmsnorm(x, g):
            var = jnp.mean(jnp.square(x), axis=-1, keepdims=True)
            return x * jax.lax.rsqrt(var + EPS_NORM) * g

        def act_quant(x):
            scale = 127.0 / jnp.clip(jnp.max(jnp.abs(x), axis=-1, keepdims=True), EPS_Q, None)
            return jnp.clip(jnp.round(x * scale), -128.0, 127.0) / scale

        def weight_quant(w):
            scale = 1.0 / jnp.clip(jnp.mean(jnp.abs(w)), EPS_Q, None)
            return jnp.clip(jnp.round(w * scale), -1.0, 1.0) / scale

        def ste(x, fn):
            return x + jax.lax.stop_gradient(fn(x) - x)

        def bitlinear(x, w, g):
            xn = rmsnorm(x, g)
            xq = ste(xn, act_quant)
            wq = ste(w, weight_quant)
            return jnp.einsum('bsd,od->bso', xq, wq)
        y = bitlinear(x, w_gate, g_gate)
        gate, v = jnp.split(y, 2, axis=-1)
        swiglu_out = gate * jax.nn.sigmoid(gate) * v
        z = bitlinear(swiglu_out, w_down, g_down)
        return z

    def _L0_ffn_ref(hidden_states, router_w, w_gate, w_up, w_down):
        import jax, jax.numpy as jnp
        import numpy as np
        B, S, H, E, K, I = (2, 256, 512, 32, 8, 192)
        Bq, Sq, Hd = hidden_states.shape
        x = hidden_states.reshape(-1, Hd)
        logits = x @ router_w.T
        probs = jax.nn.softmax(logits.astype(jnp.float32), axis=-1)
        rw, sel = jax.lax.top_k(probs, K)
        rw = rw / jnp.sum(rw, axis=-1, keepdims=True)
        rw = rw.astype(x.dtype)

        def body(acc, operand):
            e, wg, wu, wd = operand
            w_e = jnp.sum(jnp.where(sel == e, rw, jnp.zeros_like(rw)), axis=-1)
            h = jax.nn.silu(x @ wg) * (x @ wu)
            return (acc + h @ wd * w_e[:, None], None)
        acc0 = jnp.zeros_like(x)
        acc, _ = jax.lax.scan(body, acc0, (jnp.arange(E), w_gate, w_up, w_down))
        return acc.reshape(Bq, Sq, Hd)
    h = _L0_tok_ref(x, L0_tok_W, L0_tok_b, L0_tok_g1, L0_tok_b1, L0_tok_g2, L0_tok_b2)
    h = h + _L0_attn_ref(_layernorm(h, axis=-1), L0_attn_w_gate, L0_attn_g_gate, L0_attn_w_down, L0_attn_g_down)
    h = h + _L0_ffn_ref(_layernorm(h, axis=-1), L0_ffn_router_w, L0_ffn_w_gate, L0_ffn_w_up, L0_ffn_w_down)
    return h

_drawn_inputs = setup_inputs


def setup_inputs(seed=0):
    import zlib

    import numpy as np

    out = dict(_drawn_inputs(seed))
    spreads = {'L0_tok_b': (0.0, 0.1),
     'L0_tok_g1': (1.0, 0.2),
     'L0_tok_b1': (0.0, 0.1),
     'L0_tok_g2': (1.0, 0.2),
     'L0_tok_b2': (0.0, 0.1),
     'L0_attn_g_gate': (1.0, 0.2),
     'L0_attn_g_down': (1.0, 0.2)}
    factors = {}
    for name, (base, spread) in spreads.items():
        noise = np.random.default_rng([zlib.crc32(name.encode()), seed]).standard_normal(out[name].shape)
        drawn = base * np.exp(spread * noise) if base else spread * noise
        out[name] = jnp.asarray(drawn.astype(out[name].dtype))
    for name, factor in factors.items():
        out[name] = (out[name] * factor).astype(out[name].dtype)
    return out
```

```python
import concourse.bass as bass
from concourse import mybir
from contextlib import ExitStack

F32 = mybir.dt.float32
F32R = mybir.dt.float32r
BF16 = mybir.dt.bfloat16
F16 = mybir.dt.float16
I32 = mybir.dt.int32
ALU = mybir.AluOpType
ACT = mybir.ActivationFunctionType
AX = mybir.AxisListType

NB, NPATCH, TIN, FEAT = 64, 7, 16, 64
TOK = NB * NPATCH
NG, G = 4, TOK // 4
KIN = TIN * FEAT
KC = KIN // 128
D = 512
DC = D // 128
I1 = 1408
IC = I1 // 128
NE, TOPK, IE = 32, 8, 192
P = 128
NT = 64
ROW = D + NE
IH = IE // 2
WG = 2 * 4 * IE
WCOLS = WG + 2 * D
MAGIC = 1.5 * 2.0 ** 23
FAR = 1000.0
EPS6, EPS5 = 1e-6, 1e-5
N_ROOTS = 6 * NG


def wait(eng, sem, value):
    if isinstance(value, int) and value <= 0:
        return
    eng.wait_ge(sem, value)


class Step:

    def __init__(self, k, u, first=False, last=False):
        self.k, self.u, self.first, self.last = k, u, first, last

    def upto(self, d):
        return 2 * self.k + (self.u + d + 1)

    def tile(self, d):
        return 2 * self.k + (self.u + d)

    def slot(self, d):
        return (self.u + d) % 2

    def dma(self, d):
        return 16 * self.k + 16 * ((self.u + d) // 2 + 1)


def steps(eng, half):
    yield Step(0, 0, first=True)
    yield Step(0, 1, first=False)
    with eng.Fori(1, half) as k:
        yield Step(k, 0)
        yield Step(k, 1)
    yield Step(half, 0, last=True)
    yield Step(half, 1, last=True)


def program(nc, x, w_tok, b_tok, g1, b1, g2, b2, w_in, g_in, w_down, g_down, w_router, we_gate, we_up, we_down, out):
    rows_dram = nc.dram_tensor("token_rows", (TOK, ROW), F32).ap()
    place_dram = nc.dram_tensor("places", (NT, TOK), F16).ap()
    ctx = ExitStack()
    with ctx:
        def sb(name, shape, dt):
            return ctx.enter_context(nc.sbuf_tensor(name, shape, dt))

        def sem(name):
            return ctx.enter_context(nc.semaphore(name))

        big = sb("big", [128, 22 * D], F32)
        w_in_raw = big[:, :].rearrange("p (b d) -> p b d", b=22)
        w_down_raw = big[:, 0:DC * I1].rearrange("p (m i) -> p m i", m=DC)
        rows = big[0:G, 0:NG * ROW].rearrange("p (g r) -> p g r", g=NG)
        scr = big[0:G, 11 * D:11 * D + 3 * I1].rearrange("p (s i) -> p s i", s=3)
        at = [11 * D]

        def late(cols, dt=F32):
            at[0] += cols
            return big[:, at[0] - cols:at[0]].bitcast(dt) if dt != F32 else big[:, at[0] - cols:at[0]]

        fin = late(NG * D)[0:G, :].rearrange("p (g d) -> p g d", g=NG)
        got = late(2 * ROW).rearrange("p (s r) -> p s r", s=2)
        sg = late(IE)
        hid = late(IE)
        place_a = late(TOK, F16).rearrange("p (s t) -> p s t", s=2)
        place_s = late(TOK, F16).rearrange("p (s t) -> p s t", s=2)
        hit = late(TOK // 2, F16)
        xr_t = late(DC * G).rearrange("p (c t) -> p c t", c=DC)
        assert at[0] <= 22 * D
        q2 = big[0:G, 11 * D + 3 * I1:11 * D + 3 * I1 + I1 // 2].bitcast(BF16)
        w_t = sb("w_t", [128, DC * 2 * I1], BF16)
        w_t4 = w_t[:, :].rearrange("p (c o) -> p c o", c=DC)
        xt = w_t[0:G, 0:2 * NG * KIN].bitcast(F32).rearrange("p (g k) -> p g k", g=NG)
        wd_t = sb("wd_t", [128, IC, D], BF16)
        zf = wd_t[:, :, :].rearrange("p c d -> p (c d)")[:, 0:2 * KC * G].bitcast(F32).rearrange("p (c t) -> p c t", c=KC)
        whl = sb("whl", [128, 2, 2, WCOLS], F32R)
        whl_flat = whl[:, :, :, :].rearrange("p s h c -> p (s h c)")
        wtok_h = whl_flat[:, 0:KC * D].rearrange("p (c n) -> p c n", c=KC)
        wtok_l = whl_flat[:, KC * D:2 * KC * D].rearrange("p (c n) -> p c n", c=KC)
        zh = whl_flat[:, 2 * KC * D:2 * KC * D + KC * G].rearrange("p (c t) -> p c t", c=KC)
        zl = whl_flat[:, 2 * KC * D + KC * G:2 * KC * D + 2 * KC * G].rearrange("p (c t) -> p c t", c=KC)
        raw = sb("raw", [128, 2, WCOLS], F32)
        raw_flat = raw[:, :, :].rearrange("p s c -> p (s c)")
        wtok_raw = raw_flat[:, 0:KC * D].rearrange("p (c n) -> p c n", c=KC)
        q2_t = raw_flat[:, WCOLS:WCOLS + IC * TOK // 2].bitcast(BF16).rearrange("p (c t) -> p c t", c=IC)
        h = sb("h", [G, NG, D], F32)
        h_work = sb("h_work", [G, D], F32)
        q1_t = sb("q1_t", [128, DC, TOK], BF16)
        q1 = sb("q1", [G, D], BF16)
        tern = sb("tern", [128, 2, 2 * D], BF16)
        bias_bc = sb("bias_bc", [G, D], F32)
        g2_bc = sb("g2_bc", [G, D], F32)
        b2_bc = sb("b2_bc", [G, D], F32)
        gin_bc = sb("gin_bc", [G, D], F32)
        gdn_bc = sb("gdn_bc", [G, I1], F32)
        g1_c = sb("g1_c", [128, KC], F32)
        b1_c = sb("b1_c", [128, KC], F32)
        stats = sb("stats", [G, 2, 6], F32)
        mv = sb("mv", [G, 2], F32)
        ssq = sb("ssq", [G, 8], F32)
        amax = sb("amax", [G, 8], F32)
        qscale = sb("qscale", [G, 1], F32)
        deq = sb("deq", [G, 8], F32)
        deq_sq = sb("deq_sq", [G, NG], F32)
        deq2 = sb("deq2", [G, 1], F32)
        abs_sum = sb("abs_sum", [128, 2, 8], F32)
        abs_tot = sb("abs_tot", [128, 2], F32)
        zeros16 = sb("zeros16", [128, D], BF16)
        junk = sb("junk", [128, 3 * D], BF16)
        wmean = sb("wmean", [128, 2], F32)
        wscale = sb("wscale", [128, 2], F32)
        ident = sb("ident", [128, 128], F32)
        ident16 = sb("ident16", [128, 128], BF16)
        ones = sb("ones", [128, 128], F32)
        minus_half = sb("minus_half", [G, 1], F32)
        root_in = sb("root_in", [G, N_ROOTS], F32)
        root_out = sb("root_out", [G, N_ROOTS], F32)
        before = sb("before", [G, NG, TOK], BF16)
        rw_raw = sb("rw_raw", [NE, D], F32)
        rw_t = sb("rw_t", [128, DC, NE], F32)
        logit = sb("logit", [G, NE], F32)
        zapped = sb("zapped", [G, NE], F32)
        top8 = sb("top8", [G, 8], F32)
        neg_max = sb("neg_max", [G, 1], F32)
        expo = sb("expo", [G, NE], F32)
        esum = sb("esum", [G, 1], F32)
        picked = sb("picked", [G, NE], F32)
        psum8 = sb("psum8", [G, 1], F32)
        mask = sb("mask", [G, NG, NE], BF16)
        mask_t = sb("mask_t", [NE, TOK], F32)
        place = sb("place", [NE, TOK], F16)
        count = sb("count", [NE, 1], F32)
        n_over = sb("n_over", [NE, 1], F32)
        start = sb("start", [NE, 1], F32)
        iota_e = sb("iota_e", [NE, 1], F32)
        iota_e16 = sb("iota_e16", [NE, 1], F16)
        iota_t = sb("iota_t", [NE, NT], F32)
        before_e = sb("before_e", [NE, NE], F32)
        ones16 = sb("ones16", [NE, 1], F16)
        t_a = sb("t_a", [NE, NT], F32)
        t_b = sb("t_b", [NE, NT], F32)
        t_c = sb("t_c", [NE, NT], F32)
        owner = sb("owner", [NE, NT], F16)
        shift = sb("shift", [NE, NT], F16)
        shift_c = sb("shift_c", [NT, 1], F32)
        place_tile = sb("place_tile", [NT, TOK], F16)
        owner_row = sb("owner_row", [1, NT], I32)
        halff = sb("halff", [1, 1], F32)
        more_i = sb("more_i", [1, 1], I32)
        trow = sb("trow", [128, TOK], F16)
        iota_p = sb("iota_p", [128, 1], F32)
        idx_f = sb("idx_f", [128, 2], F32)
        idx = sb("idx", [128, 2], I32)
        gate = sb("gate", [128, 2], F32)
        xh = sb("xh", [128, 4, P], F32R)
        xl = sb("xl", [128, 4, P], F32R)
        hh = sb("hh", [IH, 2, P], F32R)
        hl = sb("hl", [IH, 2, P], F32R)
        yh = sb("yh", [P, 2, D], F32R)
        yl = sb("yl", [P, 2, D], F32R)
        sel = sb("sel", [P, 2, TOK], F32R)

        ps = ctx.enter_context(nc.psum_tensor("ps", [128, 8, 512], F32))

        def bank(b, n=1):
            return ps[:, b:b + n, :].rearrange("p b c -> p (b c)")

        ld_x = [sem(f"ld_x{g}") for g in range(NG)]
        ld_wtok = [sem(f"ld_wtok{n}") for n in range(2)]
        ld_vec = sem("ld_vec")
        ld_win = [sem(f"ld_win{n}") for n in range(4)]
        ld_wdown = [sem(f"ld_wdown{n}") for n in range(2)]
        ld_gu = [sem(f"ld_gu{n}") for n in range(2)]
        ld_dn = [sem(f"ld_dn{n}") for n in range(2)]
        ld_pa = [sem(f"ld_pa{n}") for n in range(2)]
        ld_ps = [sem(f"ld_ps{n}") for n in range(2)]
        ld_got = [sem(f"ld_got{n}") for n in range(2)]
        dve_chain = sem("dve_chain")
        pool_chain = sem("pool_chain")
        root_ready = sem("root_ready")
        root_done = sem("root_done")
        act_chain = sem("act_chain")
        consts = sem("consts")
        xhat_ready = sem("xhat_ready")
        t1_done = sem("t1_done")
        zf_ready = sem("zf_ready")
        zh_ready = sem("zh_ready")
        zl_ready = sem("zl_ready")
        wtok_h_ready = sem("wtok_h_ready")
        wtok_l_ready = sem("wtok_l_ready")
        tok_done = sem("tok_done")
        h_ready = sem("h_ready")
        tok_read = sem("tok_read")
        ssq1_in = sem("ssq1_in")
        ssq1_ready = sem("ssq1_ready")
        q1_ready = sem("q1_ready")
        q1t_done = sem("q1t_done")
        q1t_ready = sem("q1t_ready")
        abs_in_ready = sem("abs_in_ready")
        abs_down_ready = sem("abs_down_ready")
        tot_in = sem("tot_in")
        tot_done = sem("tot_done")
        tern_ready = sem("tern_ready")
        wt_done = sem("wt_done")
        wt_ready = sem("wt_ready")
        scales_ready = sem("scales_ready")
        gv_done = sem("gv_done")
        sig_ready = sem("sig_ready")
        gate_read = sem("gate_read")
        swi_ready = sem("swi_ready")
        ssq2_ready = sem("ssq2_ready")
        xn2_ready = sem("xn2_ready")
        amax2_ready = sem("amax2_ready")
        q2_ready = sem("q2_ready")
        q2t_done = sem("q2t_done")
        q2t_ready = sem("q2t_ready")
        z_done = sem("z_done")
        z_read = sem("z_read")
        row_ready = sem("row_ready")
        rw_done = sem("rw_done")
        rw_ready = sem("rw_ready")
        xrt_done = sem("xrt_done")
        xrt_ready = sem("xrt_ready")
        logit_done = sem("logit_done")
        max_ready = sem("max_ready")
        exp_ready = sem("exp_ready")
        gate_ready = sem("gate_ready")
        rows_out = sem("rows_out")
        rank_done = sem("rank_done")
        over_ready = sem("over_ready")
        start_done = sem("start_done")
        owner_ready = sem("owner_ready")
        tables_done = sem("tables_done")
        place_ready = sem("place_ready")
        place_out = sem("place_out")
        table_ready = sem("table_ready")
        hit_ready = sem("hit_ready")
        idx_ready = sem("idx_ready")
        gather_go = sem("gather_go")
        gate_col = sem("gate_col")
        guh_ready = sem("guh_ready")
        gul_ready = sem("gul_ready")
        dnh_ready = sem("dnh_ready")
        dnl_ready = sem("dnl_ready")
        xh_ready = sem("xh_ready")
        xl_ready = sem("xl_ready")
        silu_ready = sem("silu_ready")
        hid_ready = sem("hid_ready")
        hh_ready = sem("hh_ready")
        hl_ready = sem("hl_ready")
        yh_ready = sem("yh_ready")
        yl_ready = sem("yl_ready")
        sel_ready = sem("sel_ready")
        gu_done = sem("gu_done")
        xt_done = sem("xt_done")
        y_done = sem("y_done")
        ht_done = sem("ht_done")
        sum_done = sem("sum_done")
        fin_ready = sem("fin_ready")
        out_done = sem("out_done")

        block = ctx.enter_context(nc.Block())
        out_g = out.rearrange("(g b) n d -> g (b n) d", g=NG)
        we_gate_v = we_gate.rearrange("e (p c) i -> e p (c i)", c=4)
        we_up_v = we_up.rearrange("e (p c) i -> e p (c i)", c=4)
        we_down_v = we_down.rearrange("e (p c) d -> e p (c d)", c=2)
        ABS_PART = [0, 3, 6, 9, 11, 14, 17, 20, 22]
        WIN_PART = [0, 6, 11, 17, 22]
        win_v = w_in.rearrange("(b p) d -> p b d", p=128)
        wdown_v = w_down.rearrange("(m p) i -> p m i", p=128)

        def bcast(v, n):
            return v.rearrange("(a n) -> a n", a=1).broadcast_to([G, n])

        @block.sync
        def _(sp):
            for g in range(NG):
                for b in range(16):
                    sp.dma_start(xt[b * NPATCH:(b + 1) * NPATCH, g, :],
                                 x[16 * g + b, 0:NPATCH * TIN, :].rearrange("(n t) f -> n (t f)", t=TIN)
                                 ).then_inc(ld_x[g], 16)
                if g % 2:
                    n = g // 2
                    sp.dma_start(raw_flat[:, n * 4 * D:(n + 1) * 4 * D],
                                 w_tok.rearrange("(p c) n -> p (c n)", c=KC)[:, n * 4 * D:(n + 1) * 4 * D]
                                 ).then_inc(ld_wtok[n], 16)
            for n in range(4):
                a, b = WIN_PART[n], WIN_PART[n + 1]
                sp.dma_start(w_in_raw[:, a:b, :], win_v[:, a:b, :]).then_inc(ld_win[n], 16)
            sp.wait_ge(tern_ready, 6)
            for n in range(2):
                sp.dma_start(w_down_raw[:, 2 * n:2 * n + 2, :], wdown_v[:, 2 * n:2 * n + 2, :]).then_inc(ld_wdown[n], 16)
            sp.wait_ge(wtok_l_ready, 2)

            def load_expert(e, s):
                sp.dma_start(raw[:, s, 0:WG // 2], we_gate_v[e, :, :]).then_inc(ld_gu[s], 16)
                sp.dma_start(raw[:, s, WG // 2:WG], we_up_v[e, :, :]).then_inc(ld_gu[s], 16)
            def load_down(e, s):
                sp.dma_start(raw[0:IH, s, WG:WCOLS], we_down_v[e, :, :]).then_inc(ld_dn[s], 16)

            load_expert(0, 0)
            load_down(0, 0)
            for g in range(NG):
                if g == 0:
                    sp.wait_ge(z_done, NG)
                    load_expert(1, 1)
                    load_down(1, 1)
                sp.wait_ge(gate_ready, g + 1)
                sp.dma_start(rows_dram[g * G:(g + 1) * G, :], rows[:, g, :]).then_inc(rows_out, 16)
            sp.wait_ge(place_ready, 1)
            sp.dma_start(place_dram[:, :], place_tile[:, :]).then_inc(place_out, 16)
            sp.wait_ge(place_out, 16)
            sp.wait_ge(table_ready, 1)
            half = sp.value_load(more_i[0:1, 0:1], min_val=0, max_val=14) + NE // 2

            def load_place(dst, sems, t, s):
                sp.dma_start(dst[:, s, :], place_dram[bass.ds(t, 1), :].broadcast_to([128, TOK])).then_inc(sems[s], 16)

            def load_tile(st):
                u = st.u
                e = sp.value_load(owner_row[0:1, bass.ds(st.tile(0), 1)], min_val=0, max_val=NE - 1)
                wait(sp, gul_ready, st.upto(-2))
                sp.dma_start(raw[:, u, 0:WG // 2], we_gate_v[bass.ds(e, 1), :, :]).then_inc(ld_gu[u], 16)
                sp.dma_start(raw[:, u, WG // 2:WG], we_up_v[bass.ds(e, 1), :, :]).then_inc(ld_gu[u], 16)
                wait(sp, idx_ready, st.upto(0))
                load_place(place_a, ld_pa, st.tile(2), u)
                wait(sp, dnl_ready, st.upto(-2))
                sp.dma_start(raw[0:IH, u, WG:WCOLS], we_down_v[bass.ds(e, 1), :, :]).then_inc(ld_dn[u], 16)
                wait(sp, sel_ready, st.upto(-4))
                load_place(place_s, ld_ps, st.tile(-2), u)

            for t in range(2):
                load_place(place_a, ld_pa, t, t)
            for t in range(2):
                sp.wait_ge(idx_ready, t + 1)
                load_place(place_a, ld_pa, t + 2, t)
            load_tile(Step(1, 0))
            load_tile(Step(1, 1))
            with sp.Fori(2, half + 1) as k:
                load_tile(Step(k, 0))
                load_tile(Step(k, 1))
            for g in range(NG):
                sp.wait_ge(fin_ready, g + 1)
                sp.dma_start(out_g[g, :, :], fin[:, g, :]).then_inc(out_done, 16)
            sp.wait_ge(out_done, 16 * NG)

        @block.gpsimd
        def _(pool):
            chain = [0]

            def link(ins):
                chain[0] += 1
                ins.then_inc(pool_chain, 1)
                pool.wait_ge(pool_chain, chain[0])

            link(nc.gpsimd.memset(ones[:, :], 1.0))
            link(nc.gpsimd.memset(ident[:, :], 0.0))
            link(nc.gpsimd.affine_select(out=ident[:, :], in_=ident[:, :], compare_op=ALU.not_equal, fill=1.0,
                                         base=0, pattern=[[-1, 128]], channel_multiplier=1))
            link(nc.gpsimd.tensor_copy(ident16[:, :], ident[:, :]))
            link(nc.gpsimd.memset(minus_half[:, :], -0.5))
            nc.gpsimd.memset(zeros16[:, :], 0.0).then_inc(consts, 1)
            link(nc.gpsimd.memset(before[:, :, :], 1.0))
            nc.gpsimd.affine_select(out=before[:, :, :], in_=before[:, :, :], compare_op=ALU.is_gt, fill=0.0,
                                    base=0, pattern=[[-G, NG], [1, TOK]], channel_multiplier=-1).then_inc(consts, 1)
            link(nc.gpsimd.memset(before_e[:, :], 1.0))
            nc.gpsimd.affine_select(out=before_e[:, :], in_=before_e[:, :], compare_op=ALU.is_gt, fill=0.0,
                                    base=0, pattern=[[1, NE]], channel_multiplier=-1).then_inc(consts, 1)
            nc.gpsimd.memset(ones16[:, :], 1.0).then_inc(consts, 1)
            for t, pattern, mult in ((iota_e, [[0, 1]], 1), (iota_e16, [[0, 1]], 1), (iota_t, [[1, NT]], 0),
                                     (trow, [[1, TOK]], 0), (iota_p, [[0, 1]], 1)):
                nc.gpsimd.iota(t[:, :], pattern=pattern, base=0, channel_multiplier=mult,
                               allow_small_or_imprecise_dtypes=True).then_inc(consts, 1)

            for n in range(N_ROOTS):
                pool.wait_ge(root_ready, n + 1)
                nc.gpsimd.tensor_tensor(root_out[:, n:n + 1], root_in[:, n:n + 1], minus_half[:, :], ALU.pow
                                        ).then_inc(root_done, 1)

            def gather(t, s):
                nc.gpsimd.indirect_dma_start(got[:, s, :], None, rows_dram[:, :],
                                             bass.IndirectOffsetOnAxis(ap=idx[:, s:s + 1], axis=0)
                                             ).then_inc(ld_got[s], 16)

            def split_low(st, d):
                s = st.slot(d)
                wait(pool, guh_ready, st.upto(d))
                for n in range(2):
                    cols = slice(n * WG // 2, (n + 1) * WG // 2)
                    last = nc.gpsimd.tensor_tensor(whl[:, s, 1, cols], raw[:, s, cols],
                                                   whl[:, s, 0, cols].bitcast(F32), ALU.subtract)
                last.then_inc(gul_ready, 1)

            pool.wait_ge(rows_out, 16 * NG)
            for t in range(2):
                pool.wait_ge(idx_ready, t + 1)
                gather(t, t)
            split_low(Step(0, 0), 0)
            split_low(Step(0, 0), 1)
            pool.wait_ge(idx_ready, 3)
            pool.wait_ge(xt_done, 1)
            pool.wait_ge(gate_col, 1)
            gather(2, 0)
            pool.wait_ge(table_ready, 1)
            half = pool.value_load(more_i[0:1, 0:1], min_val=0, max_val=14) + NE // 2
            for st in steps(pool, half):
                if st.last:
                    continue
                split_low(st, 2)
                wait(pool, idx_ready, st.upto(3))
                wait(pool, xt_done, st.upto(1))
                wait(pool, gate_col, st.upto(1))
                pool.sem_inc(gather_go, 1)
                gather(None, st.slot(3))

        @block.scalar
        def _(act):
            vecs = [(bias_bc, b_tok, D), (g2_bc, g2, D), (b2_bc, b2, D), (gin_bc, g_in, D), (gdn_bc, g_down, I1)]
            act.dma_start(g1_c[:, :], g1.rearrange("(p c) -> p c", c=KC)).then_inc(ld_vec, 16)
            act.dma_start(b1_c[:, :], b1.rearrange("(p c) -> p c", c=KC)).then_inc(ld_vec, 16)
            act.dma_start(rw_raw[:, :], w_router).then_inc(ld_vec, 16)
            for dst, src, n in vecs:
                act.dma_start(dst[:, :], bcast(src, n)).then_inc(ld_vec, 16)

            def split_tok_high(n):
                act.wait_ge(ld_wtok[n], 16)
                nc.scalar.activation(wtok_h[:, 4 * n:4 * n + 4, :], wtok_raw[:, 4 * n:4 * n + 4, :], ACT.Copy
                                     ).then_inc(wtok_h_ready, 1)

            def scale_patch(g):
                act.wait_ge(t1_done, g + 1)
                if g == 0:
                    act.wait_ge(ld_vec, 16 * 8)
                for c in range(KC):
                    if g and c == 0:
                        act.wait_ge(zl_ready, g)
                        act.wait_ge(tok_done, g)
                    last = nc.scalar.activation(zf[:, c, :], bank(c // 4)[:, (c % 4) * G:(c % 4 + 1) * G], ACT.Identity,
                                                scale=g1_c[:, c:c + 1], bias=b1_c[:, c:c + 1])
                last.then_inc(zf_ready, 1)
                act.wait_ge(zf_ready, g + 1)
                nc.scalar.activation(zh[:, :, :], zf[:, :, :], ACT.Copy).then_inc(zh_ready, 1)

            scrapped = []

            def scrap(sem_, count):
                if scrapped:
                    act.wait_ge(*scrapped.pop())
                scrapped.append((sem_, count))

            def abs_in(n):
                act.wait_ge(ld_win[n // 2], 16)
                a, b = ABS_PART[n], ABS_PART[n + 1]
                scrap(abs_in_ready, n + 1)
                nc.scalar.activation(junk[:, 0:(b - a) * D], w_in_raw[:, a:b, :].rearrange("p b d -> p (b d)"), ACT.Abs,
                                     accum_out=abs_sum[:, 0, n:n + 1]).then_inc(abs_in_ready, 1)

            def square1(g):
                act.wait_ge(ssq1_in, g + 1)
                scrap(ssq1_ready, g + 1)
                nc.scalar.activation(junk[0:G, 0:D], h_work[:, :], ACT.Square,
                                     accum_out=ssq[:, g:g + 1]).then_inc(ssq1_ready, 1)

            def copy_q1t(g):
                act.wait_ge(q1t_done, g + 1)
                nc.scalar.activation(q1_t[:, :, g * G:(g + 1) * G],
                                     bank(4)[:, 0:DC * G // 2].bitcast(BF16).rearrange("p (c t) -> p c t", c=DC),
                                     ACT.Copy).then_inc(q1t_ready, 1)

            def sign_w(n):
                act.wait_ge(wt_done, n + 1)
                src = bank(6 + n % 2).bitcast(BF16)
                if n < 11:
                    dst = w_t4[:, :, 2 * n * 128:(2 * n + 2) * 128].rearrange("p c (b q) -> p b c q", b=2)
                    src = src.rearrange("p (b c q) -> p b c q", b=2, c=DC)
                else:
                    c0 = 2 * (n - 11)
                    w = min(2, IC - c0)
                    dst = wd_t[:, c0:c0 + w, :].rearrange("p c d -> p (c d)")
                    src = src[:, 0:w * D]
                nc.scalar.activation(dst, src, ACT.Sign).then_inc(wt_ready, 1)

            split_tok_high(0)
            split_tok_high(1)
            scale_patch(0)
            abs_in(0)
            scale_patch(1)
            abs_in(1)
            abs_in(2)
            square1(0)
            scale_patch(2)
            abs_in(3)
            copy_q1t(0)
            abs_in(4)
            square1(1)
            scale_patch(3)
            copy_q1t(1)
            for n in range(5, 8):
                abs_in(n)
            square1(2)
            copy_q1t(2)
            for n in range(6):
                sign_w(n)
            square1(3)
            copy_q1t(3)
            for n in range(6, 11):
                sign_w(n)
            for m in range(DC):
                act.wait_ge(ld_wdown[m // 2], 16)
                scrap(abs_down_ready, m + 1)
                nc.scalar.activation(junk[:, 0:I1], w_down_raw[:, m, :], ACT.Abs, accum_out=abs_sum[:, 1, m:m + 1]
                                     ).then_inc(abs_down_ready, 1)
            for n in range(11, 17):
                sign_w(n)

            act.wait_ge(scales_ready, 1)

            def sigmoid(g):
                act.wait_ge(gv_done, g + 1)
                if g >= 2:
                    act.wait_ge(q2_ready, g - 1)
                nc.scalar.activation(scr[:, g % 2, :], bank(0, 3)[0:G, 0:I1], ACT.Sigmoid, scale=deq[:, g:g + 1]
                                     ).then_inc(sig_ready, 1)

            def square2(g):
                act.wait_ge(swi_ready, g + 1)
                scrap(ssq2_ready, g + 1)
                nc.scalar.activation(junk[0:G, 0:I1], scr[:, g % 2, :], ACT.Square, accum_out=ssq[:, 4 + g:5 + g]
                                     ).then_inc(ssq2_ready, 1)

            def copy_q2t(g):
                for n, (a, b) in enumerate(((0, 8), (8, IC))):
                    act.wait_ge(q2t_done, 2 * g + n + 1)
                    nc.scalar.activation(q2_t[:, a:b, g * G:(g + 1) * G],
                                         bank(6)[:, 0:(b - a) * G // 2].bitcast(BF16).rearrange("p (c t) -> p c t", t=G),
                                         ACT.Copy).then_inc(q2t_ready, 1)

            sigmoid(0)
            square2(0)
            for g in range(NG):
                if g + 1 < NG:
                    sigmoid(g + 1)
                    square2(g + 1)
                copy_q2t(g)
            act.wait_ge(rw_done, 1)
            nc.scalar.activation(rw_t[:, :, :], bank(6)[:, 0:DC * NE].rearrange("p (c e) -> p c e", c=DC), ACT.Copy
                                 ).then_inc(rw_ready, 1)
            for g in range(NG):
                act.wait_ge(xrt_done, g + 1)
                if g:
                    act.wait_ge(logit_done, g)
                nc.scalar.activation(xr_t[:, :, :], bank(g % 2)[:, 0:DC * G].rearrange("p (c t) -> p c t", c=DC), ACT.Copy
                                     ).then_inc(xrt_ready, 1)
                act.wait_ge(max_ready, g + 1)
                nc.scalar.activation(expo[:, :], logit[:, :], ACT.Exp, bias=neg_max[:, 0:1], accum_out=esum[:, 0:1]
                                     ).then_inc(exp_ready, 1)

            def gu_high(st, d):
                s = st.slot(d)
                act.wait_ge(ld_gu[s], 2 * st.dma(d))
                nc.scalar.activation(whl[:, s, 0, 0:WG], raw[:, s, 0:WG], ACT.Copy).then_inc(guh_ready, 1)

            def down_high(st, d):
                s = st.slot(d)
                act.wait_ge(ld_dn[s], st.dma(d))
                nc.scalar.activation(whl[0:IH, s, 0, WG:WCOLS], raw[0:IH, s, WG:WCOLS], ACT.Copy).then_inc(dnh_ready, 1)

            def x_high(st, d):
                act.wait_ge(xt_done, st.upto(d))
                nc.scalar.activation(xh[:, :, :], bank(6).rearrange("p (c t) -> p c t", c=4), ACT.Copy
                                     ).then_inc(xh_ready, 1)

            gu_high(Step(0, 0), 0)
            gu_high(Step(0, 0), 1)
            down_high(Step(0, 0), 0)
            x_high(Step(0, 0), 0)
            act.wait_ge(table_ready, 1)
            half = act.value_load(more_i[0:1, 0:1], min_val=0, max_val=14) + NE // 2
            for st in steps(act, half):
                if not st.last:
                    act.wait_ge(gu_done, st.upto(0))
                    nc.scalar.activation(sg[:, :], bank(4)[:, 0:IE], ACT.Silu).then_inc(silu_ready, 1)
                    x_high(st, 1)
                    act.wait_ge(ht_done, st.upto(0))
                    nc.scalar.activation(hh[:, :, :], bank(5)[0:IH, 0:2 * P].rearrange("p (c t) -> p c t", c=2), ACT.Copy
                                         ).then_inc(hh_ready, 1)
                if not st.first and not (st.last and st.u == 1):
                    s = st.slot(-1)
                    act.wait_ge(y_done, st.upto(-1))
                    act.wait_ge(gate_col, st.upto(-1))
                    nc.scalar.activation(yh[:, s, :], bank(7), ACT.Copy, scale=gate[:, s:s + 1]).then_inc(yh_ready, 1)
                if not st.last:
                    gu_high(st, 2)
                    down_high(st, 1)

        @block.tensor
        def _(pe):
            def three(dst, ah, al, bh, bl, start, stop):
                nc.tensor.matmul(dst, ah, bh, start=start, stop=False)
                nc.tensor.matmul(dst, ah, bl, start=False, stop=False)
                return nc.tensor.matmul(dst, al, bh, start=False, stop=stop)

            def transpose_patch(g):
                pe.wait_ge(xhat_ready, g + 1)
                if g:
                    pe.wait_ge(zf_ready, g)
                for c in range(KC):
                    last = nc.tensor.transpose(bank(c // 4)[:, (c % 4) * G:(c % 4 + 1) * G], xt[:, g, c::KC],
                                               ident[0:G, 0:G])
                last.then_inc(t1_done, 1)

            def tok_product(g):
                acc = bank(2 + g % 2)[0:G, :]
                pe.wait_ge(zl_ready, g + 1)
                if g == 0:
                    pe.wait_ge(wtok_l_ready, 2)
                if g >= 2:
                    pe.wait_ge(tok_read, g - 1)
                for c in range(KC):
                    last = three(acc, zh[:, c, :], zl[:, c, :], wtok_h[:, c, :], wtok_l[:, c, :], c == 0, c == KC - 1)
                last.then_inc(tok_done, 1)

            def transpose_q1(g):
                pe.wait_ge(q1_ready, g + 1)
                if g:
                    pe.wait_ge(q1t_ready, g)
                for c in range(DC):
                    last = nc.tensor.transpose(bank(4)[:, c * G // 2:(c + 1) * G // 2].bitcast(BF16),
                                               q1[:, c * 128:(c + 1) * 128], ident16[0:G, 0:G])
                last.then_inc(q1t_done, 1)

            def total(which):
                n = 8 if which == 0 else DC
                nc.tensor.matmul(bank(5)[:, 8 * which:8 * which + n], ones[:, :], abs_sum[:, which, 0:n],
                                 start=True, stop=True).then_inc(tot_done, 1)

            def transpose_w(n):
                pe.wait_ge(tern_ready, n + 1)
                if n >= 2:
                    pe.wait_ge(wt_ready, n - 1)
                dst = bank(6 + n % 2).bitcast(BF16)
                if n < 11:
                    pairs = [(b * DC + c, b * DC + c) for b in range(2) for c in range(DC)]
                else:
                    w = min(2, IC - 2 * (n - 11))
                    pairs = [(m * w + c, c * DC + m) for c in range(w) for m in range(DC)]
                for a, b in pairs:
                    last = nc.tensor.transpose(dst[:, b * 128:(b + 1) * 128], tern[:, n % 2, a * 128:(a + 1) * 128],
                                               ident16[:, :])
                last.then_inc(wt_done, 1)

            pe.wait_ge(consts, 1)
            transpose_patch(0)
            for g in range(NG):
                if g + 1 < NG:
                    transpose_patch(g + 1)
                tok_product(g)
                if g:
                    transpose_q1(g - 1)
            pe.wait_ge(abs_in_ready, 8)
            total(0)
            for n in range(6):
                transpose_w(n)
            transpose_q1(3)
            for n in range(6, 11):
                transpose_w(n)

            def gate_value(g):
                if g == 0:
                    pe.wait_ge(wt_ready, 11)
                    pe.wait_ge(q1t_ready, NG)
                else:
                    pe.wait_ge(gate_read, g)
                    pe.wait_ge(swi_ready, g)
                for half_ in range(2):
                    for a in range(0, I1, 512):
                        w = min(512, I1 - a)
                        for c in range(DC):
                            last = nc.tensor.matmul(bank(3 * half_, 3)[0:G, a:a + w], q1_t[:, c, g * G:(g + 1) * G],
                                                    w_t4[:, c, half_ * I1 + a:half_ * I1 + a + w],
                                                    start=c == 0, stop=c == DC - 1)
                last.then_inc(gv_done, 1)

            def transpose_q2(g):
                pe.wait_ge(q2_ready, g + 1)
                for n, (a, b) in enumerate(((0, 8), (8, IC))):
                    if g or n:
                        pe.wait_ge(q2t_ready, 2 * g + n)
                    for c in range(a, b):
                        last = nc.tensor.transpose(bank(6)[:, (c - a) * G // 2:(c - a + 1) * G // 2].bitcast(BF16),
                                                   q2[:, c * 128:(c + 1) * 128], ident16[0:G, 0:G])
                    last.then_inc(q2t_done, 1)

            def mlp_out(g):
                pe.wait_ge(q2t_ready, 2 * g + 2)
                if g:
                    pe.wait_ge(z_read, g)
                for c in range(IC):
                    last = nc.tensor.matmul(bank(7)[0:G, :], q2_t[:, c, g * G:(g + 1) * G], wd_t[:, c, :],
                                            start=c == 0, stop=c == IC - 1)
                last.then_inc(z_done, 1)

            pe.wait_ge(tot_in, 1)
            pe.wait_ge(abs_down_ready, DC)
            total(1)
            for n in range(11, 17):
                transpose_w(n)
            pe.wait_ge(tot_in, 2)
            pe.wait_ge(wt_ready, 17)
            gate_value(0)
            for g in range(NG):
                if g + 1 < NG:
                    gate_value(g + 1)
                transpose_q2(g)
                mlp_out(g)

            for c in range(DC):
                last = nc.tensor.transpose(bank(6)[:, c * NE:(c + 1) * NE], rw_raw[:, c * 128:(c + 1) * 128],
                                           ident[0:NE, 0:NE])
            last.then_inc(rw_done, 1)
            pe.wait_ge(rw_ready, 1)
            for g in range(NG):
                pe.wait_ge(row_ready, g + 1)
                if g >= 2:
                    pe.wait_ge(xrt_ready, g - 1)
                for c in range(DC):
                    last = nc.tensor.transpose(bank(g % 2)[:, c * G:(c + 1) * G], rows[:, g, c * 128:(c + 1) * 128],
                                               ident[0:G, 0:G])
                last.then_inc(xrt_done, 1)
                pe.wait_ge(xrt_ready, g + 1)
                for c in range(DC):
                    last = nc.tensor.matmul(bank(2 + g)[0:G, 0:NE], xr_t[:, c, :], rw_t[:, c, :],
                                            start=c == 0, stop=c == DC - 1)
                last.then_inc(logit_done, 1)
            pe.wait_ge(consts, 9)
            pe.wait_ge(gate_ready, NG)
            for g in range(NG):
                nc.tensor.matmul(bank(6)[0:NE, 0:TOK], mask[:, g, :], before[:, g, :], start=g == 0, stop=g == NG - 1)
            for g in range(NG):
                last = nc.tensor.transpose(bank(7)[0:NE, g * G // 2:(g + 1) * G // 2].bitcast(BF16), mask[:, g, :],
                                           ident16[0:G, 0:G])
            last.then_inc(rank_done, 1)
            pe.wait_ge(over_ready, 1)
            nc.tensor.matmul(bank(0)[0:NE, 0:1], before_e[:, :], n_over[:, :], start=True, stop=True)
            nc.tensor.matmul(bank(0)[0:1, 1:2], n_over[:, :], ones[0:NE, 0:1], start=True, stop=True
                             ).then_inc(start_done, 1)
            pe.wait_ge(owner_ready, 1)
            nc.tensor.matmul(bank(1)[0:NT, 0:TOK], owner[:, :], place[:, :], start=True, stop=True)
            nc.tensor.matmul(bank(2)[0:NT, 0:1], shift[:, :], ones16[:, :], start=True, stop=True)
            nc.tensor.matmul(bank(3)[0:1, 0:NT], iota_e16[:, :], owner[:, :], start=True, stop=True
                             ).then_inc(tables_done, 1)

            pe.wait_ge(table_ready, 1)
            for g in range(NG):
                nc.tensor.matmul(bank(g)[0:G, :], zeros16[:, 0:G], zeros16[:, :], start=True, stop=False,
                                 skip_group_check=True)

            def transpose_x(st, d):
                s = st.slot(d)
                pe.wait_ge(ld_got[s], st.dma(d))
                for c in range(4):
                    last = nc.tensor.transpose(bank(6)[:, c * P:(c + 1) * P], got[:, s, c:D:4], ident[:, :])
                last.then_inc(xt_done, 1)

            def gate_up(st):
                s = st.u
                pe.wait_ge(xl_ready, st.upto(0))
                pe.wait_ge(gul_ready, st.upto(0))
                wait(pe, hid_ready, st.upto(-1))
                wh = whl[:, s, 0, 0:WG].rearrange("p (n c i) -> p n c i", n=2, c=4)
                wl = whl[:, s, 1, 0:WG].rearrange("p (n c i) -> p n c i", n=2, c=4)
                dst = bank(4)[:, 0:2 * IE].rearrange("p (n i) -> p n i", n=2)
                for c in range(4):
                    last = three(dst, xh[:, c, :], xl[:, c, :], wh[:, :, c, :], wl[:, :, c, :], c == 0, c == 3)
                last.then_inc(gu_done, 1)

            def down(st):
                s = st.slot(-1)
                pe.wait_ge(hl_ready, st.upto(-1))
                pe.wait_ge(dnl_ready, st.upto(-1))
                wait(pe, yl_ready, st.upto(-2))
                wh = whl[0:IH, s, 0, WG:WCOLS].rearrange("p (c d) -> p c d", c=2)
                wl = whl[0:IH, s, 1, WG:WCOLS].rearrange("p (c d) -> p c d", c=2)
                for c in range(2):
                    last = three(bank(7), hh[:, c, :], hl[:, c, :], wh[:, c, :], wl[:, c, :], c == 0, c == 1)
                last.then_inc(y_done, 1)

            def add_rows(st, stop=False):
                s = st.slot(-2)
                pe.wait_ge(sel_ready, st.upto(-2))
                pe.wait_ge(yl_ready, st.upto(-2))
                for g in range(NG):
                    for n, part in enumerate((yh, yl)):
                        last = nc.tensor.matmul(bank(g)[0:G, :], sel[:, s, g * G:(g + 1) * G], part[:, s, :],
                                                start=False, stop=stop and n == 1, skip_group_check=True)
                last.then_inc(sum_done, 1)

            transpose_x(Step(0, 0), 0)
            half = pe.value_load(more_i[0:1, 0:1], min_val=0, max_val=14) + NE // 2
            for st in steps(pe, half):
                if not st.last:
                    gate_up(st)
                    transpose_x(st, 1)
                if not st.first and not (st.last and st.u == 1):
                    down(st)
                if not st.last:
                    pe.wait_ge(hid_ready, st.upto(0))
                    for c in range(2):
                        last = nc.tensor.transpose(bank(5)[0:IH, c * P:(c + 1) * P], hid[:, c::2], ident[:, :])
                    last.then_inc(ht_done, 1)
                if not isinstance(st.k, int):
                    add_rows(st, stop=st.last and st.u == 1)

        @block.vector
        def _(dve):
            chain = [0]

            def link(ins):
                chain[0] += 1
                ins.then_inc(dve_chain, 1)
                dve.wait_ge(dve_chain, chain[0])

            def moments(src, n):
                for c in range(n // 512):
                    ins = nc.vector.bn_stats(stats[:, c, :], src[:, c * 512:(c + 1) * 512])
                link(ins)
                link(nc.vector.bn_aggr(mv[:, :], stats[:, 0:n // 512, :].rearrange("p c s -> p (c s)")))

            powers = [0]

            def power(src, scale, eps):
                n = powers[0]
                powers[0] += 1
                nc.vector.tensor_scalar(root_in[:, n:n + 1], src, scale, eps, ALU.mult, ALU.add).then_inc(root_ready, 1)
                dve.wait_ge(root_done, n + 1)
                return root_out[:, n:n + 1]

            def norm_patch(g):
                dve.wait_ge(ld_x[g], 16 * 16)
                moments(xt[:, g, :], KIN)
                rstd = power(mv[:, 1:2], 1.0, EPS6)
                nc.vector.tensor_scalar(xt[:, g, :], xt[:, g, :], mv[:, 0:1], rstd[:, 0:1], ALU.subtract, ALU.mult
                                        ).then_inc(xhat_ready, 1)

            def patch_low(g):
                dve.wait_ge(zh_ready, g + 1)
                nc.vector.tensor_tensor(zl[:, :, :], zf[:, :, :], zh[:, :, :].bitcast(F32), ALU.subtract
                                        ).then_inc(zl_ready, 1)

            def quant_scale(which, g, src_max):
                link(nc.vector.tensor_scalar(amax[:, 4 * which + g:4 * which + g + 1], src_max, EPS5, None, ALU.max))
                link(nc.vector.reciprocal(qscale[:, :], amax[:, 4 * which + g:4 * which + g + 1]))
                link(nc.vector.tensor_scalar(qscale[:, :], qscale[:, :], 127.0, None, ALU.mult))
                link(nc.vector.reciprocal(deq[:, 4 * which + g:4 * which + g + 1], qscale[:, :]))

            def tok_low(n):
                dve.wait_ge(wtok_h_ready, n + 1)
                nc.vector.tensor_tensor(wtok_l[:, 4 * n:4 * n + 4, :], wtok_raw[:, 4 * n:4 * n + 4, :],
                                        wtok_h[:, 4 * n:4 * n + 4, :].bitcast(F32), ALU.subtract
                                        ).then_inc(wtok_l_ready, 1)

            def hidden(g):
                if g == 0:
                    dve.wait_ge(ld_vec, 16 * 8)
                dve.wait_ge(tok_done, g + 1)
                ins = nc.vector.tensor_tensor(h[:, g, :], bank(2 + g % 2)[0:G, :], bias_bc[:, :], ALU.add)
                ins.then_inc(tok_read, 1)
                dve.wait_ge(tok_read, g + 1)
                hg = h[:, g, :]
                moments(hg, D)
                rstd = power(mv[:, 1:2], 1.0, EPS6)
                link(nc.vector.tensor_scalar(hg, hg, mv[:, 0:1], rstd[:, 0:1], ALU.subtract, ALU.mult))
                link(nc.vector.tensor_tensor(hg, hg, g2_bc[:, :], ALU.mult))
                link(nc.vector.tensor_tensor(hg, hg, b2_bc[:, :], ALU.add))
                moments(hg, D)
                rstd = power(mv[:, 1:2], 1.0, EPS5)
                nc.vector.tensor_scalar(h_work[:, :], hg, mv[:, 0:1], rstd[:, 0:1], ALU.subtract, ALU.mult
                                        ).then_inc(ssq1_in, 1)
                dve.wait_ge(ssq1_ready, g + 1)
                rms = power(ssq[:, g:g + 1], 1.0 / D, EPS6)
                link(nc.vector.scalar_tensor_tensor(h_work[:, :], h_work[:, :], rms[:, 0:1], gin_bc[:, :], ALU.mult, ALU.mult))
                link(nc.vector.tensor_reduce(amax[:, g:g + 1], h_work[:, :], AX.X, ALU.max, apply_absolute_value=True))
                quant_scale(0, g, amax[:, g:g + 1])
                link(nc.vector.tensor_scalar(h_work[:, :], h_work[:, :], qscale[:, 0:1], MAGIC, ALU.mult, ALU.add))
                if g:
                    dve.wait_ge(q1t_done, g)
                nc.vector.tensor_scalar(q1[:, :], h_work[:, :], -MAGIC, 127.0, ALU.add, ALU.min).then_inc(q1_ready, 1)

            def weight_scale(which, n, size):
                dve.wait_ge(tot_done, which + 1)
                dve_ins = nc.vector.tensor_reduce(abs_tot[:, which:which + 1], bank(5)[:, 8 * which:8 * which + n], AX.X, ALU.add)
                dve_ins.then_inc(tot_in, 1)
                dve.wait_ge(tot_in, which + 1)
                link(nc.vector.tensor_scalar(wmean[:, which:which + 1], abs_tot[:, which:which + 1], 1.0 / size, EPS5,
                                             ALU.mult, ALU.max))
                link(nc.vector.reciprocal(wscale[:, which:which + 1], wmean[:, which:which + 1]))

            def levels(n):
                which = 0 if n < 11 else 1
                if which == 0:
                    src = w_in_raw[:, 2 * n:2 * n + 2, :]
                    dst = tern[:, n % 2, :].rearrange("p (b d) -> p b d", b=2)
                else:
                    c0 = 2 * (n - 11)
                    w = min(2, IC - c0)
                    src = w_down_raw[:, :, c0 * 128:(c0 + w) * 128]
                    dst = tern[:, n % 2, 0:DC * w * 128].rearrange("p (m i) -> p m i", m=DC)
                link(nc.vector.tensor_scalar(src, src, wscale[:, which:which + 1], MAGIC, ALU.mult, ALU.add))
                if n >= 2:
                    dve.wait_ge(wt_done, n - 1)
                nc.vector.tensor_scalar(dst, src, -MAGIC, None, ALU.add).then_inc(tern_ready, 1)

            dve.wait_ge(consts, 1)
            norm_patch(0)
            norm_patch(1)
            tok_low(0)
            patch_low(0)
            tok_low(1)
            norm_patch(2)
            norm_patch(3)
            patch_low(1)
            hidden(0)
            patch_low(2)
            hidden(1)
            patch_low(3)
            hidden(2)
            weight_scale(0, 8, 2 * I1 * D)
            for n in range(6):
                levels(n)
            hidden(3)
            for n in range(6, 11):
                levels(n)
            weight_scale(1, DC, I1 * D)
            for n in range(11, 17):
                levels(n)
            link(nc.vector.tensor_scalar(deq[:, 0:NG], deq[:, 0:NG], wmean[0:G, 0:1], None, ALU.mult))
            nc.vector.tensor_tensor(deq_sq[:, :], deq[:, 0:NG], deq[:, 0:NG], ALU.mult).then_inc(scales_ready, 1)
            dve.wait_ge(scales_ready, 1)

            def swiglu(g):
                s = g % 2
                v = scr[:, s, :]
                dve.wait_ge(sig_ready, g + 1)
                ins = nc.vector.tensor_tensor(v, bank(0, 3)[0:G, 0:I1], v, ALU.mult)
                ins.then_inc(gate_read, 1)
                dve.wait_ge(gate_read, g + 1)
                nc.vector.scalar_tensor_tensor(v, bank(3, 3)[0:G, 0:I1], deq_sq[:, g:g + 1], v, ALU.mult, ALU.mult
                                               ).then_inc(swi_ready, 1)

            def quantise2(g):
                v = scr[:, g % 2, :]
                dve.wait_ge(ssq2_ready, g + 1)
                rms = power(ssq[:, 4 + g:5 + g], 1.0 / I1, EPS6)
                link(nc.vector.scalar_tensor_tensor(v, v, rms[:, 0:1], gdn_bc[:, :], ALU.mult, ALU.mult))
                link(nc.vector.tensor_reduce(amax[:, 4 + g:5 + g], v, AX.X, ALU.max, apply_absolute_value=True))
                quant_scale(1, g, amax[:, 4 + g:5 + g])
                link(nc.vector.tensor_scalar(v, v, qscale[:, 0:1], MAGIC, ALU.mult, ALU.add))
                if g:
                    dve.wait_ge(q2t_done, 2 * g)
                nc.vector.tensor_scalar(q2[:, :], v, -MAGIC, 127.0, ALU.add, ALU.min).then_inc(q2_ready, 1)

            def residual(g):
                dve.wait_ge(z_done, g + 1)
                link(nc.vector.tensor_scalar(deq2[:, :], deq[:, 4 + g:5 + g], wmean[0:G, 1:2], None, ALU.mult))
                nc.vector.scalar_tensor_tensor(h[:, g, :], bank(7)[0:G, :], deq2[:, 0:1], h[:, g, :], ALU.mult, ALU.add
                                               ).then_inc(z_read, 1)
                dve.wait_ge(z_read, g + 1)
                moments(h[:, g, :], D)
                rstd = power(mv[:, 1:2], 1.0, EPS5)
                nc.vector.tensor_scalar(rows[:, g, 0:D], h[:, g, :], mv[:, 0:1], rstd[:, 0:1], ALU.subtract, ALU.mult
                                        ).then_inc(row_ready, 1)

            swiglu(0)
            quantise2(0)
            for g in range(NG):
                if g + 1 < NG:
                    swiglu(g + 1)
                    quantise2(g + 1)
                residual(g)

            for g in range(NG):
                dve.wait_ge(logit_done, g + 1)
                link(nc.vector.tensor_copy(logit[:, :], bank(2 + g)[0:G, 0:NE]))
                link(nc.vector.max(top8[:, :], logit[:, :]))
                nc.vector.tensor_scalar(neg_max[:, :], top8[:, 0:1], -1.0, None, ALU.mult).then_inc(max_ready, 1)
                link(nc.vector.match_replace(zapped[:, :], top8[:, :], logit[:, :], -3.0e38))
                link(nc.vector.tensor_tensor(mask[:, g, :], zapped[:, :], logit[:, :], ALU.not_equal))
                dve.wait_ge(exp_ready, g + 1)
                link(nc.vector.reciprocal(esum[:, :], esum[:, :]))
                link(nc.vector.scalar_tensor_tensor(picked[:, :], expo[:, :], esum[:, 0:1], mask[:, g, :], ALU.mult, ALU.mult,
                                                    accum_out=psum8[:, 0:1]))
                link(nc.vector.reciprocal(psum8[:, :], psum8[:, :]))
                nc.vector.tensor_scalar(rows[:, g, D:ROW], picked[:, :], psum8[:, 0:1], None, ALU.mult).then_inc(gate_ready, 1)

            dve.wait_ge(rank_done, 1)
            rank = bank(6)[0:NE, 0:TOK]
            link(nc.vector.tensor_copy(mask_t[:, :], bank(7)[0:NE, 0:TOK // 2].bitcast(BF16)))
            link(nc.vector.tensor_tensor(count[:, :], mask_t[:, TOK - 1:TOK], rank[:, TOK - 1:TOK], ALU.add))
            link(nc.vector.tensor_scalar(n_over[:, :], count[:, :], float(P), None, ALU.is_gt))
            link(nc.vector.scalar_tensor_tensor(n_over[:, :], count[:, :], 2.0 * P, n_over[:, :], ALU.is_gt, ALU.add))
            nc.vector.scalar_tensor_tensor(n_over[:, :], count[:, :], 3.0 * P, n_over[:, :], ALU.is_gt, ALU.add
                                           ).then_inc(over_ready, 1)
            link(nc.vector.tensor_scalar(mask_t[:, :], mask_t[:, :], FAR, -FAR, ALU.mult, ALU.add))
            link(nc.vector.tensor_tensor(place[:, :], mask_t[:, :], rank, ALU.add))
            dve.wait_ge(start_done, 1)
            link(nc.vector.tensor_scalar(start[:, :], bank(0)[0:NE, 0:1], float(NE), None, ALU.add))
            link(nc.vector.tensor_scalar(halff[:, :], bank(0)[0:1, 1:2], 0.5, 0.25, ALU.mult, ALU.add))
            link(nc.vector.tensor_scalar(halff[:, :], halff[:, :], MAGIC, -MAGIC, ALU.add, ALU.add))
            link(nc.vector.tensor_copy(more_i[:, :], halff[:, :]))
            link(nc.vector.tensor_scalar(t_a[:, :], iota_t[:, :], start[:, 0:1], None, ALU.subtract))
            link(nc.vector.tensor_scalar(t_b[:, :], t_a[:, :], 0.0, None, ALU.is_ge))
            link(nc.vector.scalar_tensor_tensor(t_b[:, :], t_a[:, :], n_over[:, 0:1], t_b[:, :], ALU.is_lt, ALU.mult))
            link(nc.vector.tensor_scalar(t_c[:, :], iota_t[:, :], iota_e[:, 0:1], None, ALU.is_equal))
            link(nc.vector.tensor_tensor(t_c[:, :], t_c[:, :], t_b[:, :], ALU.add))
            link(nc.vector.tensor_copy(owner[:, :], t_c[:, :]))
            link(nc.vector.scalar_tensor_tensor(t_b[:, :], t_a[:, :], 1.0, t_b[:, :], ALU.add, ALU.mult))
            link(nc.vector.tensor_scalar(t_b[:, :], t_b[:, :], -float(P), None, ALU.mult))
            nc.vector.scalar_tensor_tensor(shift[:, :], t_c[:, :], FAR, t_b[:, :], ALU.mult, ALU.add
                                           ).then_inc(owner_ready, 1)
            dve.wait_ge(tables_done, 1)
            link(nc.vector.tensor_scalar(shift_c[:, :], bank(2)[0:NT, 0:1], -FAR, None, ALU.add))
            nc.vector.tensor_scalar(place_tile[:, :], bank(1)[0:NT, 0:TOK], shift_c[:, 0:1], None, ALU.add
                                    ).then_inc(place_ready, 1)
            nc.vector.tensor_copy(owner_row[:, :], bank(3)[0:1, 0:NT]).then_inc(table_ready, 1)

            def find(st, d):
                s = st.slot(d)
                dve.wait_ge(ld_pa[s], st.dma(d))
                nc.vector.scalar_tensor_tensor(hit[:, :], place_a[:, s, :], iota_p[:, 0:1], trow[:, :], ALU.is_equal, ALU.mult,
                                               accum_out=idx_f[:, s:s + 1]).then_inc(hit_ready, 1)
                dve.wait_ge(hit_ready, st.upto(d))
                nc.vector.tensor_copy(idx[:, s:s + 1], idx_f[:, s:s + 1]).then_inc(idx_ready, 1)

            def gates(st, d):
                s = st.slot(d)
                e = dve.value_load(owner_row[0:1, bass.ds(st.tile(d), 1)], min_val=0, max_val=NE - 1)
                dve.wait_ge(ld_got[s], st.dma(d))
                wait(dve, yl_ready, st.upto(d - 2))
                nc.vector.tensor_copy(gate[:, s:s + 1], got[:, s, bass.ds(e + D, 1)]).then_inc(gate_col, 1)

            def x_low(st, d):
                dve.wait_ge(xh_ready, st.upto(d))
                nc.vector.tensor_tensor(xl[:, :, :], bank(6).rearrange("p (c t) -> p c t", c=4), xh[:, :, :].bitcast(F32),
                                        ALU.subtract).then_inc(xl_ready, 1)

            def down_low(st, d):
                s = st.slot(d)
                dve.wait_ge(dnh_ready, st.upto(d))
                nc.vector.tensor_tensor(whl[0:IH, s, 1, WG:WCOLS], raw[0:IH, s, WG:WCOLS],
                                        whl[0:IH, s, 0, WG:WCOLS].bitcast(F32), ALU.subtract).then_inc(dnl_ready, 1)

            zero = Step(0, 0)
            find(zero, 0)
            find(zero, 1)
            gates(zero, 0)
            find(zero, 2)
            x_low(zero, 0)
            down_low(zero, 0)
            half = dve.value_load(more_i[0:1, 0:1], min_val=0, max_val=14) + NE // 2
            for st in steps(dve, half):
                if not st.last:
                    dve.wait_ge(silu_ready, st.upto(0))
                    nc.vector.tensor_tensor(hid[:, :], bank(4)[:, IE:2 * IE], sg[:, :], ALU.mult).then_inc(hid_ready, 1)
                    x_low(st, 1)
                    dve.wait_ge(hh_ready, st.upto(0))
                    nc.vector.tensor_tensor(hl[:, :, :], bank(5)[0:IH, 0:2 * P].rearrange("p (c t) -> p c t", c=2),
                                            hh[:, :, :].bitcast(F32), ALU.subtract).then_inc(hl_ready, 1)
                if not st.first and not (st.last and st.u == 1):
                    s = st.slot(-1)
                    dve.wait_ge(yh_ready, st.upto(-1))
                    nc.vector.scalar_tensor_tensor(yl[:, s, :], bank(7), gate[:, s:s + 1], yh[:, s, :].bitcast(F32),
                                                   ALU.mult, ALU.subtract).then_inc(yl_ready, 1)
                    dve.wait_ge(ld_ps[s], st.dma(-1))
                    nc.vector.tensor_scalar(sel[:, s, :], place_s[:, s, :], iota_p[:, 0:1], None, ALU.is_equal
                                            ).then_inc(sel_ready, 1)
                if not st.last:
                    gates(st, 1)
                    down_low(st, 1)
                    find(st, 3)
            dve.wait_ge(sum_done, 2 * half)
            for g in range(NG):
                nc.vector.tensor_tensor(fin[:, g, :], bank(g)[0:G, :], h[:, g, :], ALU.add).then_inc(fin_ready, 1)


_ARGS = ["x", "L0_tok_W", "L0_tok_b", "L0_tok_g1", "L0_tok_b1", "L0_tok_g2", "L0_tok_b2", "L0_attn_w_gate",
         "L0_attn_g_gate", "L0_attn_w_down", "L0_attn_g_down", "L0_ffn_router_w", "L0_ffn_w_gate", "L0_ffn_w_up",
         "L0_ffn_w_down"]


def kernel(**inputs):
    import concourse.bacc as bacc
    import numpy as np
    from concourse.bass_utils import run_bass_kernel_spmd

    nc = bacc.Bacc("TRN2", target_bir_lowering=False, num_devices=1)
    arrays, args = {}, []
    for name in _ARGS:
        a = np.ascontiguousarray(inputs[name])
        arrays[f"in_{name}"] = a
        args.append(nc.dram_tensor(f"in_{name}", a.shape, mybir.dt.from_np(a.dtype), kind="ExternalInput").ap())
    out = nc.dram_tensor("out_0", (NB, NPATCH, D), F32, kind="ExternalOutput").ap()
    program(nc, *args, out)
    r = run_bass_kernel_spmd(nc, [arrays], core_ids=[0])
    return r.results[0]["out_0"]
```

```python
import concourse.bass as bass
from concourse import mybir
from contextlib import ExitStack

F32 = mybir.dt.float32
F32R = mybir.dt.float32r
BF16 = mybir.dt.bfloat16
F16 = mybir.dt.float16
I32 = mybir.dt.int32
ALU = mybir.AluOpType
ACT = mybir.ActivationFunctionType
AX = mybir.AxisListType

NB, NPATCH, TIN, FEAT = 64, 7, 16, 64
TOK = NB * NPATCH
NG, G = 4, TOK // 4
KIN = TIN * FEAT
KC = KIN // 128
D = 512
DC = D // 128
I1 = 1408
IC = I1 // 128
NE, TOPK, IE = 32, 8, 192
P = 128
Q2T_A, Q2T_B = (0, 9), (9, 11)
NT = 64
ROW = D + NE
IH = IE // 2
WG = 2 * 4 * IE
WCOLS = WG + 2 * D
MAGIC = 1.5 * 2.0 ** 23
LEVEL_MAGIC = MAGIC + 0x3F80
FAR = 1000.0
EPS6, EPS5 = 1e-6, 1e-5
N_ROOTS = 6 * NG


def wait(eng, sem, value):
    if isinstance(value, int) and value <= 0:
        return
    eng.wait_ge(sem, value)


def pieces(g):
    runs = []
    t = g * G
    while t < (g + 1) * G:
        size = min(NB - t % NB, (g + 1) * G - t)
        runs.append((t - g * G, t // NB, t % NB, size))
        t += size
    return runs


class Step:

    def __init__(self, k, u, first=False, last=False):
        self.k, self.u, self.first, self.last = k, u, first, last

    def upto(self, d):
        return 2 * self.k + (self.u + d + 1)

    def tile(self, d):
        return 2 * self.k + (self.u + d)

    def slot(self, d):
        return (self.u + d) % 2

    def dma(self, d):
        return 16 * self.k + 16 * ((self.u + d) // 2 + 1)


def steps(eng, half):
    yield Step(0, 0, first=True)
    yield Step(0, 1, first=False)
    with eng.Fori(1, half) as k:
        yield Step(k, 0)
        yield Step(k, 1)
    yield Step(half, 0, last=True)
    yield Step(half, 1, last=True)


def program(nc, x, w_tok, b_tok, g1, b1, g2, b2, w_in, g_in, w_down, g_down, w_router, we_gate, we_up, we_down, out):
    rows_dram = nc.dram_tensor("token_rows", (TOK, ROW), F32).ap()
    place_dram = nc.dram_tensor("places", (NT, TOK), F16).ap()
    ctx = ExitStack()
    with ctx:
        def sb(name, shape, dt):
            return ctx.enter_context(nc.sbuf_tensor(name, shape, dt))

        def sem(name):
            return ctx.enter_context(nc.semaphore(name))

        big = sb("big", [128, 22 * D], F32)
        w_in_raw = big[:, :].rearrange("p (b d) -> p b d", b=22)
        at = [0]

        def late(cols, dt=F32):
            at[0] += cols
            return big[:, at[0] - cols:at[0]].bitcast(dt) if dt != F32 else big[:, at[0] - cols:at[0]]

        rows = late(NG * ROW)[0:G, :].rearrange("p (g r) -> p g r", g=NG)
        q2 = late(I1 // 2, BF16)[0:G, :]
        got = late(2 * ROW).rearrange("p (s r) -> p s r", s=2)
        xr_t = late(DC * G).rearrange("p (c t) -> p c t", c=DC)
        place_a = late(TOK, F16).rearrange("p (s t) -> p s t", s=2)
        place_s = late(TOK, F16).rearrange("p (s t) -> p s t", s=2)
        hit = late(TOK // 2, F16)
        assert at[0] <= 11 * D
        at[0] = 11 * D
        swi = late(2 * I1)[0:G, :].rearrange("p (s i) -> p s i", s=2)
        swg = late(2 * I1)[0:G, :].rearrange("p (s i) -> p s i", s=2)
        assert at[0] <= 22 * D
        at[0] = 11 * D
        fin = late(NG * D)[0:G, :].rearrange("p (g d) -> p g d", g=NG)
        sg = late(IE)
        hid = late(IE)
        mask_t = late(TOK)[0:NE, :]
        place = late(TOK // 2, F16)[0:NE, :]
        place_tile = late(TOK // 2, F16)[0:NT, :]
        w_t = sb("w_t", [128, DC * 2 * I1], BF16)
        w_t4 = w_t[:, :].rearrange("p (c o) -> p c o", c=DC)
        xt = w_t[0:G, 0:2 * NG * KIN].bitcast(F32).rearrange("p (g k) -> p g k", g=NG)
        wd_t = sb("wd_t", [128, IC, D], BF16)
        whl = sb("whl", [128, 2, 2, WCOLS], F32R)
        whl_flat = whl[:, :, :, :].rearrange("p s h c -> p (s h c)")
        wtok_h = whl_flat[:, 0:KC * D].rearrange("p (c n) -> p c n", c=KC)
        wtok_l = whl_flat[:, KC * D:2 * KC * D].rearrange("p (c n) -> p c n", c=KC)
        yh = sb("yh", [P, 2, D], F32R)
        yl = sb("yl", [P, 2, D], F32R)
        patch_parts = [(whl_flat[:, 2 * KC * D:2 * KC * D + KC * G], whl_flat[:, 2 * KC * D + KC * G:2 * KC * D + 2 * KC * G]),
                       (yh[:, :, :].rearrange("p s d -> p (s d)")[:, 0:KC * G],
                        yl[:, :, :].rearrange("p s d -> p (s d)")[:, 0:KC * G])]
        patch_h = [high.rearrange("p (b t) -> p b t", b=2) for high, _ in patch_parts]
        patch_l = [low.rearrange("p (b t) -> p b t", b=2) for _, low in patch_parts]
        raw = sb("raw", [128, 2, WCOLS], F32)
        raw_flat = raw[:, :, :].rearrange("p s c -> p (s c)")
        wtok_raw = raw_flat[:, 0:KC * D].rearrange("p (c n) -> p c n", c=KC)
        q2_t = raw_flat[:, WCOLS:WCOLS + IC * TOK // 2].bitcast(BF16).rearrange("p (c t) -> p c t", c=IC)
        w_down_last = sb("w_down_last", [128, I1], F32)
        w_down_raw = [raw_flat[:, m * I1:(m + 1) * I1] for m in range(DC - 1)] + [w_down_last[:, :]]
        h = sb("h", [G, NG, D], F32)
        h_work = sb("h_work", [G, D], F32)
        q1_t = sb("q1_t", [128, DC, TOK], BF16)
        q1 = sb("q1", [G, 2, D], BF16)
        bias_bc = sb("bias_bc", [G, D], F32)
        g2_bc = sb("g2_bc", [G, D], F32)
        b2_bc = sb("b2_bc", [G, D], F32)
        gin_bc = sb("gin_bc", [G, D], F32)
        gdn_bc = sb("gdn_bc", [G, I1], F32)
        g1_c = sb("g1_c", [128, KC], F32)
        b1_c = sb("b1_c", [128, KC], F32)
        stats = sb("stats", [G, 2, 6], F32)
        mv = sb("mv", [G, 2], F32)
        ssq = sb("ssq", [G, 8], F32)
        amax = sb("amax", [G, 8], F32)
        qscale = sb("qscale", [G, 1], F32)
        deq = sb("deq", [G, NG], F32)
        deq_sq = sb("deq_sq", [G, NG], F32)
        deq2 = sb("deq2", [G, 1], F32)
        abs_sum = sb("abs_sum", [128, 2, 8], F32)
        abs_tot = sb("abs_tot", [128, 2], F32)
        zeros16 = sb("zeros16", [128, D], BF16)
        junk = sb("junk", [128, 3 * D], BF16)
        wmean = sb("wmean", [128, 2], F32)
        wscale = sb("wscale", [128, 2], F32)
        ident = sb("ident", [128, 128], F32)
        ident16 = sb("ident16", [128, 128], BF16)
        ones = sb("ones", [128, 128], F32)
        minus_half = sb("minus_half", [G, 1], F32)
        root_in = sb("root_in", [G, N_ROOTS], F32)
        root_out = sb("root_out", [G, N_ROOTS], F32)
        before = sb("before", [G, NG, TOK], BF16)
        rw_raw = sb("rw_raw", [NE, D], F32)
        rw_t = sb("rw_t", [128, DC, NE], F32)
        logits = sb("logits", [G, NG, NE], F32)
        minus_one = sb("minus_one", [128, 1], F32)
        magic = sb("magic", [128, 1], F32)
        fscale = sb("fscale", [G, NG], F32)
        first_pick = sb("first_pick", [NE, 4, 128], F16)
        zapped = sb("zapped", [G, NE], F32)
        top8 = sb("top8", [G, 8], F32)
        neg_max = sb("neg_max", [G, NG], F32)
        expo = sb("expo", [G, NG, NE], F32)
        esum = sb("esum", [G, NG], F32)
        picked = sb("picked", [G, NG, NE], F32)
        psum8 = sb("psum8", [G, NG], F32)
        mask = sb("mask", [G, NG, NE], BF16)
        count = sb("count", [NE, 1], F32)
        n_over = sb("n_over", [NE, 1], F32)
        start = sb("start", [NE, 1], F32)
        iota_e = sb("iota_e", [NE, 1], F32)
        iota_e16 = sb("iota_e16", [NE, 1], F16)
        iota_t = sb("iota_t", [NE, NT], F32)
        before_e = sb("before_e", [NE, NE], F32)
        ones16 = sb("ones16", [NE, 1], F16)
        t_a = sb("t_a", [NE, NT], F32)
        t_b = sb("t_b", [NE, NT], F32)
        t_c = sb("t_c", [NE, NT], F32)
        owner = sb("owner", [NE, NT], F16)
        shift = sb("shift", [NE, NT], F16)
        shift_c = sb("shift_c", [NT, 1], F32)
        owner_row = sb("owner_row", [1, NT], I32)
        halff = sb("halff", [1, 1], F32)
        more_i = sb("more_i", [1, 1], I32)
        trow = sb("trow", [128, TOK], F16)
        iota_p = sb("iota_p", [128, 1], F32)
        idx_f = sb("idx_f", [128, 2], F32)
        first_f = sb("first_f", [128, 4], F32)
        first_idx = sb("first_idx", [128, 4], I32)
        idx = sb("idx", [128, 2], I32)
        gate = sb("gate", [128, 2], F32)
        xh = sb("xh", [128, 4, P], F32R)
        xl = sb("xl", [128, 4, P], F32R)
        hh = sb("hh", [IH, 2, P], F32R)
        hl = sb("hl", [IH, 2, P], F32R)
        sel = sb("sel", [P, 2, TOK], F32R)

        ps = ctx.enter_context(nc.psum_tensor("ps", [128, 8, 512], F32))

        def bank(b, n=1):
            return ps[:, b:b + n, :].rearrange("p b c -> p (b c)")

        def levels_of(w):
            return w.bitcast(BF16)[:, 0::2]

        def patch_bank(g):
            b = (0, 6)[g % 2]
            return ps[:, b:b + 2, 0:4 * G]

        ld_x = [sem(f"ld_x{g}") for g in range(NG)]
        ld_wtok = [sem(f"ld_wtok{n}") for n in range(2)]
        ld_vec = sem("ld_vec")
        ld_late = sem("ld_late")
        ld_win = [sem(f"ld_win{n}") for n in range(4)]
        ld_wdown = [sem(f"ld_wdown{n}") for n in range(DC)]
        ld_gu = [sem(f"ld_gu{n}") for n in range(2)]
        ld_dn = [sem(f"ld_dn{n}") for n in range(2)]
        ld_pa = [sem(f"ld_pa{n}") for n in range(2)]
        ld_ps = [sem(f"ld_ps{n}") for n in range(2)]
        ld_got = [sem(f"ld_got{n}") for n in range(2)]
        dve_chain = sem("dve_chain")
        pool_chain = sem("pool_chain")
        root_ready = sem("root_ready")
        root_done = sem("root_done")
        act_chain = sem("act_chain")
        consts = sem("consts")
        xhat_ready = sem("xhat_ready")
        t1_done = sem("t1_done")
        ph_ready = sem("ph_ready")
        pl_ready = sem("pl_ready")
        wtok_h_ready = sem("wtok_h_ready")
        wtok_l_ready = sem("wtok_l_ready")
        tok_done = sem("tok_done")
        tok_read = sem("tok_read")
        bias_done = sem("bias_done")
        bias_read = sem("bias_read")
        norm_ready = sem("norm_ready")
        affine_ready = sem("affine_ready")
        q1_ready = sem("q1_ready")
        q1t_done = sem("q1t_done")
        q1t_ready = sem("q1t_ready")
        abs_in_ready = sem("abs_in_ready")
        abs_down_ready = sem("abs_down_ready")
        tot_in = sem("tot_in")
        tot_done = sem("tot_done")
        level_ready = sem("level_ready")
        wt_done = sem("wt_done")
        wt_ready = sem("wt_ready")
        scales_ready = sem("scales_ready")
        gate_done = sem("gate_done")
        value_done = sem("value_done")
        sig_ready = sem("sig_ready")
        gate_read = sem("gate_read")
        swi_ready = sem("swi_ready")
        ssq2_ready = sem("ssq2_ready")
        swg_ready = sem("swg_ready")
        fscale_ready = sem("fscale_ready")
        scaled_ready = sem("scaled_ready")
        q2_ready = sem("q2_ready")
        q2t_done = sem("q2t_done")
        q2t_ready = sem("q2t_ready")
        z_done = sem("z_done")
        z_read = sem("z_read")
        row_ready = sem("row_ready")
        rw_done = sem("rw_done")
        rw_ready = sem("rw_ready")
        xrt_done = sem("xrt_done")
        xrt_ready = sem("xrt_ready")
        logit_done = sem("logit_done")
        logit_read = sem("logit_read")
        max_ready = sem("max_ready")
        exp_ready = sem("exp_ready")
        gate_ready = sem("gate_ready")
        rows_out = sem("rows_out")
        mask_ready = sem("mask_ready")
        rank_done = sem("rank_done")
        place16_ready = sem("place16_ready")
        first_place_done = sem("first_place_done")
        over_ready = sem("over_ready")
        start_done = sem("start_done")
        owner_ready = sem("owner_ready")
        tables_done = sem("tables_done")
        place_ready = sem("place_ready")
        place_out = sem("place_out")
        table_ready = sem("table_ready")
        hit_ready = sem("hit_ready")
        idx_ready = sem("idx_ready")
        gather_go = sem("gather_go")
        gate_col = sem("gate_col")
        guh_ready = sem("guh_ready")
        gul_ready = sem("gul_ready")
        dnh_ready = sem("dnh_ready")
        dnl_ready = sem("dnl_ready")
        xh_ready = sem("xh_ready")
        xl_ready = sem("xl_ready")
        silu_ready = sem("silu_ready")
        hid_ready = sem("hid_ready")
        hh_ready = sem("hh_ready")
        hl_ready = sem("hl_ready")
        yh_ready = sem("yh_ready")
        yl_ready = sem("yl_ready")
        sel_ready = sem("sel_ready")
        gu_done = sem("gu_done")
        xt_done = sem("xt_done")
        y_done = sem("y_done")
        ht_done = sem("ht_done")
        sum_done = sem("sum_done")
        fin_ready = sem("fin_ready")
        out_done = sem("out_done")

        block = ctx.enter_context(nc.Block())
        we_gate_v = we_gate.rearrange("e (p c) i -> e p (c i)", c=4)
        we_up_v = we_up.rearrange("e (p c) i -> e p (c i)", c=4)
        we_down_v = we_down.rearrange("e (p c) d -> e p (c d)", c=2)
        ABS_PART = [0, 3, 6, 9, 11, 14, 17, 20, 22]
        WIN_PART = [0, 6, 11, 17, 22]
        win_v = w_in.rearrange("(b p) d -> p b d", p=128)
        wdown_v = w_down.rearrange("(m p) i -> p m i", p=128)

        def bcast(v, n):
            return v.rearrange("(a n) -> a n", a=1).broadcast_to([G, n])

        @block.sync
        def _(sp):
            for g in range(NG):
                for p, n, b, size in pieces(g):
                    sp.dma_start(xt[p:p + size, g, :],
                                 x[b:b + size, n * TIN:(n + 1) * TIN, :].rearrange("b t f -> b (t f)")
                                 ).then_inc(ld_x[g], 16)
                if g < 2:
                    sp.dma_start(raw_flat[:, g * 4 * D:(g + 1) * 4 * D],
                                 w_tok.rearrange("(p c) n -> p (c n)", c=KC)[:, g * 4 * D:(g + 1) * 4 * D]
                                 ).then_inc(ld_wtok[g], 16)
            for dst, src, n in ((bias_bc, b_tok, D), (g2_bc, g2, D), (b2_bc, b2, D), (gin_bc, g_in, D)):
                sp.dma_start(dst[:, :], bcast(src, n)).then_inc(ld_vec, 16)
            for n in range(4):
                a, b = WIN_PART[n], WIN_PART[n + 1]
                sp.dma_start(w_in_raw[:, a:b, :], win_v[:, a:b, :]).then_inc(ld_win[n], 16)
            sp.dma_start(gdn_bc[:, :], bcast(g_down, I1)).then_inc(ld_late, 16)
            sp.dma_start(rw_raw[:, :], w_router).then_inc(ld_late, 16)
            sp.wait_ge(wtok_l_ready, 2)
            sp.wait_ge(bias_done, 1)
            for m in range(DC):
                sp.dma_start(w_down_raw[m], wdown_v[:, m, :]).then_inc(ld_wdown[m], 16)
            sp.wait_ge(wt_done, 17)

            def load_expert(e):
                sp.dma_start(raw[:, e, 0:WG // 2], we_gate_v[e, :, :]).then_inc(ld_gu[e], 16)
                sp.dma_start(raw[:, e, WG // 2:WG], we_up_v[e, :, :]).then_inc(ld_gu[e], 16)
                sp.dma_start(raw[0:IH, e, WG:WCOLS], we_down_v[e, :, :]).then_inc(ld_dn[e], 16)

            load_expert(0)
            for g in range(NG):
                sp.wait_ge(row_ready, g + 1)
                sp.dma_start(rows_dram[g * G:(g + 1) * G, 0:D], rows[:, g, 0:D]).then_inc(rows_out, 16)
            sp.wait_ge(z_done, NG)
            load_expert(1)
            sp.wait_ge(gate_ready, 1)
            sp.dma_start(rows_dram.rearrange("(g p) r -> p g r", g=NG)[:, :, D:ROW], rows[:, :, D:ROW]).then_inc(rows_out, 16)
            sp.wait_ge(place_ready, 1)
            sp.dma_start(place_dram[:, :], place_tile[:, :]).then_inc(place_out, 16)
            sp.wait_ge(place_out, 16)
            sp.wait_ge(table_ready, 1)
            half = sp.value_load(more_i[0:1, 0:1], min_val=0, max_val=14) + NE // 2

            def load_place(dst, sems, t, s):
                sp.dma_start(dst[:, s, :], place_dram[bass.ds(t, 1), :].broadcast_to([128, TOK])).then_inc(sems[s], 16)

            def load_tile(st):
                u = st.u
                e = sp.value_load(owner_row[0:1, bass.ds(st.tile(0), 1)], min_val=0, max_val=NE - 1)
                wait(sp, gul_ready, st.upto(-2))
                sp.dma_start(raw[:, u, 0:WG // 2], we_gate_v[bass.ds(e, 1), :, :]).then_inc(ld_gu[u], 16)
                sp.dma_start(raw[:, u, WG // 2:WG], we_up_v[bass.ds(e, 1), :, :]).then_inc(ld_gu[u], 16)
                wait(sp, idx_ready, st.upto(0))
                load_place(place_a, ld_pa, st.tile(2), u)
                wait(sp, dnl_ready, st.upto(-2))
                sp.dma_start(raw[0:IH, u, WG:WCOLS], we_down_v[bass.ds(e, 1), :, :]).then_inc(ld_dn[u], 16)
                wait(sp, sel_ready, st.upto(-4))
                load_place(place_s, ld_ps, st.tile(-2), u)

            load_tile(Step(1, 0))
            load_tile(Step(1, 1))
            with sp.Fori(2, half + 1) as k:
                load_tile(Step(k, 0))
                load_tile(Step(k, 1))
            for g in range(NG):
                sp.wait_ge(fin_ready, g + 1)
                for p, n, b, size in pieces(g):
                    sp.dma_start(out[b:b + size, n, :], fin[p:p + size, g, :]).then_inc(out_done, 16)
            sp.wait_ge(out_done, 16 * sum(len(pieces(g)) for g in range(NG)))

        @block.gpsimd
        def _(pool):
            chain = [0]

            def link(ins):
                chain[0] += 1
                ins.then_inc(pool_chain, 1)
                pool.wait_ge(pool_chain, chain[0])

            link(nc.gpsimd.memset(ones[:, :], 1.0))
            link(nc.gpsimd.memset(ident[:, :], 0.0))
            link(nc.gpsimd.affine_select(out=ident[:, :], in_=ident[:, :], compare_op=ALU.not_equal, fill=1.0,
                                         base=0, pattern=[[-1, 128]], channel_multiplier=1))
            link(nc.gpsimd.tensor_copy(ident16[:, :], ident[:, :]))
            link(nc.gpsimd.memset(minus_half[:, :], -0.5))
            nc.gpsimd.memset(minus_one[:, :], -1.0)
            nc.gpsimd.memset(magic[:, :], MAGIC)
            nc.gpsimd.memset(zeros16[:, :], 0.0).then_inc(consts, 1)
            link(nc.gpsimd.memset(before[:, :, :], 1.0))
            nc.gpsimd.affine_select(out=before[:, :, :], in_=before[:, :, :], compare_op=ALU.is_gt, fill=0.0,
                                    base=0, pattern=[[-G, NG], [1, TOK]], channel_multiplier=-1).then_inc(consts, 1)
            link(nc.gpsimd.memset(before_e[:, :], 1.0))
            nc.gpsimd.affine_select(out=before_e[:, :], in_=before_e[:, :], compare_op=ALU.is_gt, fill=0.0,
                                    base=0, pattern=[[1, NE]], channel_multiplier=-1).then_inc(consts, 1)
            nc.gpsimd.memset(ones16[:, :], 1.0).then_inc(consts, 1)
            for t, pattern, mult in ((iota_e, [[0, 1]], 1), (iota_e16, [[0, 1]], 1), (iota_t, [[1, NT]], 0),
                                     (trow, [[1, TOK]], 0), (iota_p, [[0, 1]], 1)):
                nc.gpsimd.iota(t[:, :], pattern=pattern, base=0, channel_multiplier=mult,
                               allow_small_or_imprecise_dtypes=True).then_inc(consts, 1)

            link(nc.gpsimd.memset(first_pick[:, :, :], 1.0))
            nc.gpsimd.affine_select(out=first_pick[:, :, :], in_=first_pick[:, :, :], compare_op=ALU.is_equal, fill=0.0,
                                    base=0, pattern=[[-1, 4], [0, 128]], channel_multiplier=1).then_inc(consts, 1)
            roots = [0]

            def root(count=1):
                for _ in range(count):
                    n = roots[0]
                    roots[0] += 1
                    pool.wait_ge(root_ready, n + 1)
                    nc.gpsimd.tensor_tensor(root_out[:, n:n + 1], root_in[:, n:n + 1], minus_half[:, :], ALU.pow
                                            ).then_inc(root_done, 1)

            def affine(g):
                if g == 0:
                    pool.wait_ge(ld_vec, 16 * 6)
                pool.wait_ge(norm_ready, g + 1)
                link(nc.gpsimd.tensor_tensor(h[:, g, :], h[:, g, :], g2_bc[:, :], ALU.mult))
                nc.gpsimd.tensor_tensor(h[:, g, :], h[:, g, :], b2_bc[:, :], ALU.add).then_inc(affine_ready, 1)

            def down_gain(g):
                if g == 0:
                    pool.wait_ge(ld_late, 32)
                pool.wait_ge(swi_ready, g + 1)
                if g >= 2:
                    pool.wait_ge(q2_ready, g - 1)
                nc.gpsimd.tensor_tensor(swg[:, g % 2, :], swi[:, g % 2, :], gdn_bc[:, :], ALU.mult).then_inc(swg_ready, 1)

            root(NG)
            root()
            affine(0)
            for g in range(1, NG):
                root(2)
                affine(g)
            root()
            down_gain(0)
            root()
            down_gain(1)
            root()
            for g in range(2, NG):
                down_gain(g)
                root(2)
            root(2)

            def gather(lists, n, s):
                nc.gpsimd.indirect_dma_start(got[:, s, :], None, rows_dram[:, :],
                                             bass.IndirectOffsetOnAxis(ap=lists[:, n:n + 1], axis=0)
                                             ).then_inc(ld_got[s], 16)

            def split_low(st, d):
                s = st.slot(d)
                wait(pool, guh_ready, st.upto(d))
                for n in range(2):
                    cols = slice(n * WG // 2, (n + 1) * WG // 2)
                    last = nc.gpsimd.tensor_tensor(whl[:, s, 1, cols], raw[:, s, cols],
                                                   whl[:, s, 0, cols].bitcast(F32), ALU.subtract)
                last.then_inc(gul_ready, 1)

            split_low(Step(0, 0), 0)
            pool.wait_ge(rows_out, 16 * (NG + 1))
            for t in range(2):
                pool.wait_ge(idx_ready, t + 1)
                gather(first_idx, t, t)
            split_low(Step(0, 0), 1)
            pool.wait_ge(idx_ready, 3)
            pool.wait_ge(xt_done, 1)
            pool.wait_ge(gate_col, 1)
            gather(first_idx, 2, 0)
            pool.wait_ge(table_ready, 1)
            half = pool.value_load(more_i[0:1, 0:1], min_val=0, max_val=14) + NE // 2
            for st in steps(pool, half):
                if st.last:
                    continue
                split_low(st, 2)
                wait(pool, idx_ready, st.upto(3))
                wait(pool, xt_done, st.upto(1))
                wait(pool, gate_col, st.upto(1))
                pool.sem_inc(gather_go, 1)
                if st.first:
                    gather(first_idx, 3, 1)
                else:
                    gather(idx, st.slot(3), st.slot(3))

        @block.scalar
        def _(act):
            act.dma_start(g1_c[:, :], g1.rearrange("(p c) -> p c", c=KC)).then_inc(ld_vec, 16)
            act.dma_start(b1_c[:, :], b1.rearrange("(p c) -> p c", c=KC)).then_inc(ld_vec, 16)

            def split_tok_high(n):
                act.wait_ge(ld_wtok[n], 16)
                if n == 0:
                    act.wait_ge(ld_vec, 16 * 6)
                for c in range(4 * n, 4 * n + 4):
                    last = nc.scalar.activation(wtok_h[:, c, :], wtok_raw[:, c, :], ACT.Copy, scale=g1_c[:, c:c + 1])
                last.then_inc(wtok_h_ready, 1)

            def patch_high(g):
                act.wait_ge(t1_done, g + 1)
                if g >= 2:
                    act.wait_ge(tok_done, g - 1)
                nc.scalar.activation(patch_h[g % 2], patch_bank(g), ACT.Copy).then_inc(ph_ready, 1)

            scrapped = []

            def scrap(sem_, count):
                if scrapped:
                    act.wait_ge(*scrapped.pop())
                scrapped.append((sem_, count))

            def abs_in(n):
                act.wait_ge(ld_win[n // 2], 16)
                a, b = ABS_PART[n], ABS_PART[n + 1]
                scrap(abs_in_ready, n + 1)
                nc.scalar.activation(junk[:, 0:(b - a) * D], w_in_raw[:, a:b, :].rearrange("p b d -> p (b d)"), ACT.Abs,
                                     accum_out=abs_sum[:, 0, n:n + 1]).then_inc(abs_in_ready, 1)

            def copy_q1t(g):
                act.wait_ge(q1t_done, g + 1)
                nc.scalar.activation(q1_t[:, :, g * G:(g + 1) * G],
                                     bank(4)[:, 0:DC * G // 2].bitcast(BF16).rearrange("p (c t) -> p c t", c=DC),
                                     ACT.Copy).then_inc(q1t_ready, 1)

            def sign_w(n):
                act.wait_ge(wt_done, n + 1)
                src = bank(6 + n % 2).bitcast(BF16)
                if n < 11:
                    dst = w_t4[:, :, 2 * n * 128:(2 * n + 2) * 128].rearrange("p c (b q) -> p b c q", b=2)
                    src = src.rearrange("p (b c q) -> p b c q", b=2, c=DC)
                else:
                    c0 = 2 * (n - 11)
                    w = min(2, IC - c0)
                    dst = wd_t[:, c0:c0 + w, :].rearrange("p c d -> p (c d)")
                    src = src[:, 0:w * D]
                nc.scalar.activation(dst, src, ACT.Sign, bias=minus_one[:, 0:1]).then_inc(wt_ready, 1)

            split_tok_high(0)
            split_tok_high(1)
            patch_high(0)
            patch_high(1)
            abs_in(0)
            abs_in(1)
            patch_high(2)
            abs_in(2)
            abs_in(3)
            patch_high(3)
            for n in range(4, 8):
                abs_in(n)
            copy_q1t(0)
            copy_q1t(1)
            for m in range(DC):
                act.wait_ge(ld_wdown[m], 16)
                scrap(abs_down_ready, m + 1)
                nc.scalar.activation(junk[:, 0:I1], w_down_raw[m], ACT.Abs, accum_out=abs_sum[:, 1, m:m + 1]
                                     ).then_inc(abs_down_ready, 1)
            for n in range(6):
                sign_w(n)
            copy_q1t(2)
            for n in range(6, 11):
                sign_w(n)
            copy_q1t(3)

            act.wait_ge(scales_ready, 1)

            def sigmoid(g):
                act.wait_ge(gate_done, g + 1)
                if g >= 2:
                    act.wait_ge(swg_ready, g - 1)
                nc.scalar.activation(swi[:, g % 2, :], bank(0, 3)[0:G, 0:I1], ACT.Sigmoid, scale=deq[:, g:g + 1]
                                     ).then_inc(sig_ready, 1)

            def square2(g):
                act.wait_ge(swi_ready, g + 1)
                scrap(ssq2_ready, g + 1)
                nc.scalar.activation(junk[0:G, 0:I1], swi[:, g % 2, :], ACT.Square, accum_out=ssq[:, 4 + g:5 + g]
                                     ).then_inc(ssq2_ready, 1)

            def scale2(g):
                act.wait_ge(fscale_ready, g + 1)
                nc.scalar.activation(swg[:, g % 2, :], swg[:, g % 2, :], ACT.Identity, scale=fscale[:, g:g + 1],
                                     bias=magic[0:G, 0:1]).then_inc(scaled_ready, 1)

            def copy_q2t(g):
                act.wait_ge(q2t_done, g + 1)
                if g:
                    act.wait_ge(q2t_ready, g)
                for (a, b), src in ((Q2T_A, bank(6)), (Q2T_B, bank(7))):
                    last = nc.scalar.activation(q2_t[:, a:b, g * G:(g + 1) * G],
                                                src[:, 0:(b - a) * G // 2].bitcast(BF16).rearrange("p (c t) -> p c t", t=G),
                                                ACT.Copy)
                last.then_inc(q2t_ready, 1)

            def copy_xrt(g):
                act.wait_ge(xrt_done, g + 1)
                if g:
                    act.wait_ge(logit_done, g)
                nc.scalar.activation(xr_t[:, :, :], bank(7)[:, 0:DC * G].rearrange("p (c t) -> p c t", c=DC), ACT.Copy
                                     ).then_inc(xrt_ready, 1)

            sigmoid(0)
            square2(0)
            for n in range(11, 17):
                sign_w(n)
            act.wait_ge(rw_done, 1)
            nc.scalar.activation(rw_t[:, :, :], bank(6)[:, 0:DC * NE].rearrange("p (c e) -> p c e", c=DC), ACT.Copy
                                 ).then_inc(rw_ready, 1)
            sigmoid(1)
            for g in range(NG):
                if g + 1 < NG:
                    square2(g + 1)
                scale2(g)
                if g + 2 < NG:
                    sigmoid(g + 2)
                if g:
                    copy_xrt(g - 1)
                copy_q2t(g)
            copy_xrt(3)
            for g in range(NG):
                act.wait_ge(max_ready, g + 1)
                nc.scalar.activation(expo[:, g, :], logits[:, g, :], ACT.Exp, bias=neg_max[:, g:g + 1],
                                     accum_out=esum[:, g:g + 1]).then_inc(exp_ready, 1)

            def gu_high(st, d):
                s = st.slot(d)
                act.wait_ge(ld_gu[s], 2 * st.dma(d))
                nc.scalar.activation(whl[:, s, 0, 0:WG], raw[:, s, 0:WG], ACT.Copy).then_inc(guh_ready, 1)

            def down_high(st, d):
                s = st.slot(d)
                act.wait_ge(ld_dn[s], st.dma(d))
                nc.scalar.activation(whl[0:IH, s, 0, WG:WCOLS], raw[0:IH, s, WG:WCOLS], ACT.Copy).then_inc(dnh_ready, 1)

            def x_high(st, d):
                act.wait_ge(xt_done, st.upto(d))
                nc.scalar.activation(xh[:, :, :], bank(6).rearrange("p (c t) -> p c t", c=4), ACT.Copy
                                     ).then_inc(xh_ready, 1)

            gu_high(Step(0, 0), 0)
            gu_high(Step(0, 0), 1)
            down_high(Step(0, 0), 0)
            x_high(Step(0, 0), 0)
            act.wait_ge(table_ready, 1)
            half = act.value_load(more_i[0:1, 0:1], min_val=0, max_val=14) + NE // 2
            for st in steps(act, half):
                if not st.last:
                    act.wait_ge(gu_done, st.upto(0))
                    nc.scalar.activation(sg[:, :], bank(4)[:, 0:IE], ACT.Silu).then_inc(silu_ready, 1)
                    x_high(st, 1)
                    act.wait_ge(ht_done, st.upto(0))
                    nc.scalar.activation(hh[:, :, :], bank(5)[0:IH, 0:2 * P].rearrange("p (c t) -> p c t", c=2), ACT.Copy
                                         ).then_inc(hh_ready, 1)
                if not st.first and not (st.last and st.u == 1):
                    s = st.slot(-1)
                    act.wait_ge(y_done, st.upto(-1))
                    act.wait_ge(gate_col, st.upto(-1))
                    nc.scalar.activation(yh[:, s, :], bank(7), ACT.Copy, scale=gate[:, s:s + 1]).then_inc(yh_ready, 1)
                if not st.last:
                    gu_high(st, 2)
                    down_high(st, 1)

        @block.tensor
        def _(pe):
            def three(dst, ah, al, bh, bl, start, stop):
                nc.tensor.matmul(dst, ah, bh, start=start, stop=False)
                nc.tensor.matmul(dst, ah, bl, start=False, stop=False)
                return nc.tensor.matmul(dst, al, bh, start=False, stop=stop)

            def transpose_patch(g):
                pe.wait_ge(xhat_ready, g + 1)
                if g >= 2:
                    pe.wait_ge(pl_ready, g - 1)
                dst = patch_bank(g)
                for c in range(KC):
                    last = nc.tensor.transpose(dst[:, c // 4, (c % 4) * G:(c % 4 + 1) * G], xt[:, g, c::KC],
                                               ident[0:G, 0:G])
                last.then_inc(t1_done, 1)

            def beta_product():
                pe.wait_ge(ld_wtok[0], 16)
                pe.wait_ge(ld_wtok[1], 16)
                pe.wait_ge(ld_vec, 16 * 6)
                for c in range(KC):
                    last = nc.tensor.matmul(bank(4)[0:G, :], b1_c[:, c:c + 1].broadcast_to([128, G]), wtok_raw[:, c, :],
                                            start=c == 0, stop=c == KC - 1)
                last.then_inc(bias_done, 1)

            def tok_product(g):
                acc = bank(2 + g % 2)[0:G, :]
                pe.wait_ge(pl_ready, g + 1)
                if g == 0:
                    pe.wait_ge(wtok_l_ready, 2)
                if g >= 2:
                    pe.wait_ge(tok_read, g - 1)
                for c in range(KC):
                    cols = slice((c % 4) * G, (c % 4 + 1) * G)
                    last = three(acc, patch_h[g % 2][:, c // 4, cols], patch_l[g % 2][:, c // 4, cols],
                                 wtok_h[:, c, :], wtok_l[:, c, :], c == 0, c == KC - 1)
                last.then_inc(tok_done, 1)

            def transpose_q1(g):
                pe.wait_ge(q1_ready, g + 1)
                if g:
                    pe.wait_ge(q1t_ready, g)
                for c in range(DC):
                    last = nc.tensor.transpose(bank(4)[:, c * G // 2:(c + 1) * G // 2].bitcast(BF16),
                                               q1[:, g % 2, c * 128:(c + 1) * 128], ident16[0:G, 0:G])
                last.then_inc(q1t_done, 1)

            def total(which):
                n = 8 if which == 0 else DC
                nc.tensor.matmul(bank(5)[:, 8 * which:8 * which + n], ones[:, :], abs_sum[:, which, 0:n],
                                 start=True, stop=True).then_inc(tot_done, 1)

            def transpose_w(n):
                pe.wait_ge(level_ready, n + 1 if n < 11 else 11 + DC)
                if n >= 2:
                    pe.wait_ge(wt_ready, n - 1)
                dst = bank(6 + n % 2).bitcast(BF16)
                if n < 11:
                    pairs = [(levels_of(w_in_raw[:, 2 * n + b, c * 128:(c + 1) * 128]), b * DC + c)
                             for b in range(2) for c in range(DC)]
                else:
                    c0 = 2 * (n - 11)
                    pairs = [(levels_of(w_down_raw[m][:, (c0 + c) * 128:(c0 + c + 1) * 128]), c * DC + m)
                             for c in range(min(2, IC - c0)) for m in range(DC)]
                for src, b in pairs:
                    last = nc.tensor.transpose(dst[:, b * 128:(b + 1) * 128], src, ident16[:, :])
                last.then_inc(wt_done, 1)

            def gate_product(g):
                if g == 0:
                    pe.wait_ge(wt_ready, 11)
                    pe.wait_ge(q1t_ready, NG)
                    pe.wait_ge(tot_in, 2)
                else:
                    pe.wait_ge(gate_read, g)
                products(g, 0).then_inc(gate_done, 1)

            def value_product(g):
                if g:
                    pe.wait_ge(swi_ready, g)
                products(g, 1).then_inc(value_done, 1)

            def products(g, half_):
                for a in range(0, I1, 512):
                    w = min(512, I1 - a)
                    for c in range(DC):
                        last = nc.tensor.matmul(bank(3 * half_, 3)[0:G, a:a + w], q1_t[:, c, g * G:(g + 1) * G],
                                                w_t4[:, c, half_ * I1 + a:half_ * I1 + a + w],
                                                start=c == 0, stop=c == DC - 1)
                return last

            def transpose_q2(g):
                pe.wait_ge(q2_ready, g + 1)
                if g:
                    pe.wait_ge(q2t_ready, g)
                if g >= 2:
                    pe.wait_ge(logit_read, g - 1)
                for (a, b), dst in ((Q2T_A, bank(6)), (Q2T_B, bank(7))):
                    if g and a:
                        pe.wait_ge(xrt_ready, g)
                    for c in range(a, b):
                        last = nc.tensor.transpose(dst[:, (c - a) * G // 2:(c - a + 1) * G // 2].bitcast(BF16),
                                                   q2[:, c * 128:(c + 1) * 128], ident16[0:G, 0:G])
                last.then_inc(q2t_done, 1)

            def mlp_out(g):
                pe.wait_ge(q2t_ready, g + 1)
                for c in range(IC):
                    last = nc.tensor.matmul(bank(7)[0:G, :], q2_t[:, c, g * G:(g + 1) * G], wd_t[:, c, :],
                                            start=c == 0, stop=c == IC - 1)
                last.then_inc(z_done, 1)

            def transpose_row(g):
                pe.wait_ge(row_ready, g + 1)
                for c in range(DC):
                    last = nc.tensor.transpose(bank(7)[:, c * G:(c + 1) * G], rows[:, g, c * 128:(c + 1) * 128],
                                               ident[0:G, 0:G])
                last.then_inc(xrt_done, 1)

            def logits_product(g):
                pe.wait_ge(xrt_ready, g + 1)
                if g:
                    pe.wait_ge(logit_read, g)
                if g + 1 < NG:
                    pe.wait_ge(q2t_ready, g + 2)
                for c in range(DC):
                    last = nc.tensor.matmul(bank(6)[0:G, 0:NE], xr_t[:, c, :], rw_t[:, c, :], start=c == 0, stop=c == DC - 1)
                last.then_inc(logit_done, 1)

            pe.wait_ge(consts, 1)
            transpose_patch(0)
            transpose_patch(1)
            beta_product()
            tok_product(0)
            transpose_patch(2)
            tok_product(1)
            transpose_patch(3)
            tok_product(2)
            tok_product(3)
            pe.wait_ge(bias_read, 1)
            transpose_q1(0)
            transpose_q1(1)
            pe.wait_ge(abs_in_ready, 8)
            total(0)
            for n in range(6):
                transpose_w(n)
            transpose_q1(2)
            for n in range(6, 11):
                transpose_w(n)
            pe.wait_ge(tot_in, 1)
            pe.wait_ge(abs_down_ready, DC)
            total(1)
            transpose_q1(3)
            gate_product(0)
            value_product(0)
            for n in range(11, 17):
                transpose_w(n)
            pe.wait_ge(ld_late, 32)
            pe.wait_ge(wt_ready, 17)
            for c in range(DC):
                last = nc.tensor.transpose(bank(6)[:, c * NE:(c + 1) * NE], rw_raw[:, c * 128:(c + 1) * 128],
                                           ident[0:NE, 0:NE])
            last.then_inc(rw_done, 1)
            gate_product(1)
            value_product(1)
            pe.wait_ge(rw_ready, 1)
            for g in range(NG):
                if g + 2 < NG:
                    gate_product(g + 2)
                    value_product(g + 2)
                if g:
                    transpose_row(g - 1)
                transpose_q2(g)
                if g:
                    logits_product(g - 1)
                mlp_out(g)
            transpose_row(3)
            logits_product(3)

            pe.wait_ge(consts, 10)
            pe.wait_ge(mask_ready, NG)
            for g in range(NG):
                nc.tensor.matmul(bank(6)[0:NE, 0:TOK], mask[:, g, :], before[:, g, :], start=g == 0, stop=g == NG - 1)
            for g in range(NG):
                last = nc.tensor.transpose(bank(7)[0:NE, g * G // 2:(g + 1) * G // 2].bitcast(BF16), mask[:, g, :],
                                           ident16[0:G, 0:G])
            last.then_inc(rank_done, 1)
            pe.wait_ge(place16_ready, 1)
            for t in range(4):
                nc.tensor.matmul(bank(t)[:, 0:TOK], first_pick[:, t, :], place[:, :], start=True, stop=True
                                 ).then_inc(first_place_done, 1)
            nc.tensor.matmul(bank(4)[0:NE, 0:1], before_e[:, :], n_over[:, :], start=True, stop=True)
            nc.tensor.matmul(bank(4)[0:1, 1:2], n_over[:, :], ones[0:NE, 0:1], start=True, stop=True
                             ).then_inc(start_done, 1)
            pe.wait_ge(owner_ready, 1)
            nc.tensor.matmul(bank(5)[0:NT, 0:TOK], owner[:, :], place[:, :], start=True, stop=True)
            nc.tensor.matmul(bank(4)[0:NT, 2:3], shift[:, :], ones16[:, :], start=True, stop=True)
            nc.tensor.matmul(bank(4)[0:1, 8:8 + NT], iota_e16[:, :], owner[:, :], start=True, stop=True
                             ).then_inc(tables_done, 1)

            pe.wait_ge(table_ready, 1)
            for g in range(NG):
                nc.tensor.matmul(bank(g)[0:G, :], zeros16[:, 0:G], zeros16[:, :], start=True, stop=False,
                                 skip_group_check=True)

            def transpose_x(st, d):
                s = st.slot(d)
                pe.wait_ge(ld_got[s], st.dma(d))
                for c in range(4):
                    last = nc.tensor.transpose(bank(6)[:, c * P:(c + 1) * P], got[:, s, c:D:4], ident[:, :])
                last.then_inc(xt_done, 1)

            def gate_up(st):
                s = st.u
                pe.wait_ge(xl_ready, st.upto(0))
                pe.wait_ge(gul_ready, st.upto(0))
                wait(pe, hid_ready, st.upto(-1))
                wh = whl[:, s, 0, 0:WG].rearrange("p (n c i) -> p n c i", n=2, c=4)
                wl = whl[:, s, 1, 0:WG].rearrange("p (n c i) -> p n c i", n=2, c=4)
                dst = bank(4)[:, 0:2 * IE].rearrange("p (n i) -> p n i", n=2)
                for c in range(4):
                    last = three(dst, xh[:, c, :], xl[:, c, :], wh[:, :, c, :], wl[:, :, c, :], c == 0, c == 3)
                last.then_inc(gu_done, 1)

            def down(st):
                s = st.slot(-1)
                pe.wait_ge(hl_ready, st.upto(-1))
                pe.wait_ge(dnl_ready, st.upto(-1))
                wait(pe, yl_ready, st.upto(-2))
                wh = whl[0:IH, s, 0, WG:WCOLS].rearrange("p (c d) -> p c d", c=2)
                wl = whl[0:IH, s, 1, WG:WCOLS].rearrange("p (c d) -> p c d", c=2)
                for c in range(2):
                    last = three(bank(7), hh[:, c, :], hl[:, c, :], wh[:, c, :], wl[:, c, :], c == 0, c == 1)
                last.then_inc(y_done, 1)

            def add_rows(st, stop=False):
                s = st.slot(-2)
                pe.wait_ge(sel_ready, st.upto(-2))
                pe.wait_ge(yl_ready, st.upto(-2))
                for g in range(NG):
                    for n, part in enumerate((yh, yl)):
                        last = nc.tensor.matmul(bank(g)[0:G, :], sel[:, s, g * G:(g + 1) * G], part[:, s, :],
                                                start=False, stop=stop and n == 1, skip_group_check=True)
                last.then_inc(sum_done, 1)

            transpose_x(Step(0, 0), 0)
            half = pe.value_load(more_i[0:1, 0:1], min_val=0, max_val=14) + NE // 2
            for st in steps(pe, half):
                if not st.last:
                    gate_up(st)
                    transpose_x(st, 1)
                if not st.first and not (st.last and st.u == 1):
                    down(st)
                if not st.last:
                    pe.wait_ge(hid_ready, st.upto(0))
                    for c in range(2):
                        last = nc.tensor.transpose(bank(5)[0:IH, c * P:(c + 1) * P], hid[:, c::2], ident[:, :])
                    last.then_inc(ht_done, 1)
                if not isinstance(st.k, int):
                    add_rows(st, stop=st.last and st.u == 1)

        @block.vector
        def _(dve):
            chain = [0]

            def link(ins):
                chain[0] += 1
                ins.then_inc(dve_chain, 1)
                dve.wait_ge(dve_chain, chain[0])

            def moments(src, n):
                for c in range(n // 512):
                    ins = nc.vector.bn_stats(stats[:, c, :], src[:, c * 512:(c + 1) * 512])
                link(ins)
                link(nc.vector.bn_aggr(mv[:, :], stats[:, 0:n // 512, :].rearrange("p c s -> p (c s)")))

            powers = [0]

            def power(src, scale, eps):
                return get_power(ask_power(src, scale, eps))

            def ask_power(src, scale, eps):
                n = powers[0]
                powers[0] += 1
                nc.vector.tensor_scalar(root_in[:, n:n + 1], src, scale, eps, ALU.mult, ALU.add).then_inc(root_ready, 1)
                return n

            def get_power(n):
                dve.wait_ge(root_done, n + 1)
                return root_out[:, n:n + 1]

            def norm_patch(g):
                dve.wait_ge(ld_x[g], 16 * len(pieces(g)))
                moments(xt[:, g, :], KIN)
                rstd = power(mv[:, 1:2], 1.0, EPS6)
                nc.vector.tensor_scalar(xt[:, g, :], xt[:, g, :], mv[:, 0:1], rstd[:, 0:1], ALU.subtract, ALU.mult
                                        ).then_inc(xhat_ready, 1)

            def patch_low(g):
                dve.wait_ge(ph_ready, g + 1)
                nc.vector.tensor_tensor(patch_l[g % 2], patch_bank(g), patch_h[g % 2].bitcast(F32), ALU.subtract
                                        ).then_inc(pl_ready, 1)

            def quant_scale(which, g, norm):
                n = 4 * which + g
                link(nc.vector.tensor_scalar(amax[:, n:n + 1], amax[:, n:n + 1], norm[:, 0:1], EPS5, ALU.mult, ALU.max))
                link(nc.vector.reciprocal(qscale[:, :], amax[:, n:n + 1]))
                return nc.vector.tensor_scalar(fscale[:, g:g + 1], qscale[:, :], 127.0, norm[:, 0:1], ALU.mult, ALU.mult)

            def tok_low(n):
                dve.wait_ge(wtok_h_ready, n + 1)
                for c in range(4 * n, 4 * n + 4):
                    last = nc.vector.scalar_tensor_tensor(wtok_l[:, c, :], wtok_raw[:, c, :], g1_c[:, c:c + 1],
                                                          wtok_h[:, c, :].bitcast(F32), ALU.mult, ALU.subtract)
                last.then_inc(wtok_l_ready, 1)

            def full_bias():
                dve.wait_ge(bias_done, 1)
                nc.vector.tensor_tensor(bias_bc[:, :], bank(4)[0:G, :], bias_bc[:, :], ALU.add).then_inc(bias_read, 1)
                dve.wait_ge(bias_read, 1)

            def token_norm(g):
                dve.wait_ge(tok_done, g + 1)
                nc.vector.tensor_tensor(h[:, g, :], bank(2 + g % 2)[0:G, :], bias_bc[:, :], ALU.add).then_inc(tok_read, 1)
                dve.wait_ge(tok_read, g + 1)
                moments(h[:, g, :], D)
                rstd = power(mv[:, 1:2], 1.0, EPS6)
                nc.vector.tensor_scalar(h[:, g, :], h[:, g, :], mv[:, 0:1], rstd[:, 0:1], ALU.subtract, ALU.mult
                                        ).then_inc(norm_ready, 1)

            def quantise1(g):
                dve.wait_ge(affine_ready, g + 1)
                moments(h[:, g, :], D)
                n = ask_power(mv[:, 1:2], 1.0 + EPS6, EPS5 * EPS6)
                link(nc.vector.scalar_tensor_tensor(h_work[:, :], h[:, g, :], mv[:, 0:1], gin_bc[:, :],
                                                    ALU.subtract, ALU.mult))
                link(nc.vector.tensor_reduce(amax[:, g:g + 1], h_work[:, :], AX.X, ALU.max, apply_absolute_value=True))
                link(quant_scale(0, g, get_power(n)))
                link(nc.vector.tensor_scalar(h_work[:, :], h_work[:, :], fscale[:, g:g + 1], MAGIC, ALU.mult, ALU.add))
                if g >= 2:
                    dve.wait_ge(q1t_done, g - 1)
                nc.vector.tensor_scalar(q1[:, g % 2, :], h_work[:, :], -MAGIC, 127.0, ALU.add, ALU.min
                                        ).then_inc(q1_ready, 1)

            def weight_scale(which, n, size):
                dve.wait_ge(tot_done, which + 1)
                dve_ins = nc.vector.tensor_reduce(abs_tot[:, which:which + 1], bank(5)[:, 8 * which:8 * which + n], AX.X, ALU.add)
                dve_ins.then_inc(tot_in, 1)
                dve.wait_ge(tot_in, which + 1)
                link(nc.vector.tensor_scalar(wmean[:, which:which + 1], abs_tot[:, which:which + 1], 1.0 / size, EPS5,
                                             ALU.mult, ALU.max))
                link(nc.vector.reciprocal(wscale[:, which:which + 1], wmean[:, which:which + 1]))

            def levels(n):
                which = 0 if n < 11 else 1
                w = w_in_raw[:, 2 * n:2 * n + 2, :] if n < 11 else w_down_raw[n - 11]
                nc.vector.tensor_scalar(w, w, wscale[:, which:which + 1], LEVEL_MAGIC, ALU.mult, ALU.add
                                        ).then_inc(level_ready, 1)

            dve.wait_ge(consts, 1)
            norm_patch(0)
            norm_patch(1)
            tok_low(0)
            patch_low(0)
            tok_low(1)
            norm_patch(2)
            patch_low(1)
            norm_patch(3)
            dve.wait_ge(ld_vec, 16 * 6)
            full_bias()
            patch_low(2)
            token_norm(0)
            patch_low(3)
            for g in range(1, NG):
                token_norm(g)
                quantise1(g - 1)
            weight_scale(0, 8, 2 * I1 * D)
            for n in range(11):
                levels(n)
            weight_scale(1, DC, I1 * D)
            quantise1(3)
            link(nc.vector.tensor_scalar(deq[:, 0:NG], amax[:, 0:NG], 1.0 / 127.0, wmean[0:G, 0:1], ALU.mult, ALU.mult))
            nc.vector.tensor_tensor(deq_sq[:, :], deq[:, 0:NG], deq[:, 0:NG], ALU.mult).then_inc(scales_ready, 1)
            for n in range(11, 11 + DC):
                levels(n)
            dve.wait_ge(scales_ready, 1)

            def swiglu(g):
                v = swi[:, g % 2, :]
                dve.wait_ge(sig_ready, g + 1)
                nc.vector.tensor_tensor(v, bank(0, 3)[0:G, 0:I1], v, ALU.mult).then_inc(gate_read, 1)
                dve.wait_ge(value_done, g + 1)
                dve.wait_ge(gate_read, g + 1)
                nc.vector.scalar_tensor_tensor(v, bank(3, 3)[0:G, 0:I1], deq_sq[:, g:g + 1], v, ALU.mult, ALU.mult
                                               ).then_inc(swi_ready, 1)

            def factor2(g):
                n = 4 + g
                dve.wait_ge(ssq2_ready, g + 1)
                p = ask_power(ssq[:, n:n + 1], 1.0 / I1, EPS6)
                dve.wait_ge(swg_ready, g + 1)
                link(nc.vector.tensor_reduce(amax[:, n:n + 1], swg[:, g % 2, :], AX.X, ALU.max, apply_absolute_value=True))
                quant_scale(1, g, get_power(p)).then_inc(fscale_ready, 1)

            def quantise2(g):
                dve.wait_ge(scaled_ready, g + 1)
                if g:
                    dve.wait_ge(q2t_done, g)
                nc.vector.tensor_scalar(q2[:, :], swg[:, g % 2, :], -MAGIC, 127.0, ALU.add, ALU.min).then_inc(q2_ready, 1)

            def residual(g):
                dve.wait_ge(z_done, g + 1)
                link(nc.vector.tensor_scalar(deq2[:, :], amax[:, 4 + g:5 + g], 1.0 / 127.0, wmean[0:G, 1:2],
                                             ALU.mult, ALU.mult))
                nc.vector.scalar_tensor_tensor(h[:, g, :], bank(7)[0:G, :], deq2[:, 0:1], h[:, g, :], ALU.mult, ALU.add
                                               ).then_inc(z_read, 1)
                dve.wait_ge(z_read, g + 1)
                moments(h[:, g, :], D)
                rstd = power(mv[:, 1:2], 1.0, EPS5)
                nc.vector.tensor_scalar(rows[:, g, 0:D], h[:, g, :], mv[:, 0:1], rstd[:, 0:1], ALU.subtract, ALU.mult
                                        ).then_inc(row_ready, 1)

            def top(g):
                dve.wait_ge(logit_done, g + 1)
                row = logits[:, g, :]
                nc.vector.tensor_copy(row, bank(6)[0:G, 0:NE]).then_inc(logit_read, 1)
                dve.wait_ge(logit_read, g + 1)
                link(nc.vector.max(top8[:, :], row))
                nc.vector.tensor_scalar(neg_max[:, g:g + 1], top8[:, 0:1], -1.0, None, ALU.mult).then_inc(max_ready, 1)
                link(nc.vector.match_replace(zapped[:, :], top8[:, :], row, -3.0e38))
                nc.vector.tensor_tensor(mask[:, g, :], zapped[:, :], row, ALU.not_equal).then_inc(mask_ready, 1)

            swiglu(0)
            for g in range(NG):
                if g + 1 < NG:
                    swiglu(g + 1)
                if g >= 2:
                    top(g - 2)
                factor2(g)
                if g:
                    residual(g - 1)
                quantise2(g)
            top(2)
            residual(3)
            top(3)

            def picked_weights():
                dve.wait_ge(exp_ready, NG)
                dve.wait_ge(mask_ready, NG)
                link(nc.vector.reciprocal(esum[:, :], esum[:, :]))
                for g in range(NG):
                    last = nc.vector.scalar_tensor_tensor(picked[:, g, :], expo[:, g, :], esum[:, g:g + 1], mask[:, g, :],
                                                          ALU.mult, ALU.mult, accum_out=psum8[:, g:g + 1])
                link(last)
                link(nc.vector.reciprocal(psum8[:, :], psum8[:, :]))
                for g in range(NG):
                    last = nc.vector.tensor_scalar(rows[:, g, D:ROW], picked[:, g, :], psum8[:, g:g + 1], None, ALU.mult)
                last.then_inc(gate_ready, 1)

            picked_weights()

            dve.wait_ge(rank_done, 1)
            rank = bank(6)[0:NE, 0:TOK]
            link(nc.vector.tensor_copy(mask_t[:, :], bank(7)[0:NE, 0:TOK // 2].bitcast(BF16)))
            link(nc.vector.tensor_tensor(count[:, :], mask_t[:, TOK - 1:TOK], rank[:, TOK - 1:TOK], ALU.add))
            link(nc.vector.tensor_scalar(mask_t[:, :], mask_t[:, :], FAR, -FAR, ALU.mult, ALU.add))
            link(nc.vector.tensor_tensor(place[:, :], mask_t[:, :], rank, ALU.add))
            link(nc.vector.tensor_scalar(n_over[:, :], count[:, :], float(P), None, ALU.is_gt))
            link(nc.vector.scalar_tensor_tensor(n_over[:, :], count[:, :], 2.0 * P, n_over[:, :], ALU.is_gt, ALU.add))
            nc.vector.scalar_tensor_tensor(n_over[:, :], count[:, :], 3.0 * P, n_over[:, :], ALU.is_gt, ALU.add
                                           ).then_inc(place16_ready, 1)

            for t in range(4):
                dve.wait_ge(first_place_done, t + 1)
                nc.vector.scalar_tensor_tensor(hit[:, :], bank(t)[:, 0:TOK], iota_p[:, 0:1], trow[:, :], ALU.is_equal, ALU.mult,
                                               accum_out=first_f[:, t:t + 1]).then_inc(hit_ready, 1)
                dve.wait_ge(hit_ready, t + 1)
                nc.vector.tensor_copy(first_idx[:, t:t + 1], first_f[:, t:t + 1]).then_inc(idx_ready, 1)

            dve.wait_ge(start_done, 1)
            link(nc.vector.tensor_scalar(start[:, :], bank(4)[0:NE, 0:1], float(NE), None, ALU.add))
            link(nc.vector.tensor_scalar(halff[:, :], bank(4)[0:1, 1:2], 0.5, 0.25, ALU.mult, ALU.add))
            link(nc.vector.tensor_scalar(halff[:, :], halff[:, :], MAGIC, -MAGIC, ALU.add, ALU.add))
            link(nc.vector.tensor_copy(more_i[:, :], halff[:, :]))
            link(nc.vector.tensor_scalar(t_a[:, :], iota_t[:, :], start[:, 0:1], None, ALU.subtract))
            link(nc.vector.tensor_scalar(t_b[:, :], t_a[:, :], 0.0, None, ALU.is_ge))
            link(nc.vector.scalar_tensor_tensor(t_b[:, :], t_a[:, :], n_over[:, 0:1], t_b[:, :], ALU.is_lt, ALU.mult))
            link(nc.vector.tensor_scalar(t_c[:, :], iota_t[:, :], iota_e[:, 0:1], None, ALU.is_equal))
            link(nc.vector.tensor_tensor(t_c[:, :], t_c[:, :], t_b[:, :], ALU.add))
            link(nc.vector.tensor_copy(owner[:, :], t_c[:, :]))
            link(nc.vector.scalar_tensor_tensor(t_b[:, :], t_a[:, :], 1.0, t_b[:, :], ALU.add, ALU.mult))
            link(nc.vector.tensor_scalar(t_b[:, :], t_b[:, :], -float(P), None, ALU.mult))
            nc.vector.scalar_tensor_tensor(shift[:, :], t_c[:, :], FAR, t_b[:, :], ALU.mult, ALU.add
                                           ).then_inc(owner_ready, 1)
            dve.wait_ge(tables_done, 1)
            link(nc.vector.tensor_scalar(shift_c[:, :], bank(4)[0:NT, 2:3], -FAR, None, ALU.add))
            nc.vector.tensor_scalar(place_tile[:, :], bank(5)[0:NT, 0:TOK], shift_c[:, 0:1], None, ALU.add
                                    ).then_inc(place_ready, 1)
            nc.vector.tensor_copy(owner_row[:, :], bank(4)[0:1, 8:8 + NT]).then_inc(table_ready, 1)

            def find(st, d):
                s = st.slot(d)
                dve.wait_ge(ld_pa[s], st.dma(d - 4))
                nc.vector.scalar_tensor_tensor(hit[:, :], place_a[:, s, :], iota_p[:, 0:1], trow[:, :], ALU.is_equal, ALU.mult,
                                               accum_out=idx_f[:, s:s + 1]).then_inc(hit_ready, 1)
                dve.wait_ge(hit_ready, st.upto(d))
                nc.vector.tensor_copy(idx[:, s:s + 1], idx_f[:, s:s + 1]).then_inc(idx_ready, 1)

            def gates(st, d):
                s = st.slot(d)
                e = dve.value_load(owner_row[0:1, bass.ds(st.tile(d), 1)], min_val=0, max_val=NE - 1)
                dve.wait_ge(ld_got[s], st.dma(d))
                wait(dve, yl_ready, st.upto(d - 2))
                nc.vector.tensor_copy(gate[:, s:s + 1], got[:, s, bass.ds(e + D, 1)]).then_inc(gate_col, 1)

            def x_low(st, d):
                dve.wait_ge(xh_ready, st.upto(d))
                nc.vector.tensor_tensor(xl[:, :, :], bank(6).rearrange("p (c t) -> p c t", c=4), xh[:, :, :].bitcast(F32),
                                        ALU.subtract).then_inc(xl_ready, 1)

            def down_low(st, d):
                s = st.slot(d)
                dve.wait_ge(dnh_ready, st.upto(d))
                nc.vector.tensor_tensor(whl[0:IH, s, 1, WG:WCOLS], raw[0:IH, s, WG:WCOLS],
                                        whl[0:IH, s, 0, WG:WCOLS].bitcast(F32), ALU.subtract).then_inc(dnl_ready, 1)

            zero = Step(0, 0)
            dve.wait_ge(table_ready, 1)
            gates(zero, 0)
            x_low(zero, 0)
            down_low(zero, 0)
            half = dve.value_load(more_i[0:1, 0:1], min_val=0, max_val=14) + NE // 2
            for st in steps(dve, half):
                if not st.last:
                    dve.wait_ge(silu_ready, st.upto(0))
                    nc.vector.tensor_tensor(hid[:, :], bank(4)[:, IE:2 * IE], sg[:, :], ALU.mult).then_inc(hid_ready, 1)
                    x_low(st, 1)
                    dve.wait_ge(hh_ready, st.upto(0))
                    nc.vector.tensor_tensor(hl[:, :, :], bank(5)[0:IH, 0:2 * P].rearrange("p (c t) -> p c t", c=2),
                                            hh[:, :, :].bitcast(F32), ALU.subtract).then_inc(hl_ready, 1)
                if not st.first and not (st.last and st.u == 1):
                    s = st.slot(-1)
                    dve.wait_ge(yh_ready, st.upto(-1))
                    nc.vector.scalar_tensor_tensor(yl[:, s, :], bank(7), gate[:, s:s + 1], yh[:, s, :].bitcast(F32),
                                                   ALU.mult, ALU.subtract).then_inc(yl_ready, 1)
                    dve.wait_ge(ld_ps[s], st.dma(-1))
                    nc.vector.tensor_scalar(sel[:, s, :], place_s[:, s, :], iota_p[:, 0:1], None, ALU.is_equal
                                            ).then_inc(sel_ready, 1)
                if not st.last:
                    gates(st, 1)
                    down_low(st, 1)
                    if not st.first:
                        find(st, 3)
            dve.wait_ge(sum_done, 2 * half)
            for g in range(NG):
                nc.vector.tensor_tensor(fin[:, g, :], bank(g)[0:G, :], h[:, g, :], ALU.add).then_inc(fin_ready, 1)


_ARGS = ["x", "L0_tok_W", "L0_tok_b", "L0_tok_g1", "L0_tok_b1", "L0_tok_g2", "L0_tok_b2", "L0_attn_w_gate",
         "L0_attn_g_gate", "L0_attn_w_down", "L0_attn_g_down", "L0_ffn_router_w", "L0_ffn_w_gate", "L0_ffn_w_up",
         "L0_ffn_w_down"]


def kernel(**inputs):
    import concourse.bacc as bacc
    import numpy as np
    from concourse.bass_utils import run_bass_kernel_spmd

    nc = bacc.Bacc("TRN2", target_bir_lowering=False, num_devices=1)
    arrays, args = {}, []
    for name in _ARGS:
        a = np.ascontiguousarray(inputs[name])
        arrays[f"in_{name}"] = a
        args.append(nc.dram_tensor(f"in_{name}", a.shape, mybir.dt.from_np(a.dtype), kind="ExternalInput").ap())
    out = nc.dram_tensor("out_0", (NB, NPATCH, D), F32, kind="ExternalOutput").ap()
    program(nc, *args, out)
    r = run_bass_kernel_spmd(nc, [arrays], core_ids=[0])
    return r.results[0]["out_0"]
```

```python
import concourse.bass as bass
from concourse import mybir
from contextlib import ExitStack

F32 = mybir.dt.float32
F32R = mybir.dt.float32r
BF16 = mybir.dt.bfloat16
F16 = mybir.dt.float16
I32 = mybir.dt.int32
ALU = mybir.AluOpType
ACT = mybir.ActivationFunctionType
AX = mybir.AxisListType

NB, NPATCH, TIN, FEAT = 64, 7, 16, 64
TOK = NB * NPATCH
NG, G = 4, TOK // 4
KIN = TIN * FEAT
KC = KIN // 128
D = 512
DC = D // 128
I1 = 1408
IC = I1 // 128
NE, TOPK, IE = 32, 8, 192
P = 128
NT = 64
ROW = D + NE
IH = IE // 2
WG = 2 * 4 * IE
WCOLS = WG + 2 * D
MAGIC = 1.5 * 2.0 ** 23
LEVEL_MAGIC = MAGIC + 0x3F80
FAR = 1000.0
EPS6, EPS5 = 1e-6, 1e-5
N_ROOTS = 6 * NG


def wait(eng, sem, value):
    if isinstance(value, int) and value <= 0:
        return
    eng.wait_ge(sem, value)


def pieces(g):
    runs = []
    t = g * G
    while t < (g + 1) * G:
        size = min(NB - t % NB, (g + 1) * G - t)
        runs.append((t - g * G, t // NB, t % NB, size))
        t += size
    return runs


class Step:

    def __init__(self, k, u, first=False, last=False):
        self.k, self.u, self.first, self.last = k, u, first, last

    def upto(self, d):
        return 2 * self.k + (self.u + d + 1)

    def tile(self, d):
        return 2 * self.k + (self.u + d)

    def slot(self, d):
        return (self.u + d) % 2

    def dma(self, d):
        return 16 * self.k + 16 * ((self.u + d) // 2 + 1)


def steps(eng, half):
    yield Step(0, 0, first=True)
    yield Step(0, 1, first=False)
    with eng.Fori(1, half) as k:
        yield Step(k, 0)
        yield Step(k, 1)
    yield Step(half, 0, last=True)
    yield Step(half, 1, last=True)


def program(nc, x, w_tok, b_tok, g1, b1, g2, b2, w_in, g_in, w_down, g_down, w_router, we_gate, we_up, we_down, out):
    rows_dram = nc.dram_tensor("token_rows", (TOK, ROW), F32).ap()
    place_dram = nc.dram_tensor("places", (NT, TOK), F16).ap()
    ctx = ExitStack()
    with ctx:
        def sb(name, shape, dt):
            return ctx.enter_context(nc.sbuf_tensor(name, shape, dt))

        def sem(name):
            return ctx.enter_context(nc.semaphore(name))

        big = sb("big", [128, 22 * D], F32)
        w_in_raw = big[:, :].rearrange("p (b d) -> p b d", b=22)
        at = [0]

        def late(cols, dt=F32):
            at[0] += cols
            return big[:, at[0] - cols:at[0]].bitcast(dt) if dt != F32 else big[:, at[0] - cols:at[0]]

        rows = late(NG * ROW)[0:G, :].rearrange("p (g r) -> p g r", g=NG)
        total_t = big[:, 0:DC * TOK].rearrange("p (c t) -> p c t", c=DC)
        q2 = late(I1 // 2, BF16)[0:G, :]
        got = late(2 * ROW).rearrange("p (s r) -> p s r", s=2)
        place_a = late(TOK, F16).rearrange("p (s t) -> p s t", s=2)
        place_s = late(TOK, F16).rearrange("p (s t) -> p s t", s=2)
        hit = late(TOK // 2, F16)
        assert at[0] <= 11 * D
        at[0] = 11 * D
        swi = late(2 * I1)[0:G, :].rearrange("p (s i) -> p s i", s=2)
        swg = late(2 * I1)[0:G, :].rearrange("p (s i) -> p s i", s=2)
        assert at[0] <= 22 * D
        at[0] = 11 * D
        fin = late(NG * D)[0:G, :].rearrange("p (g d) -> p g d", g=NG)
        sg = late(IE)
        hid = late(IE)
        xr_t = late(2 * DC * G).rearrange("p (s c t) -> p s c t", s=2, c=DC)
        mask_t = late(TOK)[0:NE, :]
        place = late(TOK // 2, F16)[0:NE, :]
        place_tile = late(TOK // 2, F16)[0:NT, :]
        w_t = sb("w_t", [128, DC * 2 * I1], BF16)
        w_t4 = w_t[:, :].rearrange("p (c o) -> p c o", c=DC)
        xt = w_t[0:G, 0:2 * NG * KIN].bitcast(F32).rearrange("p (g k) -> p g k", g=NG)
        wd_t = sb("wd_t", [128, IC, D], BF16)
        whl = sb("whl", [128, 2, 2, WCOLS], F32R)
        whl_flat = whl[:, :, :, :].rearrange("p s h c -> p (s h c)")
        wtok_h = whl_flat[:, 0:KC * D].rearrange("p (c n) -> p c n", c=KC)
        wtok_l = whl_flat[:, KC * D:2 * KC * D].rearrange("p (c n) -> p c n", c=KC)
        yh = sb("yh", [P, 2, D], F32R)
        yl = sb("yl", [P, 2, D], F32R)
        patch_parts = [(whl_flat[:, 2 * KC * D:2 * KC * D + KC * G], whl_flat[:, 2 * KC * D + KC * G:2 * KC * D + 2 * KC * G]),
                       (yh[:, :, :].rearrange("p s d -> p (s d)")[:, 0:KC * G],
                        yl[:, :, :].rearrange("p s d -> p (s d)")[:, 0:KC * G])]
        patch_h = [high.rearrange("p (b t) -> p b t", b=2) for high, _ in patch_parts]
        patch_l = [low.rearrange("p (b t) -> p b t", b=2) for _, low in patch_parts]
        raw = sb("raw", [128, 2, WCOLS], F32)
        raw_flat = raw[:, :, :].rearrange("p s c -> p (s c)")
        wtok_raw = raw_flat[:, 0:KC * D].rearrange("p (c n) -> p c n", c=KC)
        q2_t = raw_flat[:, WCOLS:WCOLS + IC * TOK // 2].bitcast(BF16).rearrange("p (c t) -> p c t", c=IC)
        w_down_last = sb("w_down_last", [128, I1], F32)
        w_down_raw = [raw_flat[:, m * I1:(m + 1) * I1] for m in range(DC - 1)] + [w_down_last[:, :]]
        h = sb("h", [G, NG, D], F32)
        h_work = sb("h_work", [G, D], F32)
        q1_t = sb("q1_t", [128, DC, TOK], BF16)
        q1 = sb("q1", [G, 2, D], BF16)
        bias_bc = sb("bias_bc", [G, D], F32)
        g2_bc = sb("g2_bc", [G, D], F32)
        b2_bc = sb("b2_bc", [G, D], F32)
        gin_bc = sb("gin_bc", [G, D], F32)
        gdn_bc = sb("gdn_bc", [G, I1], F32)
        g1_c = sb("g1_c", [128, KC], F32)
        b1_c = sb("b1_c", [128, KC], F32)
        stats = sb("stats", [G, 2, 6], F32)
        mv = sb("mv", [G, NG, 2], F32)
        ssq = sb("ssq", [G, 8], F32)
        amax = sb("amax", [G, 8], F32)
        qscale = sb("qscale", [G, 1], F32)
        deq = sb("deq", [G, NG], F32)
        deq_sq = sb("deq_sq", [G, NG], F32)
        deq2 = sb("deq2", [G, 1], F32)
        abs_sum = sb("abs_sum", [128, 8 + DC], F32)
        abs_tot = sb("abs_tot", [128, 2], F32)
        zeros16 = sb("zeros16", [128, D], BF16)
        junk = sb("junk", [128, 3 * D], BF16)
        wmean = sb("wmean", [128, 2], F32)
        wscale = sb("wscale", [128, 2], F32)
        ident = sb("ident", [128, 128], F32)
        ident16 = sb("ident16", [128, 128], BF16)
        ones = sb("ones", [128, 128], F32)
        minus_half = sb("minus_half", [G, 1], F32)
        root_in = sb("root_in", [G, N_ROOTS], F32)
        root_out = sb("root_out", [G, N_ROOTS], F32)
        before = sb("before", [G, NG, TOK], BF16)
        rw_raw = sb("rw_raw", [NE, D], F32)
        rw_t = sb("rw_t", [128, DC, NE], F32)
        logits = sb("logits", [G, NG, NE], F32)
        minus_one = sb("minus_one", [128, 1], F32)
        magic = sb("magic", [128, 1], F32)
        fscale = sb("fscale", [G, NG], F32)
        first_pick = sb("first_pick", [NE, 4, 128], F16)
        zapped = sb("zapped", [G, NE], F32)
        top8 = sb("top8", [G, 8], F32)
        neg_max = sb("neg_max", [G, NG], F32)
        expo = sb("expo", [G, NG, NE], F32)
        esum = sb("esum", [G, NG], F32)
        picked = sb("picked", [G, NG, NE], F32)
        psum8 = sb("psum8", [G, NG], F32)
        mask = sb("mask", [G, NG, NE], BF16)
        count = sb("count", [NE, 1], F32)
        n_over = sb("n_over", [NE, 1], F32)
        start = sb("start", [NE, 1], F32)
        iota_e = sb("iota_e", [NE, 1], F32)
        iota_e16 = sb("iota_e16", [NE, 1], F16)
        iota_t = sb("iota_t", [NE, NT], F32)
        before_e = sb("before_e", [NE, NE], F32)
        ones16 = sb("ones16", [NE, 1], F16)
        t_a = sb("t_a", [NE, NT], F32)
        t_b = sb("t_b", [NE, NT], F32)
        t_c = sb("t_c", [NE, NT], F32)
        owner = sb("owner", [NE, NT], F16)
        shift = sb("shift", [NE, NT], F16)
        shift_c = sb("shift_c", [NT, 1], F32)
        owner_row = sb("owner_row", [1, NT], I32)
        halff = sb("halff", [1, 1], F32)
        more_i = sb("more_i", [1, 1], I32)
        trow = sb("trow", [128, TOK], F16)
        iota_p = sb("iota_p", [128, 1], F32)
        idx_f = sb("idx_f", [128, 2], F32)
        first_f = sb("first_f", [128, 4], F32)
        first_idx = sb("first_idx", [128, 4], I32)
        idx = sb("idx", [128, 2], I32)
        gate = sb("gate", [128, 2], F32)
        xh = sb("xh", [128, 4, P], F32R)
        xl = sb("xl", [128, 4, P], F32R)
        hh = sb("hh", [IH, 2, P], F32R)
        hl = sb("hl", [IH, 2, P], F32R)
        sel = sb("sel", [P, 2, TOK], F32R)

        warm_out = sb("warm_out", [1, 4], F32)

        ps = ctx.enter_context(nc.psum_tensor("ps", [128, 8, 512], F32))

        def bank(b, n=1):
            return ps[:, b:b + n, :].rearrange("p b c -> p (b c)")

        def q2t_parts(g):
            b = 6 if g < 3 else 0
            return ((0, 9), bank(b)), ((9, IC), bank(b + 1))

        def q1t_bank(g):
            return bank((4, 7, 7, 6)[g])

        def z_bank(g):
            return bank(7 if g < 3 else 2)[0:G, :]

        def levels_of(w):
            return w.bitcast(BF16)[:, 0::2]

        def patch_bank(g):
            b = (0, 6)[g % 2]
            return ps[:, b:b + 2, 0:4 * G]

        ld_x = [sem(f"ld_x{g}") for g in range(NG)]
        ld_wtok = [sem(f"ld_wtok{n}") for n in range(2)]
        ld_vec = sem("ld_vec")
        ld_patch = sem("ld_patch")
        ld_late = sem("ld_late")
        ld_win = [sem(f"ld_win{n}") for n in range(4)]
        ld_wdown = [sem(f"ld_wdown{n}") for n in range(DC)]
        ld_gu = [[sem(f"ld_{name}{s}") for s in range(2)] for name in ("we_gate", "we_up")]
        ld_dn = [sem(f"ld_dn{n}") for n in range(2)]
        ld_pa = [sem(f"ld_pa{n}") for n in range(2)]
        ld_ps = [sem(f"ld_ps{n}") for n in range(2)]
        ld_got = [sem(f"ld_got{n}") for n in range(2)]
        dve_chain = sem("dve_chain")
        pool_chain = sem("pool_chain")
        root_ready = sem("root_ready")
        root_done = sem("root_done")
        consts = sem("consts")
        xhat_ready = sem("xhat_ready")
        t1_done = sem("t1_done")
        ph_ready = sem("ph_ready")
        pl_ready = sem("pl_ready")
        wtok_h_ready = sem("wtok_h_ready")
        wtok_l_ready = sem("wtok_l_ready")
        tok_done = sem("tok_done")
        tok_read = sem("tok_read")
        bias_done = sem("bias_done")
        bias_read = sem("bias_read")
        norm_ready = sem("norm_ready")
        affine_ready = sem("affine_ready")
        q1_ready = sem("q1_ready")
        q1t_done = sem("q1t_done")
        q1t_ready = sem("q1t_ready")
        abs_in_ready = sem("abs_in_ready")
        abs_down_ready = sem("abs_down_ready")
        tot_done = sem("tot_done")
        tot_read = sem("tot_read")
        level_ready = sem("level_ready")
        pool_level_ready = sem("pool_level_ready")
        wt_done = sem("wt_done")
        wt_ready = sem("wt_ready")
        scales_ready = sem("scales_ready")
        gate_done = sem("gate_done")
        value_done = sem("value_done")
        sig_ready = sem("sig_ready")
        gate_read = sem("gate_read")
        swi_ready = sem("swi_ready")
        ssq2_ready = sem("ssq2_ready")
        swg_ready = sem("swg_ready")
        fscale_ready = sem("fscale_ready")
        scaled_ready = sem("scaled_ready")
        q2_ready = sem("q2_ready")
        q2t_done = sem("q2t_done")
        q2t_ready = sem("q2t_ready")
        z_done = sem("z_done")
        z_read = sem("z_read")
        row_ready = sem("row_ready")
        rw_done = sem("rw_done")
        rw_ready = sem("rw_ready")
        xrt_done = sem("xrt_done")
        xrt_ready = sem("xrt_ready")
        logit_done = sem("logit_done")
        logit_read = sem("logit_read")
        max_ready = sem("max_ready")
        exp_ready = sem("exp_ready")
        gate_ready = sem("gate_ready")
        rows_out = sem("rows_out")
        mask_ready = sem("mask_ready")
        rank_done = sem("rank_done")
        place16_ready = sem("place16_ready")
        first_place_done = sem("first_place_done")
        over_ready = sem("over_ready")
        start_done = sem("start_done")
        owner_ready = sem("owner_ready")
        tables_done = sem("tables_done")
        place_ready = sem("place_ready")
        place_out = sem("place_out")
        table_ready = sem("table_ready")
        half_ready = sem("half_ready")
        hit_ready = sem("hit_ready")
        idx_ready = sem("idx_ready")
        gather_go = sem("gather_go")
        gate_col = sem("gate_col")
        guh_ready = [sem("we_gate_high_ready"), sem("we_up_high_ready")]
        gul_ready = [sem("we_gate_low_ready"), sem("we_up_low_ready")]
        dnh_ready = sem("dnh_ready")
        dnl_ready = sem("dnl_ready")
        xh_ready = sem("xh_ready")
        xl_ready = sem("xl_ready")
        silu_ready = sem("silu_ready")
        hid_ready = sem("hid_ready")
        hh_ready = sem("hh_ready")
        hl_ready = sem("hl_ready")
        yh_ready = sem("yh_ready")
        yl_ready = sem("yl_ready")
        sel_ready = sem("sel_ready")
        gu_done = sem("gu_done")
        xt_done = sem("xt_done")
        y_done = sem("y_done")
        ht_done = sem("ht_done")
        total_done = sem("total_done")
        total_act = sem("total_act")
        total_dve = sem("total_dve")
        back_done = sem("back_done")
        fin_ready = sem("fin_ready")
        out_done = sem("out_done")
        pool_out_done = sem("pool_out_done")

        block = ctx.enter_context(nc.Block())
        we_gate_v = we_gate.rearrange("e (p c) i -> e p (c i)", c=4)
        we_up_v = we_up.rearrange("e (p c) i -> e p (c i)", c=4)
        we_down_v = we_down.rearrange("e (p c) d -> e p (c d)", c=2)
        ABS_COLS = (slice(0, 8), slice(8, 8 + DC))
        ABS_PART = [0, 3, 6, 9, 11, 14, 17, 20, 22]
        WIN_PART = [0, 6, 11, 17, 22]
        win_v = w_in.rearrange("(b p) d -> p b d", p=128)
        wdown_v = w_down.rearrange("(m p) i -> p m i", p=128)

        def bcast(v, n):
            return v.rearrange("(a n) -> a n", a=1).broadcast_to([G, n])

        def store(eng, g, done):
            eng.wait_ge(fin_ready, g + 1)
            for p, n, b, size in pieces(g):
                eng.dma_start(out[b:b + size, n, :], fin[p:p + size, g, :]).then_inc(done, 16)

        @block.sync
        def _(sp):
            for g in range(NG):
                for p, n, b, size in pieces(g):
                    sp.dma_start(xt[p:p + size, g, :],
                                 x[b:b + size, n * TIN:(n + 1) * TIN, :].rearrange("b t f -> b (t f)")
                                 ).then_inc(ld_x[g], 16)
                if g < 2:
                    sp.dma_start(raw_flat[:, g * 4 * D:(g + 1) * 4 * D],
                                 w_tok.rearrange("(p c) n -> p (c n)", c=KC)[:, g * 4 * D:(g + 1) * 4 * D]
                                 ).then_inc(ld_wtok[g], 16)
            for dst, src, n in ((bias_bc, b_tok, D), (g2_bc, g2, D), (b2_bc, b2, D), (gin_bc, g_in, D)):
                sp.dma_start(dst[:, :], bcast(src, n)).then_inc(ld_vec, 16)
            for n in range(4):
                a, b = WIN_PART[n], WIN_PART[n + 1]
                sp.dma_start(w_in_raw[:, a:b, :], win_v[:, a:b, :]).then_inc(ld_win[n], 16)
            sp.dma_start(gdn_bc[:, :], bcast(g_down, I1)).then_inc(ld_late, 16)
            sp.dma_start(rw_raw[:, :], w_router).then_inc(ld_late, 16)
            sp.wait_ge(wtok_l_ready, 2)
            sp.wait_ge(bias_done, 1)
            for m in range(DC):
                sp.dma_start(w_down_raw[m], wdown_v[:, m, :]).then_inc(ld_wdown[m], 16)
            sp.wait_ge(wt_done, 17)

            def load_gate_up(half_, e, s):
                sp.dma_start(raw[:, s, half_ * WG // 2:(half_ + 1) * WG // 2], (we_gate_v, we_up_v)[half_][e, :, :]
                             ).then_inc(ld_gu[half_][s], 16)

            def load_expert(e):
                load_gate_up(0, e, e)
                load_gate_up(1, e, e)
                sp.dma_start(raw[0:IH, e, WG:WCOLS], we_down_v[e, :, :]).then_inc(ld_dn[e], 16)

            load_expert(0)
            for g in range(NG):
                sp.wait_ge(row_ready, g + 1)
                sp.dma_start(rows_dram[g * G:(g + 1) * G, 0:D], rows[:, g, 0:D]).then_inc(rows_out, 16)
            sp.wait_ge(z_done, NG)
            load_expert(1)
            sp.wait_ge(gate_ready, 1)
            sp.dma_start(rows_dram.rearrange("(g p) r -> p g r", g=NG)[:, :, D:ROW], rows[:, :, D:ROW]).then_inc(rows_out, 16)
            for half_ in range(2):
                sp.wait_ge(gul_ready[half_], 1)
                load_gate_up(half_, 2, 0)
            sp.wait_ge(place_ready, 1)
            sp.dma_start(place_dram[:, :], place_tile[:, :]).then_inc(place_out, 16)
            for half_ in range(2):
                sp.wait_ge(gul_ready[half_], 2)
                load_gate_up(half_, 3, 1)
            sp.wait_ge(place_out, 16)
            sp.wait_ge(table_ready, 1)
            half = sp.value_load(more_i[0:1, 0:1], min_val=0, max_val=14) + NE // 2

            def load_place(dst, sems, t, s):
                sp.dma_start(dst[:, s, :], place_dram[bass.ds(t, 1), :].broadcast_to([128, TOK])).then_inc(sems[s], 16)

            def load_tile(st, early=False):
                u = st.u
                e = sp.value_load(owner_row[0:1, bass.ds(st.tile(0), 1)], min_val=0, max_val=NE - 1)
                if not early:
                    wait(sp, gul_ready[0], st.upto(-2))
                    load_gate_up(0, bass.ds(e, 1), u)
                wait(sp, idx_ready, st.upto(0))
                load_place(place_a, ld_pa, st.tile(2), u)
                if not early:
                    wait(sp, gul_ready[1], st.upto(-2))
                    load_gate_up(1, bass.ds(e, 1), u)
                wait(sp, dnl_ready, st.upto(-2))
                sp.dma_start(raw[0:IH, u, WG:WCOLS], we_down_v[bass.ds(e, 1), :, :]).then_inc(ld_dn[u], 16)
                wait(sp, sel_ready, st.upto(-4))
                load_place(place_s, ld_ps, st.tile(-2), u)

            load_tile(Step(1, 0), early=True)
            load_tile(Step(1, 1), early=True)
            with sp.Fori(2, half + 1) as k:
                load_tile(Step(k, 0))
                load_tile(Step(k, 1))
            for g in (0, 2, 3):
                store(sp, g, out_done)
            sp.wait_ge(out_done, 16 * sum(len(pieces(g)) for g in (0, 2, 3)))

        @block.gpsimd
        def _(pool):
            chain = [0]

            def link(ins):
                chain[0] += 1
                ins.then_inc(pool_chain, 1)
                pool.wait_ge(pool_chain, chain[0])

            link(nc.gpsimd.memset(ones[:, :], 1.0))
            link(nc.gpsimd.memset(ident[:, :], 0.0))
            link(nc.gpsimd.affine_select(out=ident[:, :], in_=ident[:, :], compare_op=ALU.not_equal, fill=1.0,
                                         base=0, pattern=[[-1, 128]], channel_multiplier=1))
            link(nc.gpsimd.tensor_copy(ident16[:, :], ident[:, :]))
            link(nc.gpsimd.memset(minus_half[:, :], -0.5))
            nc.gpsimd.memset(minus_one[:, :], -1.0)
            nc.gpsimd.memset(magic[:, :], MAGIC)
            nc.gpsimd.memset(zeros16[:, :], 0.0).then_inc(consts, 1)
            roots = [0]

            def root(count=1):
                for _ in range(count):
                    n = roots[0]
                    roots[0] += 1
                    pool.wait_ge(root_ready, n + 1)
                    nc.gpsimd.tensor_tensor(root_out[:, n:n + 1], root_in[:, n:n + 1], minus_half[:, :], ALU.pow
                                            ).then_inc(root_done, 1)

            def affine(g):
                if g == 0:
                    pool.wait_ge(ld_vec, 16 * 4)
                pool.wait_ge(norm_ready, g + 1)
                link(nc.gpsimd.tensor_tensor(h[:, g, :], h[:, g, :], g2_bc[:, :], ALU.mult))
                nc.gpsimd.tensor_tensor(h[:, g, :], h[:, g, :], b2_bc[:, :], ALU.add).then_inc(affine_ready, 1)

            def down_gain(g):
                if g == 0:
                    pool.wait_ge(ld_late, 32)
                pool.wait_ge(swi_ready, g + 1)
                if g >= 2:
                    pool.wait_ge(q2_ready, g - 1)
                nc.gpsimd.tensor_tensor(swg[:, g % 2, :], swi[:, g % 2, :], gdn_bc[:, :], ALU.mult).then_inc(swg_ready, 1)

            root(2)
            link(nc.gpsimd.memset(before[:, :, :], 1.0))
            nc.gpsimd.affine_select(out=before[:, :, :], in_=before[:, :, :], compare_op=ALU.is_gt, fill=0.0,
                                    base=0, pattern=[[-G, NG], [1, TOK]], channel_multiplier=-1).then_inc(consts, 1)
            link(nc.gpsimd.memset(before_e[:, :], 1.0))
            nc.gpsimd.affine_select(out=before_e[:, :], in_=before_e[:, :], compare_op=ALU.is_gt, fill=0.0,
                                    base=0, pattern=[[1, NE]], channel_multiplier=-1).then_inc(consts, 1)
            nc.gpsimd.memset(ones16[:, :], 1.0).then_inc(consts, 1)
            for t, pattern, mult in ((iota_e, [[0, 1]], 1), (iota_e16, [[0, 1]], 1), (iota_t, [[1, NT]], 0),
                                     (trow, [[1, TOK]], 0), (iota_p, [[0, 1]], 1)):
                nc.gpsimd.iota(t[:, :], pattern=pattern, base=0, channel_multiplier=mult,
                               allow_small_or_imprecise_dtypes=True).then_inc(consts, 1)

            link(nc.gpsimd.memset(first_pick[:, :, :], 1.0))
            nc.gpsimd.affine_select(out=first_pick[:, :, :], in_=first_pick[:, :, :], compare_op=ALU.is_equal, fill=0.0,
                                    base=0, pattern=[[-1, 4], [0, 128]], channel_multiplier=1).then_inc(consts, 1)
            root(2)
            root()
            affine(0)
            root(2)
            affine(1)
            root()
            affine(2)
            pool.wait_ge(tot_read, 2)
            for m in range(2):
                nc.gpsimd.tensor_scalar(w_down_raw[m], w_down_raw[m], wscale[:, 1:2], LEVEL_MAGIC, ALU.mult, ALU.add
                                        ).then_inc(pool_level_ready, 1)
            root(2)
            affine(3)
            root(2)
            down_gain(0)
            root()
            for g in range(1, NG):
                down_gain(g)
                root()
            root(NG)

            def gather(lists, n, s):
                nc.gpsimd.indirect_dma_start(got[:, s, :], None, rows_dram[:, :],
                                             bass.IndirectOffsetOnAxis(ap=lists[:, n:n + 1], axis=0)
                                             ).then_inc(ld_got[s], 16)

            def split_low(st, d, n):
                s = st.slot(d)
                wait(pool, guh_ready[n], st.upto(d))
                cols = slice(n * WG // 2, (n + 1) * WG // 2)
                nc.gpsimd.tensor_tensor(whl[:, s, 1, cols], raw[:, s, cols],
                                        whl[:, s, 0, cols].bitcast(F32), ALU.subtract).then_inc(gul_ready[n], 1)

            split_low(Step(0, 0), 0, 0)
            pool.wait_ge(rows_out, 16 * (NG + 1))
            for t in range(2):
                pool.wait_ge(idx_ready, t + 1)
                gather(first_idx, t, t)
            split_low(Step(0, 0), 0, 1)
            split_low(Step(0, 0), 1, 0)
            pool.wait_ge(idx_ready, 3)
            pool.wait_ge(xt_done, 1)
            pool.wait_ge(gate_col, 1)
            gather(first_idx, 2, 0)
            split_low(Step(0, 0), 1, 1)
            pool.wait_ge(half_ready, 1)
            half = pool.value_load(more_i[0:1, 0:1], min_val=0, max_val=14) + NE // 2
            for st in steps(pool, half):
                if st.last:
                    continue
                split_low(st, 2, 0)
                wait(pool, idx_ready, st.upto(3))
                wait(pool, xt_done, st.upto(1))
                wait(pool, gate_col, st.upto(1))
                pool.sem_inc(gather_go, 1)
                if st.first:
                    gather(first_idx, 3, 1)
                else:
                    gather(idx, st.slot(3), st.slot(3))
                split_low(st, 2, 1)
            store(pool, 1, pool_out_done)
            pool.wait_ge(pool_out_done, 16 * len(pieces(1)))

        @block.scalar
        def _(act):
            act.dma_start(g1_c[:, :], g1.rearrange("(p c) -> p c", c=KC)).then_inc(ld_patch, 16)
            act.dma_start(b1_c[:, :], b1.rearrange("(p c) -> p c", c=KC)).then_inc(ld_patch, 16)

            def split_tok_high(n):
                act.wait_ge(ld_wtok[n], 16)
                if n == 0:
                    act.wait_ge(ld_patch, 32)
                for c in range(4 * n, 4 * n + 4):
                    last = nc.scalar.activation(wtok_h[:, c, :], wtok_raw[:, c, :], ACT.Copy, scale=g1_c[:, c:c + 1])
                last.then_inc(wtok_h_ready, 1)

            def patch_high(g):
                act.wait_ge(t1_done, g + 1)
                if g >= 2:
                    act.wait_ge(tok_done, g - 1)
                nc.scalar.activation(patch_h[g % 2], patch_bank(g), ACT.Copy).then_inc(ph_ready, 1)

            def prepare(n, func):
                nc.scalar.activation(warm_out[:, n:n + 1], ones[0:1, 0:1], func)

            scrapped = []

            def scrap(sem_, count):
                if scrapped:
                    act.wait_ge(*scrapped.pop())
                scrapped.append((sem_, count))

            def abs_in(n):
                act.wait_ge(ld_win[n // 2], 16)
                a, b = ABS_PART[n], ABS_PART[n + 1]
                scrap(abs_in_ready, n + 1)
                nc.scalar.activation(junk[:, 0:(b - a) * D], w_in_raw[:, a:b, :].rearrange("p b d -> p (b d)"), ACT.Abs,
                                     accum_out=abs_sum[:, n:n + 1]).then_inc(abs_in_ready, 1)

            def copy_q1t(g):
                act.wait_ge(q1t_done, g + 1)
                nc.scalar.activation(q1_t[:, :, g * G:(g + 1) * G],
                                     q1t_bank(g)[:, 0:DC * G // 2].bitcast(BF16).rearrange("p (c t) -> p c t", c=DC),
                                     ACT.Copy).then_inc(q1t_ready, 1)

            def sign_w(n):
                act.wait_ge(wt_done, n + 1)
                src = bank(6 + n % 2).bitcast(BF16)
                if n < 11:
                    dst = w_t4[:, :, 2 * n * 128:(2 * n + 2) * 128].rearrange("p c (b q) -> p b c q", b=2)
                    src = src.rearrange("p (b c q) -> p b c q", b=2, c=DC)
                else:
                    c0 = 2 * (n - 11)
                    w = min(2, IC - c0)
                    dst = wd_t[:, c0:c0 + w, :].rearrange("p c d -> p (c d)")
                    src = src[:, 0:w * D]
                nc.scalar.activation(dst, src, ACT.Sign, bias=minus_one[:, 0:1]).then_inc(wt_ready, 1)

            act.wait_ge(consts, 1)
            prepare(0, ACT.Sigmoid)
            split_tok_high(0)
            split_tok_high(1)
            patch_high(0)
            patch_high(1)
            abs_in(0)
            abs_in(1)
            patch_high(2)
            abs_in(2)
            abs_in(3)
            patch_high(3)
            for n in range(4, 8):
                abs_in(n)
            for m in range(DC):
                act.wait_ge(ld_wdown[m], 16)
                scrap(abs_down_ready, m + 1)
                nc.scalar.activation(junk[:, 0:I1], w_down_raw[m], ACT.Abs, accum_out=abs_sum[:, 8 + m:9 + m]
                                     ).then_inc(abs_down_ready, 1)
            copy_q1t(0)
            for n in range(13):
                sign_w(n)

            def sigmoid(g):
                act.wait_ge(gate_done, g + 1)
                act.wait_ge(scales_ready, g + 1)
                if g >= 2:
                    act.wait_ge(swg_ready, g - 1)
                nc.scalar.activation(swi[:, g % 2, :], bank(0, 3)[0:G, 0:I1], ACT.Sigmoid, scale=deq[:, g:g + 1]
                                     ).then_inc(sig_ready, 1)

            def square2(g):
                act.wait_ge(swi_ready, g + 1)
                scrap(ssq2_ready, g + 1)
                nc.scalar.activation(junk[0:G, 0:I1], swi[:, g % 2, :], ACT.Square, accum_out=ssq[:, 4 + g:5 + g]
                                     ).then_inc(ssq2_ready, 1)

            def scale2(g):
                act.wait_ge(fscale_ready, g + 1)
                nc.scalar.activation(swg[:, g % 2, :], swg[:, g % 2, :], ACT.Identity, scale=fscale[:, g:g + 1],
                                     bias=magic[0:G, 0:1]).then_inc(scaled_ready, 1)

            def copy_q2t(g):
                act.wait_ge(q2t_done, g + 1)
                if g:
                    act.wait_ge(q2t_ready, g)
                for (a, b), src in q2t_parts(g):
                    last = nc.scalar.activation(q2_t[:, a:b, g * G:(g + 1) * G],
                                                src[:, 0:(b - a) * G // 2].bitcast(BF16).rearrange("p (c t) -> p c t", t=G),
                                                ACT.Copy)
                last.then_inc(q2t_ready, 1)

            def copy_xrt(g):
                act.wait_ge(xrt_done, g + 1)
                if g >= 2:
                    act.wait_ge(logit_done, g - 1)
                nc.scalar.activation(xr_t[:, g % 2, :, :], bank(3 + g % 2)[:, 0:DC * G].rearrange("p (c t) -> p c t", c=DC),
                                     ACT.Copy).then_inc(xrt_ready, 1)

            sigmoid(0)
            for n in range(13, 17):
                sign_w(n)
            copy_q1t(1)
            act.wait_ge(rw_done, 1)
            nc.scalar.activation(rw_t[:, :, :], bank(6)[:, 0:DC * NE].rearrange("p (c e) -> p c e", c=DC), ACT.Copy
                                 ).then_inc(rw_ready, 1)
            square2(0)
            sigmoid(1)
            copy_q1t(2)
            copy_q1t(3)
            square2(1)
            sigmoid(2)
            scale2(0)
            copy_q2t(0)
            square2(2)
            sigmoid(3)
            prepare(1, ACT.Exp)
            scale2(1)
            copy_q2t(1)
            square2(3)
            scale2(2)
            copy_q2t(2)
            scale2(3)
            copy_q2t(3)
            for g in range(NG):
                copy_xrt(g)
            for g in range(NG):
                act.wait_ge(max_ready, g + 1)
                nc.scalar.activation(expo[:, g, :], logits[:, g, :], ACT.Exp, bias=neg_max[:, g:g + 1],
                                     accum_out=esum[:, g:g + 1]).then_inc(exp_ready, 1)
            prepare(2, ACT.Silu)

            def gu_high(half_, st, d):
                s = st.slot(d)
                cols = slice(half_ * WG // 2, (half_ + 1) * WG // 2)
                act.wait_ge(ld_gu[half_][s], st.dma(d))
                nc.scalar.activation(whl[:, s, 0, cols], raw[:, s, cols], ACT.Copy).then_inc(guh_ready[half_], 1)

            def down_high(st, d):
                s = st.slot(d)
                act.wait_ge(ld_dn[s], st.dma(d))
                nc.scalar.activation(whl[0:IH, s, 0, WG:WCOLS], raw[0:IH, s, WG:WCOLS], ACT.Copy).then_inc(dnh_ready, 1)

            def x_high(st, d):
                act.wait_ge(xt_done, st.upto(d))
                nc.scalar.activation(xh[:, :, :], bank(6).rearrange("p (c t) -> p c t", c=4), ACT.Copy
                                     ).then_inc(xh_ready, 1)

            for d in range(2):
                for half_ in range(2):
                    gu_high(half_, Step(0, 0), d)
            down_high(Step(0, 0), 0)
            x_high(Step(0, 0), 0)
            act.wait_ge(half_ready, 1)
            half = act.value_load(more_i[0:1, 0:1], min_val=0, max_val=14) + NE // 2
            for st in steps(act, half):
                if not st.last:
                    act.wait_ge(gu_done, st.upto(0))
                    nc.scalar.activation(sg[:, :], bank(4)[:, 0:IE], ACT.Silu).then_inc(silu_ready, 1)
                    x_high(st, 1)
                    gu_high(0, st, 2)
                    act.wait_ge(ht_done, st.upto(0))
                    nc.scalar.activation(hh[:, :, :], bank(5)[0:IH, 0:2 * P].rearrange("p (c t) -> p c t", c=2), ACT.Copy
                                         ).then_inc(hh_ready, 1)
                if not st.first and not (st.last and st.u == 1):
                    s = st.slot(-1)
                    act.wait_ge(y_done, st.upto(-1))
                    act.wait_ge(gate_col, st.upto(-1))
                    nc.scalar.activation(yh[:, s, :], bank(7), ACT.Copy, scale=gate[:, s:s + 1]).then_inc(yh_ready, 1)
                if not st.last:
                    gu_high(1, st, 2)
                    down_high(st, 1)
            for c in (1, 3):
                act.wait_ge(total_done, c + 1)
                nc.scalar.activation(total_t[:, c, :], bank(c)[:, 0:TOK], ACT.Copy).then_inc(total_act, 1)

        @block.tensor
        def _(pe):
            def three(dst, ah, al, bh, bl, start, stop):
                nc.tensor.matmul(dst, ah, bh, start=start, stop=False)
                nc.tensor.matmul(dst, ah, bl, start=False, stop=False)
                return nc.tensor.matmul(dst, al, bh, start=False, stop=stop)

            def transpose_patch(g):
                pe.wait_ge(xhat_ready, g + 1)
                if g >= 2:
                    pe.wait_ge(pl_ready, g - 1)
                dst = patch_bank(g)
                for c in range(KC):
                    last = nc.tensor.transpose(dst[:, c // 4, (c % 4) * G:(c % 4 + 1) * G], xt[:, g, c::KC],
                                               ident[0:G, 0:G])
                last.then_inc(t1_done, 1)

            def beta_product():
                pe.wait_ge(ld_wtok[0], 16)
                pe.wait_ge(ld_wtok[1], 16)
                pe.wait_ge(ld_patch, 32)
                for c in range(KC):
                    last = nc.tensor.matmul(bank(4)[0:G, :], b1_c[:, c:c + 1].broadcast_to([128, G]), wtok_raw[:, c, :],
                                            start=c == 0, stop=c == KC - 1)
                last.then_inc(bias_done, 1)

            def tok_product(g):
                acc = bank(2 + g % 2)[0:G, :]
                pe.wait_ge(pl_ready, g + 1)
                if g == 0:
                    pe.wait_ge(wtok_l_ready, 2)
                if g >= 2:
                    pe.wait_ge(tok_read, g - 1)
                for c in range(KC):
                    cols = slice((c % 4) * G, (c % 4 + 1) * G)
                    last = three(acc, patch_h[g % 2][:, c // 4, cols], patch_l[g % 2][:, c // 4, cols],
                                 wtok_h[:, c, :], wtok_l[:, c, :], c == 0, c == KC - 1)
                last.then_inc(tok_done, 1)

            def transpose_q1(g):
                pe.wait_ge(q1_ready, g + 1)
                if g:
                    pe.wait_ge(q1t_ready, g)
                if g == 1:
                    pe.wait_ge(wt_ready, 16)
                for c in range(DC):
                    last = nc.tensor.transpose(q1t_bank(g)[:, c * G // 2:(c + 1) * G // 2].bitcast(BF16),
                                               q1[:, g % 2, c * 128:(c + 1) * 128], ident16[0:G, 0:G])
                last.then_inc(q1t_done, 1)

            def total(which):
                if which == 0:
                    pe.wait_ge(abs_in_ready, 8)
                else:
                    pe.wait_ge(abs_down_ready, DC)
                    pe.wait_ge(tot_read, 1)
                nc.tensor.matmul(bank(5)[:, ABS_COLS[which]], ones[:, :], abs_sum[:, ABS_COLS[which]], start=True, stop=True
                                 ).then_inc(tot_done, 1)

            def transpose_w(n):
                pe.wait_ge(level_ready, n + 1 if n < 11 else 13)
                if n >= 11:
                    pe.wait_ge(pool_level_ready, 2)
                if n >= 2:
                    pe.wait_ge(wt_ready, n - 1)
                dst = bank(6 + n % 2).bitcast(BF16)
                if n < 11:
                    pairs = [(levels_of(w_in_raw[:, 2 * n + b, c * 128:(c + 1) * 128]), b * DC + c)
                             for b in range(2) for c in range(DC)]
                else:
                    c0 = 2 * (n - 11)
                    pairs = [(levels_of(w_down_raw[m][:, (c0 + c) * 128:(c0 + c + 1) * 128]), c * DC + m)
                             for c in range(min(2, IC - c0)) for m in range(DC)]
                for src, b in pairs:
                    last = nc.tensor.transpose(dst[:, b * 128:(b + 1) * 128], src, ident16[:, :])
                last.then_inc(wt_done, 1)

            def gate_product(g):
                if g == 0:
                    pe.wait_ge(tok_read, NG)
                    pe.wait_ge(wt_ready, 11)
                else:
                    pe.wait_ge(gate_read, g)
                pe.wait_ge(q1t_ready, g + 1)
                products(g, 0).then_inc(gate_done, 1)

            def value_product(g):
                if g == 0:
                    pe.wait_ge(q1t_ready, 1)
                    pe.wait_ge(tot_read, 2)
                else:
                    pe.wait_ge(swi_ready, g)
                products(g, 1).then_inc(value_done, 1)

            def products(g, half_):
                for a in range(0, I1, 512):
                    w = min(512, I1 - a)
                    for c in range(DC):
                        last = nc.tensor.matmul(bank(3 * half_, 3)[0:G, a:a + w], q1_t[:, c, g * G:(g + 1) * G],
                                                w_t4[:, c, half_ * I1 + a:half_ * I1 + a + w],
                                                start=c == 0, stop=c == DC - 1)
                return last

            def transpose_q2(g):
                pe.wait_ge(q2_ready, g + 1)
                if g == 0:
                    pe.wait_ge(q1t_ready, NG)
                if g in (1, 2):
                    pe.wait_ge(q2t_ready, g)
                for (a, b), dst in q2t_parts(g):
                    if a and g in (1, 2):
                        pe.wait_ge(z_read, g)
                    for c in range(a, b):
                        last = nc.tensor.transpose(dst[:, (c - a) * G // 2:(c - a + 1) * G // 2].bitcast(BF16),
                                                   q2[:, c * 128:(c + 1) * 128], ident16[0:G, 0:G])
                last.then_inc(q2t_done, 1)

            def mlp_out(g, between=None):
                pe.wait_ge(q2t_ready, g + 1)
                for c in range(IC):
                    if between is not None and c == IC // 2:
                        transpose_q2(between)
                    last = nc.tensor.matmul(z_bank(g), q2_t[:, c, g * G:(g + 1) * G], wd_t[:, c, :],
                                            start=c == 0, stop=c == IC - 1)
                last.then_inc(z_done, 1)

            def transpose_row(g):
                pe.wait_ge(row_ready, g + 1)
                if g >= 2:
                    pe.wait_ge(xrt_ready, g - 1)
                for c in range(DC):
                    last = nc.tensor.transpose(bank(3 + g % 2)[:, c * G:(c + 1) * G], rows[:, g, c * 128:(c + 1) * 128],
                                               ident[0:G, 0:G])
                last.then_inc(xrt_done, 1)

            def logits_product(g):
                pe.wait_ge(xrt_ready, g + 1)
                if g >= 2:
                    pe.wait_ge(logit_read, g - 1)
                for c in range(DC):
                    last = nc.tensor.matmul(bank(5 + g % 2)[0:G, 0:NE], xr_t[:, g % 2, c, :], rw_t[:, c, :], start=c == 0, stop=c == DC - 1)
                last.then_inc(logit_done, 1)

            pe.wait_ge(consts, 1)
            transpose_patch(0)
            transpose_patch(1)
            beta_product()
            tok_product(0)
            transpose_patch(2)
            tok_product(1)
            transpose_patch(3)
            tok_product(2)
            tok_product(3)
            pe.wait_ge(bias_read, 1)
            transpose_q1(0)
            total(0)
            for n in range(2):
                transpose_w(n)
            total(1)
            for n in range(2, 13):
                transpose_w(n)
            gate_product(0)
            for n in range(13, 15):
                transpose_w(n)
            value_product(0)
            for n in range(15, 17):
                transpose_w(n)
            transpose_q1(1)
            pe.wait_ge(ld_late, 32)
            pe.wait_ge(wt_ready, 17)
            for c in range(DC):
                last = nc.tensor.transpose(bank(6)[:, c * NE:(c + 1) * NE], rw_raw[:, c * 128:(c + 1) * 128],
                                           ident[0:NE, 0:NE])
            last.then_inc(rw_done, 1)
            gate_product(1)
            transpose_q1(2)
            value_product(1)
            pe.wait_ge(rw_ready, 1)
            transpose_q1(3)
            gate_product(2)
            value_product(2)
            transpose_q2(0)
            gate_product(3)
            mlp_out(0)
            value_product(3)
            transpose_q2(1)
            mlp_out(1)
            transpose_q2(2)
            mlp_out(2, between=3)
            mlp_out(3)
            transpose_row(0)
            transpose_row(1)
            logits_product(0)
            logits_product(1)
            transpose_row(2)
            transpose_row(3)
            logits_product(2)
            logits_product(3)

            def transpose_x(st, d):
                s = st.slot(d)
                pe.wait_ge(ld_got[s], st.dma(d))
                for c in range(4):
                    last = nc.tensor.transpose(bank(6)[:, c * P:(c + 1) * P], got[:, s, c:D:4], ident[:, :])
                last.then_inc(xt_done, 1)

            def zero_sum(c):
                pe.wait_ge(idx_ready, c + 1)
                nc.tensor.matmul(bank(c)[:, 0:TOK], zeros16[:, 0:128], zeros16[:, 0:TOK], start=True, stop=False,
                                 skip_group_check=True)

            pe.wait_ge(consts, 10)
            for g in range(NG):
                pe.wait_ge(mask_ready, g + 1)
                nc.tensor.matmul(bank(0)[0:NE, 0:TOK], mask[:, g, :], before[:, g, :], start=g == 0, stop=g == NG - 1)
                last = nc.tensor.transpose(bank(7)[0:NE, g * G // 2:(g + 1) * G // 2].bitcast(BF16), mask[:, g, :],
                                           ident16[0:G, 0:G])
            last.then_inc(rank_done, 1)
            pe.wait_ge(place16_ready, 1)
            for t in range(4):
                nc.tensor.matmul(bank(t)[:, 0:TOK], first_pick[:, t, :], place[:, :], start=True, stop=True
                                 ).then_inc(first_place_done, 1)
            pe.wait_ge(over_ready, 1)
            nc.tensor.matmul(bank(4)[0:NE, 0:1], before_e[:, :], n_over[:, :], start=True, stop=True)
            nc.tensor.matmul(bank(4)[0:1, 1:2], n_over[:, :], ones[0:NE, 0:1], start=True, stop=True
                             ).then_inc(start_done, 1)
            zero_sum(0)
            zero_sum(1)
            transpose_x(Step(0, 0), 0)
            pe.wait_ge(owner_ready, 1)
            nc.tensor.matmul(bank(5)[0:NT, 0:TOK], owner[:, :], place[:, :], start=True, stop=True)
            nc.tensor.matmul(bank(7)[0:NT, 2:3], shift[:, :], ones16[:, :], start=True, stop=True)
            nc.tensor.matmul(bank(7)[0:1, 8:8 + NT], iota_e16[:, :], owner[:, :], start=True, stop=True
                             ).then_inc(tables_done, 1)

            zero_sum(2)
            zero_sum(3)

            def gate_up(st):
                s = st.u
                pe.wait_ge(xl_ready, st.upto(0))
                pe.wait_ge(gul_ready[0], st.upto(0))
                pe.wait_ge(gul_ready[1], st.upto(0))
                wait(pe, hid_ready, st.upto(-1))
                wh = whl[:, s, 0, 0:WG].rearrange("p (n c i) -> p n c i", n=2, c=4)
                wl = whl[:, s, 1, 0:WG].rearrange("p (n c i) -> p n c i", n=2, c=4)
                dst = bank(4)[:, 0:2 * IE].rearrange("p (n i) -> p n i", n=2)
                for c in range(4):
                    last = three(dst, xh[:, c, :], xl[:, c, :], wh[:, :, c, :], wl[:, :, c, :], c == 0, c == 3)
                last.then_inc(gu_done, 1)

            def down(st):
                s = st.slot(-1)
                pe.wait_ge(hl_ready, st.upto(-1))
                pe.wait_ge(dnl_ready, st.upto(-1))
                wait(pe, yl_ready, st.upto(-2))
                wh = whl[0:IH, s, 0, WG:WCOLS].rearrange("p (c d) -> p c d", c=2)
                wl = whl[0:IH, s, 1, WG:WCOLS].rearrange("p (c d) -> p c d", c=2)
                for c in range(2):
                    last = three(bank(7), hh[:, c, :], hl[:, c, :], wh[:, c, :], wl[:, c, :], c == 0, c == 1)
                last.then_inc(y_done, 1)

            def add_rows(st, stop=False):
                s = st.slot(-2)
                pe.wait_ge(sel_ready, st.upto(-2))
                pe.wait_ge(yl_ready, st.upto(-2))
                for c in range(DC):
                    for n, part in enumerate((yh, yl)):
                        last = nc.tensor.matmul(bank(c)[:, 0:TOK], part[:, s, c * 128:(c + 1) * 128], sel[:, s, :],
                                                start=False, stop=stop and n == 1, skip_group_check=True)
                    if stop:
                        last.then_inc(total_done, 1)

            pe.wait_ge(half_ready, 1)
            half = pe.value_load(more_i[0:1, 0:1], min_val=0, max_val=14) + NE // 2
            for st in steps(pe, half):
                if not st.last:
                    gate_up(st)
                    transpose_x(st, 1)
                if not st.first and not (st.last and st.u == 1):
                    down(st)
                if not st.last:
                    pe.wait_ge(hid_ready, st.upto(0))
                    for c in range(2):
                        last = nc.tensor.transpose(bank(5)[0:IH, c * P:(c + 1) * P], hid[:, c::2], ident[:, :])
                    last.then_inc(ht_done, 1)
                if not isinstance(st.k, int):
                    add_rows(st, stop=st.last and st.u == 1)
            pe.wait_ge(total_act, 2)
            pe.wait_ge(total_dve, 2)
            for g in range(NG):
                for c in range(DC):
                    last = nc.tensor.transpose(bank(4 + g)[0:G, c * 128:(c + 1) * 128],
                                               total_t[:, c, g * G:(g + 1) * G], ident[:, :])
                last.then_inc(back_done, 1)

        @block.vector
        def _(dve):
            chain = [0]

            def link(ins):
                chain[0] += 1
                ins.then_inc(dve_chain, 1)
                dve.wait_ge(dve_chain, chain[0])

            def moments(src, n, slot=0):
                for c in range(n // 512):
                    ins = nc.vector.bn_stats(stats[:, c, :], src[:, c * 512:(c + 1) * 512])
                link(ins)
                link(nc.vector.bn_aggr(mv[:, slot, :], stats[:, 0:n // 512, :].rearrange("p c s -> p (c s)")))

            powers = [0]

            def power(src, scale, eps):
                return get_power(ask_power(src, scale, eps))

            def ask_power(src, scale, eps):
                n = powers[0]
                powers[0] += 1
                nc.vector.tensor_scalar(root_in[:, n:n + 1], src, scale, eps, ALU.mult, ALU.add).then_inc(root_ready, 1)
                return n

            def get_power(n):
                dve.wait_ge(root_done, n + 1)
                return root_out[:, n:n + 1]

            def norm_patch(g):
                dve.wait_ge(ld_x[g], 16 * len(pieces(g)))
                moments(xt[:, g, :], KIN)
                rstd = power(mv[:, 0, 1:2], 1.0, EPS6)
                nc.vector.tensor_scalar(xt[:, g, :], xt[:, g, :], mv[:, 0, 0:1], rstd[:, 0:1], ALU.subtract, ALU.mult
                                        ).then_inc(xhat_ready, 1)

            def patch_low(g):
                dve.wait_ge(ph_ready, g + 1)
                nc.vector.tensor_tensor(patch_l[g % 2], patch_bank(g), patch_h[g % 2].bitcast(F32), ALU.subtract
                                        ).then_inc(pl_ready, 1)

            def quant_scale(which, g, norm):
                n = 4 * which + g
                link(nc.vector.tensor_scalar(amax[:, n:n + 1], amax[:, n:n + 1], norm[:, 0:1], EPS5, ALU.mult, ALU.max))
                link(nc.vector.reciprocal(qscale[:, :], amax[:, n:n + 1]))
                return nc.vector.tensor_scalar(fscale[:, g:g + 1], qscale[:, :], 127.0, norm[:, 0:1], ALU.mult, ALU.mult)

            def tok_low(n):
                dve.wait_ge(wtok_h_ready, n + 1)
                dve.wait_ge(ld_patch, 32)
                for c in range(4 * n, 4 * n + 4):
                    last = nc.vector.scalar_tensor_tensor(wtok_l[:, c, :], wtok_raw[:, c, :], g1_c[:, c:c + 1],
                                                          wtok_h[:, c, :].bitcast(F32), ALU.mult, ALU.subtract)
                last.then_inc(wtok_l_ready, 1)

            def full_bias():
                dve.wait_ge(bias_done, 1)
                nc.vector.tensor_tensor(bias_bc[:, :], bank(4)[0:G, :], bias_bc[:, :], ALU.add).then_inc(bias_read, 1)
                dve.wait_ge(bias_read, 1)

            def token_sum(g):
                dve.wait_ge(tok_done, g + 1)
                nc.vector.tensor_tensor(h[:, g, :], bank(2 + g % 2)[0:G, :], bias_bc[:, :], ALU.add).then_inc(tok_read, 1)

            def token_norm(g):
                dve.wait_ge(tok_read, g + 1)
                moments(h[:, g, :], D)
                rstd = power(mv[:, 0, 1:2], 1.0, EPS6)
                nc.vector.tensor_scalar(h[:, g, :], h[:, g, :], mv[:, 0, 0:1], rstd[:, 0:1], ALU.subtract, ALU.mult
                                        ).then_inc(norm_ready, 1)

            def quantise1(g):
                dve.wait_ge(affine_ready, g + 1)
                moments(h[:, g, :], D)
                n = ask_power(mv[:, 0, 1:2], 1.0 + EPS6, EPS5 * EPS6)
                link(nc.vector.scalar_tensor_tensor(h_work[:, :], h[:, g, :], mv[:, 0, 0:1], gin_bc[:, :],
                                                    ALU.subtract, ALU.mult))
                link(nc.vector.tensor_reduce(amax[:, g:g + 1], h_work[:, :], AX.X, ALU.max, apply_absolute_value=True))
                link(quant_scale(0, g, get_power(n)))
                link(nc.vector.tensor_scalar(h_work[:, :], h_work[:, :], fscale[:, g:g + 1], MAGIC, ALU.mult, ALU.add))
                if g >= 2:
                    dve.wait_ge(q1t_done, g - 1)
                nc.vector.tensor_scalar(q1[:, g % 2, :], h_work[:, :], -MAGIC, 127.0, ALU.add, ALU.min
                                        ).then_inc(q1_ready, 1)

            def weight_scale(which, size):
                dve.wait_ge(tot_done, which + 1)
                w = slice(which, which + 1)
                link(nc.vector.tensor_reduce(abs_tot[:, w], bank(5)[:, ABS_COLS[which]], AX.X, ALU.add))
                link(nc.vector.tensor_scalar(wmean[:, w], abs_tot[:, w], 1.0 / size, EPS5, ALU.mult, ALU.max))
                nc.vector.reciprocal(wscale[:, w], wmean[:, w]).then_inc(tot_read, 1)
                dve.wait_ge(tot_read, which + 1)

            def product_scale(g):
                link(nc.vector.tensor_scalar(deq[:, g:g + 1], amax[:, g:g + 1], 1.0 / 127.0, wmean[0:G, 0:1],
                                             ALU.mult, ALU.mult))
                nc.vector.tensor_tensor(deq_sq[:, g:g + 1], deq[:, g:g + 1], deq[:, g:g + 1], ALU.mult
                                        ).then_inc(scales_ready, 1)

            def levels(n):
                which = 0 if n < 11 else 1
                w = w_in_raw[:, 2 * n:2 * n + 2, :] if n < 11 else w_down_raw[n - 9]
                nc.vector.tensor_scalar(w, w, wscale[:, which:which + 1], LEVEL_MAGIC, ALU.mult, ALU.add
                                        ).then_inc(level_ready, 1)

            dve.wait_ge(consts, 1)
            norm_patch(0)
            norm_patch(1)
            tok_low(0)
            tok_low(1)
            patch_low(0)
            patch_low(1)
            norm_patch(2)
            norm_patch(3)
            dve.wait_ge(ld_vec, 16 * 4)
            full_bias()
            patch_low(2)
            token_sum(0)
            token_norm(0)
            patch_low(3)
            token_sum(1)
            token_norm(1)
            quantise1(0)
            token_sum(2)
            token_norm(2)
            token_sum(3)
            weight_scale(0, 2 * I1 * D)
            product_scale(0)
            for n in range(4):
                levels(n)
            weight_scale(1, I1 * D)
            for n in range(4, 13):
                levels(n)
            quantise1(1)
            product_scale(1)
            token_norm(3)

            def gate_part(g):
                v = swi[:, g % 2, :]
                dve.wait_ge(sig_ready, g + 1)
                nc.vector.tensor_tensor(v, bank(0, 3)[0:G, 0:I1], v, ALU.mult).then_inc(gate_read, 1)

            def value_part(g):
                v = swi[:, g % 2, :]
                dve.wait_ge(value_done, g + 1)
                dve.wait_ge(scales_ready, g + 1)
                dve.wait_ge(gate_read, g + 1)
                nc.vector.scalar_tensor_tensor(v, bank(3, 3)[0:G, 0:I1], deq_sq[:, g:g + 1], v, ALU.mult, ALU.mult
                                               ).then_inc(swi_ready, 1)

            norm2 = [0] * NG

            def ask_norm2(g):
                dve.wait_ge(ssq2_ready, g + 1)
                norm2[g] = ask_power(ssq[:, 4 + g:5 + g], 1.0 / I1, EPS6)

            def factor2(g):
                n = 4 + g
                dve.wait_ge(swg_ready, g + 1)
                link(nc.vector.tensor_reduce(amax[:, n:n + 1], swg[:, g % 2, :], AX.X, ALU.max, apply_absolute_value=True))
                quant_scale(1, g, get_power(norm2[g])).then_inc(fscale_ready, 1)

            def quantise2(g):
                dve.wait_ge(scaled_ready, g + 1)
                if g:
                    dve.wait_ge(q2t_done, g)
                nc.vector.tensor_scalar(q2[:, :], swg[:, g % 2, :], -MAGIC, 127.0, ALU.add, ALU.min).then_inc(q2_ready, 1)

            def residual(g):
                dve.wait_ge(z_done, g + 1)
                link(nc.vector.tensor_scalar(deq2[:, :], amax[:, 4 + g:5 + g], 1.0 / 127.0, wmean[0:G, 1:2],
                                             ALU.mult, ALU.mult))
                nc.vector.scalar_tensor_tensor(h[:, g, :], z_bank(g), deq2[:, 0:1], h[:, g, :], ALU.mult, ALU.add
                                               ).then_inc(z_read, 1)
                dve.wait_ge(z_read, g + 1)

            def row_norm(g):
                moments(h[:, g, :], D, g)
                return ask_power(mv[:, g, 1:2], 1.0, EPS5)

            def row(g, n):
                nc.vector.tensor_scalar(rows[:, g, 0:D], h[:, g, :], mv[:, g, 0:1], get_power(n), ALU.subtract, ALU.mult
                                        ).then_inc(row_ready, 1)

            def top(g):
                dve.wait_ge(logit_done, g + 1)
                row = logits[:, g, :]
                nc.vector.tensor_copy(row, bank(5 + g % 2)[0:G, 0:NE]).then_inc(logit_read, 1)
                dve.wait_ge(logit_read, g + 1)
                link(nc.vector.max(top8[:, :], row))
                nc.vector.tensor_scalar(neg_max[:, g:g + 1], top8[:, 0:1], -1.0, None, ALU.mult).then_inc(max_ready, 1)
                link(nc.vector.match_replace(zapped[:, :], top8[:, :], row, -3.0e38))
                nc.vector.tensor_tensor(mask[:, g, :], zapped[:, :], row, ALU.not_equal).then_inc(mask_ready, 1)

            gate_part(0)
            value_part(0)
            quantise1(2)
            product_scale(2)
            quantise1(3)
            product_scale(3)
            gate_part(1)
            value_part(1)
            ask_norm2(0)
            factor2(0)
            gate_part(2)
            quantise2(0)
            value_part(2)
            ask_norm2(1)
            factor2(1)
            gate_part(3)
            residual(0)
            quantise2(1)
            ask_norm2(2)
            value_part(3)
            factor2(2)
            ask_norm2(3)
            residual(1)
            quantise2(2)
            factor2(3)
            quantise2(3)
            norms = [row_norm(0), row_norm(1)]
            row(0, norms[0])
            row(1, norms[1])
            residual(2)
            norms.append(row_norm(2))
            residual(3)
            norms.append(row_norm(3))
            row(2, norms[2])
            row(3, norms[3])
            for g in range(NG):
                top(g)

            def picked_weights():
                dve.wait_ge(exp_ready, NG)
                dve.wait_ge(mask_ready, NG)
                link(nc.vector.reciprocal(esum[:, :], esum[:, :]))
                for g in range(NG):
                    last = nc.vector.scalar_tensor_tensor(picked[:, g, :], expo[:, g, :], esum[:, g:g + 1], mask[:, g, :],
                                                          ALU.mult, ALU.mult, accum_out=psum8[:, g:g + 1])
                link(last)
                link(nc.vector.reciprocal(psum8[:, :], psum8[:, :]))
                for g in range(NG):
                    last = nc.vector.tensor_scalar(rows[:, g, D:ROW], picked[:, g, :], psum8[:, g:g + 1], None, ALU.mult)
                last.then_inc(gate_ready, 1)

            picked_weights()

            dve.wait_ge(rank_done, 1)
            rank = bank(0)[0:NE, 0:TOK]
            link(nc.vector.tensor_copy(mask_t[:, :], bank(7)[0:NE, 0:TOK // 2].bitcast(BF16)))
            link(nc.vector.tensor_tensor(count[:, :], mask_t[:, TOK - 1:TOK], rank[:, TOK - 1:TOK], ALU.add))
            link(nc.vector.tensor_scalar(mask_t[:, :], mask_t[:, :], FAR, -FAR, ALU.mult, ALU.add))
            nc.vector.tensor_tensor(place[:, :], mask_t[:, :], rank, ALU.add).then_inc(place16_ready, 1)
            link(nc.vector.tensor_scalar(n_over[:, :], count[:, :], float(P), None, ALU.is_gt))
            link(nc.vector.scalar_tensor_tensor(n_over[:, :], count[:, :], 2.0 * P, n_over[:, :], ALU.is_gt, ALU.add))
            nc.vector.scalar_tensor_tensor(n_over[:, :], count[:, :], 3.0 * P, n_over[:, :], ALU.is_gt, ALU.add
                                           ).then_inc(over_ready, 1)

            def find_first(t):
                dve.wait_ge(first_place_done, t + 1)
                nc.vector.scalar_tensor_tensor(hit[:, :], bank(t)[:, 0:TOK], iota_p[:, 0:1], trow[:, :], ALU.is_equal, ALU.mult,
                                               accum_out=first_f[:, t:t + 1]).then_inc(hit_ready, 1)
                dve.wait_ge(hit_ready, t + 1)
                nc.vector.tensor_copy(first_idx[:, t:t + 1], first_f[:, t:t + 1]).then_inc(idx_ready, 1)

            def x_low(st, d):
                dve.wait_ge(xh_ready, st.upto(d))
                nc.vector.tensor_tensor(xl[:, :, :], bank(6).rearrange("p (c t) -> p c t", c=4), xh[:, :, :].bitcast(F32),
                                        ALU.subtract).then_inc(xl_ready, 1)

            find_first(0)
            find_first(1)
            dve.wait_ge(start_done, 1)
            link(nc.vector.tensor_scalar(start[:, :], bank(4)[0:NE, 0:1], float(NE), None, ALU.add))
            link(nc.vector.tensor_scalar(halff[:, :], bank(4)[0:1, 1:2], 0.5, 0.25, ALU.mult, ALU.add))
            link(nc.vector.tensor_scalar(halff[:, :], halff[:, :], MAGIC, -MAGIC, ALU.add, ALU.add))
            nc.vector.tensor_copy(more_i[:, :], halff[:, :]).then_inc(half_ready, 1)
            link(nc.vector.tensor_scalar(t_a[:, :], iota_t[:, :], start[:, 0:1], None, ALU.subtract))
            link(nc.vector.tensor_scalar(t_b[:, :], t_a[:, :], 0.0, None, ALU.is_ge))
            link(nc.vector.scalar_tensor_tensor(t_b[:, :], t_a[:, :], n_over[:, 0:1], t_b[:, :], ALU.is_lt, ALU.mult))
            link(nc.vector.tensor_scalar(t_c[:, :], iota_t[:, :], iota_e[:, 0:1], None, ALU.is_equal))
            link(nc.vector.tensor_tensor(t_c[:, :], t_c[:, :], t_b[:, :], ALU.add))
            link(nc.vector.tensor_copy(owner[:, :], t_c[:, :]))
            link(nc.vector.scalar_tensor_tensor(t_b[:, :], t_a[:, :], 1.0, t_b[:, :], ALU.add, ALU.mult))
            link(nc.vector.tensor_scalar(t_b[:, :], t_b[:, :], -float(P), None, ALU.mult))
            nc.vector.scalar_tensor_tensor(shift[:, :], t_c[:, :], FAR, t_b[:, :], ALU.mult, ALU.add
                                           ).then_inc(owner_ready, 1)
            find_first(2)
            find_first(3)
            zero = Step(0, 0)
            x_low(zero, 0)
            dve.wait_ge(tables_done, 1)
            link(nc.vector.tensor_scalar(shift_c[:, :], bank(7)[0:NT, 2:3], -FAR, None, ALU.add))
            nc.vector.tensor_scalar(place_tile[:, :], bank(5)[0:NT, 0:TOK], shift_c[:, 0:1], None, ALU.add
                                    ).then_inc(place_ready, 1)
            nc.vector.tensor_copy(owner_row[:, :], bank(7)[0:1, 8:8 + NT]).then_inc(table_ready, 1)

            def find(st, d):
                s = st.slot(d)
                dve.wait_ge(ld_pa[s], st.dma(d - 4))
                nc.vector.scalar_tensor_tensor(hit[:, :], place_a[:, s, :], iota_p[:, 0:1], trow[:, :], ALU.is_equal, ALU.mult,
                                               accum_out=idx_f[:, s:s + 1]).then_inc(hit_ready, 1)
                dve.wait_ge(hit_ready, st.upto(d))
                nc.vector.tensor_copy(idx[:, s:s + 1], idx_f[:, s:s + 1]).then_inc(idx_ready, 1)

            def gates(st, d):
                s = st.slot(d)
                e = dve.value_load(owner_row[0:1, bass.ds(st.tile(d), 1)], min_val=0, max_val=NE - 1)
                dve.wait_ge(ld_got[s], st.dma(d))
                wait(dve, yl_ready, st.upto(d - 2))
                nc.vector.tensor_copy(gate[:, s:s + 1], got[:, s, bass.ds(e + D, 1)]).then_inc(gate_col, 1)

            def down_low(st, d):
                s = st.slot(d)
                dve.wait_ge(dnh_ready, st.upto(d))
                nc.vector.tensor_tensor(whl[0:IH, s, 1, WG:WCOLS], raw[0:IH, s, WG:WCOLS],
                                        whl[0:IH, s, 0, WG:WCOLS].bitcast(F32), ALU.subtract).then_inc(dnl_ready, 1)

            dve.wait_ge(ld_got[0], 16)
            nc.vector.tensor_copy(gate[:, 0:1], got[:, 0, D:D + 1]).then_inc(gate_col, 1)
            down_low(zero, 0)
            dve.wait_ge(table_ready, 1)
            half = dve.value_load(more_i[0:1, 0:1], min_val=0, max_val=14) + NE // 2
            for st in steps(dve, half):
                if not st.last:
                    dve.wait_ge(silu_ready, st.upto(0))
                    nc.vector.tensor_tensor(hid[:, :], bank(4)[:, IE:2 * IE], sg[:, :], ALU.mult).then_inc(hid_ready, 1)
                    x_low(st, 1)
                    dve.wait_ge(hh_ready, st.upto(0))
                    nc.vector.tensor_tensor(hl[:, :, :], bank(5)[0:IH, 0:2 * P].rearrange("p (c t) -> p c t", c=2),
                                            hh[:, :, :].bitcast(F32), ALU.subtract).then_inc(hl_ready, 1)
                if not st.first and not (st.last and st.u == 1):
                    s = st.slot(-1)
                    dve.wait_ge(yh_ready, st.upto(-1))
                    nc.vector.scalar_tensor_tensor(yl[:, s, :], bank(7), gate[:, s:s + 1], yh[:, s, :].bitcast(F32),
                                                   ALU.mult, ALU.subtract).then_inc(yl_ready, 1)
                    dve.wait_ge(ld_ps[s], st.dma(-1))
                    nc.vector.tensor_scalar(sel[:, s, :], place_s[:, s, :], iota_p[:, 0:1], None, ALU.is_equal
                                            ).then_inc(sel_ready, 1)
                if not st.last:
                    gates(st, 1)
                    if not st.first:
                        find(st, 3)
                    down_low(st, 1)
            for c in (0, 2):
                dve.wait_ge(total_done, c + 1)
                nc.vector.tensor_copy(total_t[:, c, :], bank(c)[:, 0:TOK]).then_inc(total_dve, 1)
            for g in range(NG):
                dve.wait_ge(back_done, g + 1)
                nc.vector.tensor_tensor(fin[:, g, :], bank(4 + g)[0:G, :], h[:, g, :], ALU.add).then_inc(fin_ready, 1)


_ARGS = ["x", "L0_tok_W", "L0_tok_b", "L0_tok_g1", "L0_tok_b1", "L0_tok_g2", "L0_tok_b2", "L0_attn_w_gate",
         "L0_attn_g_gate", "L0_attn_w_down", "L0_attn_g_down", "L0_ffn_router_w", "L0_ffn_w_gate", "L0_ffn_w_up",
         "L0_ffn_w_down"]


def kernel(**inputs):
    import concourse.bacc as bacc
    import numpy as np
    from concourse.bass_utils import run_bass_kernel_spmd

    nc = bacc.Bacc("TRN2", target_bir_lowering=False, num_devices=1)
    arrays, args = {}, []
    for name in _ARGS:
        a = np.ascontiguousarray(inputs[name])
        arrays[f"in_{name}"] = a
        args.append(nc.dram_tensor(f"in_{name}", a.shape, mybir.dt.from_np(a.dtype), kind="ExternalInput").ap())
    out = nc.dram_tensor("out_0", (NB, NPATCH, D), F32, kind="ExternalOutput").ap()
    program(nc, *args, out)
    r = run_bass_kernel_spmd(nc, [arrays], core_ids=[0])
    return r.results[0]["out_0"]
```
